# Optimizing a Trainium2 kernel written in Bass

```python
import numpy as np
import jax
import jax.numpy as jnp

def _softmax(x, axis=-1):
    return jax.nn.softmax(x, axis=axis)

def _gelu(x):
    return jax.nn.gelu(x, approximate=True)

def _silu(x):
    return jax.nn.silu(x)

def _sigmoid(x):
    return jax.nn.sigmoid(x)

def _layernorm(x, axis=-1, eps=1e-05):
    m = jnp.mean(x, axis=axis, keepdims=True)
    v = jnp.var(x, axis=axis, keepdims=True)
    return (x - m) / jnp.sqrt(v + eps)

def _scatter_add(tgt, idx, src, axis=0):
    return tgt.at[idx].add(src)

def _segment_sum(src, seg, n):
    return jax.ops.segment_sum(src, seg, n)
kernel_name = 'mk_macaron_d1_jaxref_r8_53ef5b'

def setup_inputs(seed: int=0):
    np.random.seed(seed)
    _w = jnp.asarray

    def _L0_attn_setup():
        import jax, jax.numpy as jnp
        import numpy as np
        B, T, C = (64, 32, 128)
        N_HEAD, HEAD_SIZE, KV_RANK = (16, 64, 128)
        BLOCK_SIZE = 32
        key = jax.random.key(seed)
        ks = jax.random.split(key, 5)
        HD = N_HEAD * HEAD_SIZE

        def init(k, shape):
            fan_in = shape[0]
            bound = 1.0 / np.sqrt(fan_in)
            return jax.random.uniform(k, shape, jnp.float32, -bound, bound)
        return {'x': jax.random.normal(ks[0], (B, T, C), jnp.float32), 'w_kv_down': init(ks[1], (C, KV_RANK)), 'w_kv_up': init(ks[2], (KV_RANK, 2 * HD)), 'w_q': init(ks[3], (C, HD)), 'w_out': init(ks[4], (HD, C))}
    _L0_attn_in = _L0_attn_setup()

    def _L0_ffn_setup():
        import jax, jax.numpy as jnp
        import numpy as np
        E = 8
        K = 2
        D = 128
        F = 512
        EPS = 1e-05

        def _layernorm(h, g, b):
            mu = h.mean(axis=-1, keepdims=True)
            var = ((h - mu) ** 2).mean(axis=-1, keepdims=True)
            return (h - mu) * jax.lax.rsqrt(var + EPS) * g[:, None, :] + b[:, None, :]
        key = jax.random.key(seed)
        ks = jax.random.split(key, 8)
        B, S = (2, 256)
        x = jax.random.normal(ks[0], (B, S, D), dtype=jnp.float32)
        Wr = jax.random.normal(ks[1], (D, E), dtype=jnp.float32) / np.sqrt(D)
        br = jnp.zeros((E,), dtype=jnp.float32)
        W1 = jax.random.normal(ks[2], (E, D, F), dtype=jnp.float32) / np.sqrt(D)
        b1 = jnp.zeros((E, F), dtype=jnp.float32)
        g1 = jnp.ones((E, F), dtype=jnp.float32)
        be1 = jnp.zeros((E, F), dtype=jnp.float32)
        W2 = jax.random.normal(ks[3], (E, F, D), dtype=jnp.float32) / np.sqrt(F)
        b2 = jnp.zeros((E, D), dtype=jnp.float32)
        g2 = jnp.ones((E, D), dtype=jnp.float32)
        be2 = jnp.zeros((E, D), dtype=jnp.float32)
        return {'x': x, 'Wr': Wr, 'br': br, 'W1': W1, 'b1': b1, 'g1': g1, 'be1': be1, 'W2': W2, 'b2': b2, 'g2': g2, 'be2': be2}
    _L0_ffn_in = _L0_ffn_setup()
    _d = {'L0_attn_x': _L0_attn_in['x'], 'L0_attn_w_kv_down': _L0_attn_in['w_kv_down'], 'L0_attn_w_kv_up': _L0_attn_in['w_kv_up'], 'L0_attn_w_q': _L0_attn_in['w_q'], 'L0_attn_w_out': _L0_attn_in['w_out'], 'L0_ffn_Wr': _L0_ffn_in['Wr'], 'L0_ffn_br': _L0_ffn_in['br'], 'L0_ffn_W1': _L0_ffn_in['W1'], 'L0_ffn_b1': _L0_ffn_in['b1'], 'L0_ffn_g1': _L0_ffn_in['g1'], 'L0_ffn_be1': _L0_ffn_in['be1'], 'L0_ffn_W2': _L0_ffn_in['W2'], 'L0_ffn_b2': _L0_ffn_in['b2'], 'L0_ffn_g2': _L0_ffn_in['g2'], 'L0_ffn_be2': _L0_ffn_in['be2']}
    _x0 = _d['L0_attn_x']
    _d['L0_attn_x'] = jax.random.normal(jax.random.fold_in(jax.random.key(seed), 1), (2, 1024, 128), dtype=_x0.dtype)
    del _x0
    return _d

def reference(L0_attn_x, L0_attn_w_kv_down, L0_attn_w_kv_up, L0_attn_w_q, L0_attn_w_out, L0_ffn_Wr, L0_ffn_br, L0_ffn_W1, L0_ffn_b1, L0_ffn_g1, L0_ffn_be1, L0_ffn_W2, L0_ffn_b2, L0_ffn_g2, L0_ffn_be2):

    def _L0_attn_ref(x, w_kv_down, w_kv_up, w_q, w_out):
        import jax, jax.numpy as jnp
        import numpy as np
        B, T, C = (64, 32, 128)
        N_HEAD, HEAD_SIZE, KV_RANK = (16, 64, 128)
        BLOCK_SIZE = 32
        Bx, Tx, Cx = x.shape
        HD = N_HEAD * HEAD_SIZE
        latent_kv = x @ w_kv_down
        kv = latent_kv @ w_kv_up
        k, v = (kv[..., :HD], kv[..., HD:])
        k = k.reshape(Bx, Tx, N_HEAD, HEAD_SIZE)
        v = v.reshape(Bx, Tx, N_HEAD, HEAD_SIZE)
        q = (x @ w_q).reshape(Bx, Tx, N_HEAD, HEAD_SIZE)
        scale = HEAD_SIZE ** (-0.5)
        att = jnp.einsum('bqhd,bkhd->bhqk', q, k) * scale
        causal = jnp.tril(jnp.ones((Tx, Tx), dtype=bool))
        att = jnp.where(causal, att, -jnp.inf)
        att = jax.nn.softmax(att, axis=-1)
        y = jnp.einsum('bhqk,bkhd->bqhd', att, v)
        y = y.reshape(Bx, Tx, HD)
        return y @ w_out

    def _L0_ffn_ref(x, Wr, br, W1, b1, g1, be1, W2, b2, g2, be2):
        import jax, jax.numpy as jnp
        import numpy as np
        E = 8
        K = 2
        D = 128
        F = 512
        EPS = 1e-05

        def _layernorm(h, g, b):
            mu = h.mean(axis=-1, keepdims=True)
            var = ((h - mu) ** 2).mean(axis=-1, keepdims=True)
            return (h - mu) * jax.lax.rsqrt(var + EPS) * g[:, None, :] + b[:, None, :]
        B, S, _ = x.shape
        xt = x.reshape(-1, D)
        logits = xt @ Wr + br
        p = jax.nn.softmax(logits, axis=-1)
        probs, idx = jax.lax.top_k(p, K)
        probs = probs / probs.sum(axis=-1, keepdims=True)
        h = jnp.einsum('td,edf->etf', xt, W1) + b1[:, None, :]
        h = _layernorm(jax.nn.relu(h), g1, be1)
        y = jnp.einsum('etf,efd->etd', h, W2) + b2[:, None, :]
        y = _layernorm(jax.nn.relu(y), g2, be2)
        gate = (jax.nn.one_hot(idx, E, dtype=x.dtype) * probs[..., None]).sum(axis=1)
        out = jnp.einsum('te,etd->td', gate, y)
        return out.reshape(B, S, D)
    x = L0_attn_x
    x = x + 0.5 * _L0_ffn_ref(_layernorm(x, axis=-1), L0_ffn_Wr, L0_ffn_br, L0_ffn_W1, L0_ffn_b1, L0_ffn_g1, L0_ffn_be1, L0_ffn_W2, L0_ffn_b2, L0_ffn_g2, L0_ffn_be2)
    x = x + _L0_attn_ref(_layernorm(x, axis=-1), L0_attn_w_kv_down, L0_attn_w_kv_up, L0_attn_w_q, L0_attn_w_out)
    x = x + 0.5 * _L0_ffn_ref(_layernorm(x, axis=-1), L0_ffn_Wr, L0_ffn_br, L0_ffn_W1, L0_ffn_b1, L0_ffn_g1, L0_ffn_be1, L0_ffn_W2, L0_ffn_b2, L0_ffn_g2, L0_ffn_be2)
    return x

_drawn_inputs = setup_inputs


def setup_inputs(seed=0):
    import zlib

    import numpy as np

    out = dict(_drawn_inputs(seed))
    spreads = {'L0_ffn_br': (0.0, 0.1),
     'L0_ffn_b1': (0.0, 0.1),
     'L0_ffn_g1': (1.0, 0.2),
     'L0_ffn_be1': (0.0, 0.1),
     'L0_ffn_b2': (0.0, 0.1),
     'L0_ffn_g2': (1.0, 0.2),
     'L0_ffn_be2': (0.0, 0.1)}
    factors = {'L0_attn_w_q': 3.853}
    for name, (base, spread) in spreads.items():
        noise = np.random.default_rng([zlib.crc32(name.encode()), seed]).standard_normal(out[name].shape)
        drawn = base * np.exp(spread * noise) if base else spread * noise
        out[name] = jnp.asarray(drawn.astype(out[name].dtype))
    for name, factor in factors.items():
        out[name] = (out[name] * factor).astype(out[name].dtype)
    return out
```

```python
import math
from contextlib import ExitStack

import concourse.bass as bass
from concourse import mybir

FP32 = mybir.dt.float32
BF16 = mybir.dt.bfloat16
I32 = mybir.dt.int32
U32 = mybir.dt.uint32
ALU = mybir.AluOpType
ACT = mybir.ActivationFunctionType
AX = mybir.AxisListType

P = 128
D = 128
TOK = 2048
NT = TOK // P
E = 8
K = 2
F = 512
FC = F // P
EPS = 1e-5
NS = K * TOK // P + E - 1
XB = 4
LEAD = 6
LOOP_END = NS - LEAD - (NS - LEAD - 4) % XB
DUMP = K * TOK


def make_constants(nc, pool_eng, c, made):
    pool_eng.memset(c["ident"][:, :], 0.0).then_inc(made, 1)
    pool_eng.memset(c["upper"][:, :], 1.0).then_inc(made, 1)
    pool_eng.memset(c["ones"][:, :], 1.0).then_inc(made, 1)
    pool_eng.memset(c["sel3"][:, :], 0.0).then_inc(made, 1)
    pool_eng.memset(c["scanmask"][:, :], 1.0).then_inc(made, 1)
    pool_eng.memset(c["eps"][:, :], EPS).then_inc(made, 1)
    pool_eng.iota(c["iota"][:, :], [[1, P]], base=0, channel_multiplier=0,
                  allow_small_or_imprecise_dtypes=True).then_inc(made, 1)
    pool_eng.iota(c["part"][:, :], [[0, 1]], base=0, channel_multiplier=1,
                  allow_small_or_imprecise_dtypes=True).then_inc(made, 1)
    pool_eng.iota(c["early"][:, :], [[-1, E]], base=E, channel_multiplier=0,
                  allow_small_or_imprecise_dtypes=True).then_inc(made, 1)
    pool_eng.iota(c["pairtile"][:, :], [[1, K * NT]], base=0, channel_multiplier=0,
                  allow_small_or_imprecise_dtypes=True).then_inc(made, 1)
    pool_eng.iota(c["dumprow"][:, :], [[0, (NS + 1) // 2], [P, 2]], base=DUMP, channel_multiplier=1,
                  allow_small_or_imprecise_dtypes=True).then_inc(made, 1)
    pool_eng.memset(c["identb"][:, :], 0.0).then_inc(made, 1)
    pool_eng.memset(c["negmask"][:, :], 0.0).then_inc(made, 1)
    pool_eng.memset(c["eye"][:, :], 0.0).then_inc(made, 1)
    pool_eng.memset(c["lnscale"][:, :], math.log(P_SCALE)).then_inc(made, 1)
    pool_eng.wait_ge(made, 15)
    pool_eng.affine_select(out=c["identb"][:, :], in_=c["identb"][:, :], compare_op=ALU.not_equal,
                           fill=1.0, base=0, pattern=[[-1, P]], channel_multiplier=1).then_inc(made, 1)
    pool_eng.affine_select(out=c["negmask"][:, :], in_=c["negmask"][:, :], compare_op=ALU.is_ge,
                           fill=NEG, base=0, pattern=[[-1, P]], channel_multiplier=1).then_inc(made, 1)
    pool_eng.affine_select(out=c["eye"][:, :].rearrange("p (i j) -> p i j", j=QT), in_=c["eye"][:, :].rearrange("p (i j) -> p i j", j=QT),
                           compare_op=ALU.not_equal, fill=1.0, base=0, pattern=[[1, QT], [-1, QT]],
                           channel_multiplier=0).then_inc(made, 1)
    pool_eng.affine_select(out=c["ident"][:, :], in_=c["ident"][:, :], compare_op=ALU.not_equal,
                           fill=1.0, base=0, pattern=[[-1, P]], channel_multiplier=1).then_inc(made, 1)
    pool_eng.affine_select(out=c["upper"][:, :], in_=c["upper"][:, :], compare_op=ALU.is_gt,
                           fill=0.0, base=0, pattern=[[1, P]], channel_multiplier=-1).then_inc(made, 1)
    pool_eng.memset(c["sel3"][0:3, :], 1.0).then_inc(made, 1)
    pool_eng.memset(c["scanmask"][:, :].rearrange("p (e t) -> p e t", e=E)[:, :, 0:1], 0.0).then_inc(made, 1)


CONSTANTS_MADE = 22


def ffn_phase(nc, tag, c, w, X, scratch, x_in=None, x_out=None):
    ctx = ExitStack()
    with ctx:
        def sb(name, shape, dt=FP32):
            return ctx.enter_context(nc.sbuf_tensor(f"{tag}_{name}", shape, dt))

        def sem(name):
            return nc.alloc_semaphore(name=f"{tag}_{name}")

        W1 = sb("W1", [P, E * F])
        W2 = sb("W2", [P, E * FC, D])
        wr = sb("wr", [P, E])
        br = sb("br", [P, E])
        gb_rows = sb("gb_rows", [2 * E * FC, P])
        gb = sb("gb", [P, 2 * E * FC])
        bias = sb("bias", [P, 32 + 8])
        b2row = sb("b2row", [1, E * D])
        c2row = sb("c2row", [1, E * D])
        bpart = sb("bpart", [P, 3, 40], BF16)
        brest = sb("brest", [P, 2, 40])
        rows = sb("rows", [P, E * F + E * D], BF16)
        g2 = sb("g2", [P, E * D])
        be2 = sb("be2", [P, E * D])
        s1 = sb("s1", [P, NT])
        mean = sb("mean", [P, NT])
        xn = sb("xn", [P, NT, D])
        sq = sb("sq", [P, NT, D])
        s2 = sb("s2", [P, NT])
        std = sb("std", [P, NT])
        rstd = sb("rstd", [P, NT])
        xnT = sb("xnT", [P, NT * P])
        logit = sb("logit", [P, NT, E])
        cand = sb("cand", [P, NT, E])
        pick = sb("pick", [P, K, NT, E])
        top = sb("top", [P, K, NT])
        best = sb("best", [P, NT])
        both = sb("both", [P, NT * E], BF16)
        gate = sb("gate", [P, K, NT])
        gden = sb("gden", [P, NT])
        ex = sb("ex", [P, NT])
        total = sb("total", [P, E * NT])
        incl = sb("incl", [P, E * NT])
        before = sb("before", [P, E, NT])
        ntile_i = sb("ntile_i", [P, E], I32)
        ntile = sb("ntile", [P, E])
        ends = sb("ends", [P, E])
        base = sb("base", [P, E])
        posall = sb("posall", [P, NT, E])
        possel = sb("possel", [P, NT, E])
        pos = sb("pos", [P, K, NT])
        pos_i = sb("pos_i", [P, K * NT], I32)
        hilo_i = sb("hilo_i", [P, 2, K * NT], I32)
        hilo = sb("hilo", [P, 2, K * NT])
        lo1h = sb("lo1h", [P, K * NT, P], BF16)
        hi1h = sb("hi1h", [P, K * NT, 3, NS], BF16)
        inv = sb("inv", [P, 3, NS])
        code = sb("code", [P, NS])
        late = sb("late", [P, NS])
        dump = sb("dump", [P, NS])
        gat_u = sb("gat_u", [P, NS + XB], U32)
        sca_u = sb("sca_u", [P, NS + XB], U32)
        past = sb("past", [1, NS, E])
        eid_f = sb("eid_f", [1, NS])
        eid = sb("eid", [1, NS + XB], I32)
        gidx = sb("gidx", [P, XB], U32)
        sidx = sb("sidx", [P, XB], U32)
        xg = sb("xg", [P, XB, D])
        xgT = sb("xgT", [P, 2, P])
        h = sb("h", [P, 2, F])
        hn = sb("hn", [P, 2, F])
        hnT = sb("hnT", [P, 2, F])
        stat1 = sb("stat1", [P, 2, 6])
        mv1 = sb("mv1", [P, 2, 2])
        sd1 = sb("sd1", [P, 2])
        rs1 = sb("rs1", [P, 2])
        y = sb("y", [P, 2, D])
        yg = sb("yg", [P, 2, D])
        yo = sb("yo", [P, 2, D])
        stat2 = sb("stat2", [P, 2, 6])
        mv2 = sb("mv2", [P, 2, 2])
        sd2 = sb("sd2", [P, 2])
        rs2 = sb("rs2", [P, 2])
        Yk = sb("Yk", [P, K, NT, D])

        banks = [ctx.enter_context(nc.psum_tensor(f"{tag}_bank{i}", [P, 512], FP32)) for i in range(8)]
        ps_h = banks[0:2]
        ps_t = banks[2:4]
        ps_y = banks[4:6]
        ps_x = banks[6:8]

        x_loaded = sem("x_loaded")
        w_small = sem("w_small")
        w_post = sem("w_post")
        w1_loaded = sem("w1_loaded")
        w2_loaded = sem("w2_loaded")
        const = sem("const")
        chain_v = sem("chain_v")
        sq_done = sem("sq_done")
        var_done = sem("var_done")
        std_done = sem("std_done")
        centred = sem("centred")
        xn_done = sem("xn_done")
        xn_stored = sem("xn_stored")
        xnT_ps = sem("xnT_ps")
        xnT_done = sem("xnT_done")
        logits_ps = sem("logits_ps")
        both_done = sem("both_done")
        counts_ps = sem("counts_ps")
        gap_done = sem("gap_done")
        ex_done = sem("ex_done")
        onehots = sem("onehots")
        inv_ps = sem("inv_ps")
        routed = sem("routed")
        gb_ps = sem("gb_ps")
        gb_done = sem("gb_done")
        c2_ps = sem("c2_ps")
        c2_done = sem("c2_done")
        c2_spread = sem("c2_spread")
        w2_scaled = sem("w2_scaled")
        rows_zero = sem("rows_zero")
        chain_p = sem("chain_p")
        parts_done = sem("parts_done")
        rows_done = sem("rows_done")
        idx_done = sem("idx_done")
        xg_loaded = [sem(f"xg_loaded{n}") for n in range(XB)]
        xgT_ps = sem("xgT_ps")
        xgT_done = sem("xgT_done")
        h_ps = sem("h_ps")
        h_done = sem("h_done")
        mv1_done = sem("mv1_done")
        sd1_done = sem("sd1_done")
        hn_done = sem("hn_done")
        hnT_ps = sem("hnT_ps")
        hnT_done = sem("hnT_done")
        y_ps = sem("y_ps")
        y_done = sem("y_done")
        mv2_done = sem("mv2_done")
        sd2_done = sem("sd2_done")
        rs1_done = sem("rs1_done")
        measured = sem("measured")
        yg_done = sem("yg_done")
        yo_done = sem("yo_done")
        y_stored = [sem(f"y_stored{n}") for n in range(2)]
        yk_loaded = [sem(f"yk_loaded{n}") for n in range(2)]
        x_new = sem("x_new")
        prod2 = sem("prod2")
        out_stored = sem("out_stored")

        xn_rows = scratch["xn"]
        y_rows = scratch["y"]

        block = ctx.enter_context(nc.Block())
        HALF = NT // 2

        @block.sync
        def _(sp):
            if x_in is not None:
                src = x_in.rearrange("b (t p) d -> p (b t) d", p=P)
                for half in range(2):
                    ts = slice(half * HALF, half * HALF + HALF)
                    sp.dma_start(X[:, ts, :], src[:, ts, :]).then_inc(x_loaded, 16)
            sp.dma_start(wr[:, :], w["Wr"]).then_inc(w_small, 16)
            sp.dma_start(br[:, :], w["br"].partition_broadcast(P)).then_inc(w_small, 16)
            sp.dma_start(gb_rows[0:E * FC, :], w["g1"].rearrange("e (c p) -> (e c) p", p=P)).then_inc(w_small, 16)
            sp.dma_start(gb_rows[E * FC:2 * E * FC, :], w["be1"].rearrange("e (c p) -> (e c) p", p=P)).then_inc(w_small, 16)
            sp.dma_start(bias[:, 0:32], w["b1"].rearrange("e (q j) -> (e q) j", j=32)).then_inc(w_small, 16)
            sp.dma_start(b2row[:, :], w["b2"].rearrange("(o e) d -> o (e d)", o=1)).then_inc(w_small, 16)
            sp.dma_start(W2[:, :, :], w["W2"].rearrange("e (c p) d -> p (e c) d", p=P)).then_inc(w2_loaded, 16)
            sp.dma_start(W1[:, :].rearrange("p (e f) -> p e f", e=E), w["W1"].rearrange("e d f -> d e f")).then_inc(w1_loaded, 16)
            dst = xn_rows.rearrange("(t p) d -> p t d", p=P)
            for half in range(2):
                ts = slice(half * HALF, half * HALF + HALF)
                sp.wait_ge(xn_done, half + 1)
                sp.dma_start(dst[:, ts, :], xn[:, ts, :]).then_inc(xn_stored, 16)
            sp.dma_start(g2[:, :], w["g2"].rearrange("e d -> (e d)").partition_broadcast(P)).then_inc(w_post, 16)
            sp.dma_start(be2[:, :], w["be2"].rearrange("e d -> (e d)").partition_broadcast(P)).then_inc(w_post, 16)
            sp.wait_ge(c2_done, 1)
            sp.dma_start(bias[:, 32:40], c2row[0:1, :].rearrange("o (p j) -> o p j", j=8)).then_inc(c2_spread, 16)
            sp.wait_ge(parts_done, 1)
            sp.wait_ge(rows_zero, 1)
            for part in range(3):
                sp.dma_start(rows[part:part + 1, 0:E * F].rearrange("o (p j) -> o p j", j=32),
                             bpart[:, part, 0:32]).then_inc(rows_done, 16)
                sp.dma_start(rows[part:part + 1, E * F:].rearrange("o (p j) -> o p j", j=8),
                             bpart[:, part, 32:40]).then_inc(rows_done, 16)
            for par in range(2):
                sp.wait_ge(y_stored[par], 16 * len(range(par, NS, 2)))
            for half in range(2):
                ts = slice(half * HALF, half * HALF + HALF)
                for k in range(K):
                    src = y_rows[k * TOK:(k + 1) * TOK, :].rearrange("(t p) d -> p t d", p=P)
                    sp.dma_start(Yk[:, k, ts, :], src[:, ts, :]).then_inc(yk_loaded[half], 16)
            if x_out is not None:
                dst = x_out.rearrange("b (t p) d -> p (b t) d", p=P)
                for half in range(2):
                    ts = slice(half * HALF, half * HALF + HALF)
                    sp.wait_ge(x_new, half + 1)
                    sp.dma_start(dst[:, ts, :], X[:, ts, :]).then_inc(out_stored, 16)
                sp.wait_ge(out_stored, 32)

        @block.gpsimd
        def _(pool):
            count = [0]

            def link(instruction):
                count[0] += 1
                instruction.then_inc(chain_p, 1)
                pool.wait_ge(chain_p, count[0])

            if x_in is not None:
                make_constants(nc, pool, c, const)
            pool.memset(rows[:, :], 0.0).then_inc(rows_zero, 1)
            pool.wait_ge(w_small, 96)
            pool.wait_ge(c2_spread, 16)
            link(pool.tensor_copy(bpart[:, 0, :], bias[:, :]))
            link(pool.tensor_tensor(brest[:, 0, :], bias[:, :], bpart[:, 0, :], ALU.subtract))
            link(pool.tensor_copy(bpart[:, 1, :], brest[:, 0, :]))
            link(pool.tensor_tensor(brest[:, 1, :], brest[:, 0, :], bpart[:, 1, :], ALU.subtract))
            pool.tensor_copy(bpart[:, 2, :], brest[:, 1, :]).then_inc(parts_done, 1)
            pool.wait_ge(gb_done, 1)
            pool.wait_ge(c2_ps, 1)
            pool.tensor_tensor(W2[:, :, :], W2[:, :, :],
                               gb[:, 0:E * FC].unsqueeze(2).to_broadcast([P, E * FC, D]),
                               ALU.mult).then_inc(w2_scaled, 1)

            def token_rows(i, buf):
                if not (isinstance(i, int) and i < XB):
                    pool.wait_ge(xgT_ps, i - (XB - 1))
                pool.tensor_copy(gidx[:, buf:buf + 1], gat_u[:, bass.ds(i, 1)]).then_inc(idx_done, 1)

            def pair_rows(i, buf):
                pool.tensor_copy(sidx[:, buf:buf + 1], sca_u[:, bass.ds(i, 1)]).then_inc(idx_done, 1)

            def gather(buf):
                pool.indirect_dma_start(xg[:, buf, :], None, xn_rows,
                                        bass.IndirectOffsetOnAxis(ap=gidx[:, buf:buf + 1], axis=0),
                                        bounds_check=TOK - 1).then_inc(xg_loaded[buf], 16)

            def step(i, u):
                par = u % 2
                static = isinstance(i, int)
                ahead = not static or i + LEAD < NS
                pool.wait_ge(yo_done, i + 1)
                if ahead:
                    token_rows(i + LEAD, (u + LEAD) % XB)
                pool.wait_ge(idx_done, 2 * i + LEAD + 2 if ahead else NS + i + 1)
                if not (static and i == NS - 1):
                    pair_rows(i + 1, (u + 1) % XB)
                if ahead:
                    gather((u + LEAD) % XB)
                pool.indirect_dma_start(y_rows, bass.IndirectOffsetOnAxis(ap=sidx[:, u:u + 1], axis=0),
                                        yo[:, par, :], None,
                                        bounds_check=K * TOK + 2 * P - 1).then_inc(y_stored[par], 16)

            pool.wait_ge(routed, 1)
            pool.wait_ge(xn_stored, 32)
            for i in range(LEAD):
                token_rows(i, i % XB)
                pool.wait_ge(idx_done, i + 1)
                gather(i % XB)
            pair_rows(0, 0)
            for i in range(4):
                step(i, i % XB)
            with pool.Fori(4, LOOP_END, XB) as i:
                for u in range(XB):
                    step(i + u, u)
            for i in range(LOOP_END, NS):
                step(i, i % XB)
            for half in range(2):
                ts = slice(half * HALF, half * HALF + HALF)
                pool.wait_ge(yk_loaded[half], 32)
                pool.tensor_tensor(Yk[:, 1, ts, :], Yk[:, 1, ts, :],
                                   gate[:, 1, ts].unsqueeze(2).to_broadcast([P, HALF, D]),
                                   ALU.mult).then_inc(prod2, 1)

        @block.scalar
        def _(act):
            if x_in is not None:
                act.wait_ge(const, CONSTANTS_MADE)
            for half in range(2):
                ts = slice(half * HALF, half * HALF + HALF)
                act.wait_ge(centred, half + 1)
                act.activation(sq[:, ts, :], xn[:, ts, :], ACT.Square).then_inc(sq_done, 1)
            for half in range(2):
                ts = slice(half * HALF, half * HALF + HALF)
                act.wait_ge(var_done, half + 1)
                act.activation(std[:, ts], s2[:, ts], ACT.Sqrt, bias=c["eps"][:, 0:1], scale=1.0 / D).then_inc(std_done, 1)
            for g in range(NT // 4):
                act.wait_ge(xnT_ps, g + 1)
                act.activation(xnT[:, g * 512:(g + 1) * 512], banks[g][:, :], ACT.Copy).then_inc(xnT_done, 1)
            act.wait_ge(gb_ps, 1)
            act.activation(gb[:, :], banks[5][:, 0:2 * E * FC], ACT.Copy).then_inc(gb_done, 1)
            act.wait_ge(gap_done, 1)
            act.activation(ex[:, :], gden[:, :], ACT.Exp).then_inc(ex_done, 1)

            def relu_h(i, par, first):
                act.wait_ge(h_ps, i + 1)
                if not first:
                    act.wait_ge(hn_done, i - 1)
                act.activation(h[:, par, :], ps_h[par][:, :], ACT.Relu).then_inc(h_done, 1)

            def copy_xT(i, par, first):
                act.wait_ge(xgT_ps, i + 1)
                if not first:
                    act.wait_ge(h_ps, i - 1)
                act.activation(xgT[:, par, :], ps_x[par][:, 0:P], ACT.Copy).then_inc(xgT_done, 1)

            def relu_y(i, par, first):
                act.wait_ge(y_ps, i + 1)
                if not first:
                    act.wait_ge(yg_done, i - 1)
                act.activation(y[:, par, :], ps_y[par][:, 0:D], ACT.Relu).then_inc(y_done, 1)

            def sd_h(i, par, first):
                act.wait_ge(mv1_done, i + 1)
                act.activation(sd1[:, par:par + 1], mv1[:, par, 1:2], ACT.Sqrt, bias=c["eps"][:, 0:1]).then_inc(sd1_done, 1)

            def copy_hT(i, par, first):
                act.wait_ge(hnT_ps, i + 1)
                if not first:
                    act.wait_ge(y_ps, i - 1)
                act.activation(hnT[:, par, :], ps_t[par][:, :], ACT.Copy).then_inc(hnT_done, 1)

            def sd_y(i, par, first):
                act.wait_ge(mv2_done, i + 1)
                act.activation(sd2[:, par:par + 1], mv2[:, par, 1:2], ACT.Sqrt, bias=c["eps"][:, 0:1]).then_inc(sd2_done, 1)

            def step(i, u):
                par = u % 2
                static = isinstance(i, int)
                live = lambda t: not static or 0 <= t < NS
                first = lambda t: static and t < 2
                if live(i):
                    relu_h(i, par, first(i))
                if live(i + 1):
                    copy_xT(i + 1, 1 - par, first(i + 1))
                if live(i - 2):
                    relu_y(i - 2, par, first(i - 2))
                if live(i):
                    sd_h(i, par, first(i))
                if live(i - 1):
                    copy_hT(i - 1, 1 - par, first(i - 1))
                if live(i - 2):
                    sd_y(i - 2, par, first(i - 2))

            copy_xT(0, 0, True)
            for i in range(4):
                step(i, i % XB)
            with act.Fori(4, LOOP_END, XB) as i:
                for u in range(XB):
                    step(i + u, u)
            for i in range(LOOP_END, NS + 2):
                step(i, i % XB)

        @block.tensor
        def _(pe):
            if x_in is not None:
                pe.wait_ge(const, CONSTANTS_MADE)
            ident = c["ident"]
            for t in range(NT):
                if t % HALF == 0:
                    pe.wait_ge(xn_done, t // HALF + 1)
                last = pe.transpose(banks[t // 4][:, t % 4 * P:(t % 4 + 1) * P], xn[:, t, :], ident[:, :])
                if t % 4 == 3:
                    last.then_inc(xnT_ps, 1)
            pe.wait_ge(w_small, 96)
            for t in range(NT):
                if t % 4 == 0:
                    pe.wait_ge(xnT_done, t // 4 + 1)
                last = pe.matmul(banks[4][:, t * E:(t + 1) * E], xnT[:, t * P:(t + 1) * P], wr[:, :], start=True, stop=True)
            last.then_inc(logits_ps, 1)
            pe.transpose(banks[5][:, 0:2 * E * FC], gb_rows[:, :], ident[0:2 * E * FC, 0:2 * E * FC]).then_inc(gb_ps, 1)
            pe.wait_ge(gb_done, 1)
            pe.wait_ge(w2_loaded, 16)
            for e in range(E):
                for ch in range(FC):
                    j = e * FC + ch
                    last = pe.matmul(banks[6 + e // 4][0:1, e % 4 * D:(e % 4 + 1) * D], gb[:, E * FC + j:E * FC + j + 1],
                                     W2[:, j, :], start=(ch == 0), stop=(ch == FC - 1))
            last.then_inc(c2_ps, 1)
            pe.wait_ge(both_done, 1)
            pe.wait_ge(xnT_done, 4)
            pe.matmul(banks[0][:, 0:NT * E], c["upper"][:, :], both[:, :], start=True, stop=True)
            pe.matmul(banks[1][:, 0:NT * E], c["ones"][:, :], both[:, :], start=True, stop=True).then_inc(counts_ps, 1)
            for q in range(K * NT):
                if q % NT == 0:
                    pe.wait_ge(onehots, 4 * (q // NT + 1))
                last = pe.matmul(banks[2][:, 0:3 * NS], lo1h[:, q, :], hi1h[:, q, :, :].rearrange("p w s -> p (w s)"),
                                 start=(q == 0), stop=(q == K * NT - 1))
            last.then_inc(inv_ps, 1)

            def transpose_x(i, par, buf, first):
                pe.wait_ge(xg_loaded[buf], 16 // XB * (i - buf) + 16)
                if not first:
                    pe.wait_ge(xgT_done, i - 1)
                pe.transpose(ps_x[par][:, 0:P], xg[:, buf, :], ident[:, :]).then_inc(xgT_ps, 1)

            def up(i, par, first):
                e = pe.value_load(eid[0:1, bass.ds(i, 1)], min_val=0, max_val=E - 1)
                pe.wait_ge(xgT_done, i + 1)
                if not first:
                    pe.wait_ge(h_done, i - 1)
                pe.matmul(ps_h[par][:, :], c["sel3"][:, :], rows[:, bass.ts(e, F)], start=True, stop=False)
                pe.matmul(ps_h[par][:, :], xgT[:, par, :], W1[:, bass.ts(e, F)], start=False, stop=True).then_inc(h_ps, 1)

            def transpose_h(i, par, first):
                pe.wait_ge(hn_done, i + 1)
                if not first:
                    pe.wait_ge(hnT_done, i - 1)
                for ch in range(FC):
                    last = pe.transpose(ps_t[par][:, ch * P:(ch + 1) * P], hn[:, par, ch * P:(ch + 1) * P], ident[:, :])
                last.then_inc(hnT_ps, 1)

            def down(i, par, first):
                e = pe.value_load(eid[0:1, bass.ds(i, 1)], min_val=0, max_val=E - 1)
                pe.wait_ge(hnT_done, i + 1)
                if not first:
                    pe.wait_ge(y_done, i - 1)
                pe.matmul(ps_y[par][:, 0:D], c["sel3"][:, :], rows[:, bass.ds(e * D + E * F, D)], start=True, stop=False)
                w2 = W2[:, :, :].rearrange("p j d -> p (j d)")
                for ch in range(FC):
                    last = pe.matmul(ps_y[par][:, 0:D], hnT[:, par, ch * P:(ch + 1) * P],
                                     w2[:, bass.ds(e * (FC * D) + ch * D, D)], start=False, stop=(ch == FC - 1))
                last.then_inc(y_ps, 1)

            def step(i, u):
                par = u % 2
                static = isinstance(i, int)
                live = lambda t: not static or 0 <= t < NS
                first = lambda t: static and t < 2
                if live(i):
                    up(i, par, first(i))
                if live(i + 1):
                    transpose_x(i + 1, 1 - par, (u + 1) % XB, first(i + 1))
                if live(i - 2):
                    down(i - 2, par, first(i - 2))
                if live(i - 1):
                    transpose_h(i - 1, 1 - par, first(i - 1))

            pe.wait_ge(w1_loaded, 16)
            pe.wait_ge(w2_scaled, 1)
            pe.wait_ge(rows_done, 96)
            pe.wait_ge(c2_done, 1)
            pe.wait_ge(routed, 1)
            transpose_x(0, 0, 0, True)
            for i in range(4):
                step(i, i % XB)
            with pe.Fori(4, LOOP_END, XB) as i:
                for u in range(XB):
                    step(i + u, u)
            for i in range(LOOP_END, NS + 2):
                step(i, i % XB)

        @block.vector
        def _(dve):
            count = [0]

            def link(instruction):
                count[0] += 1
                instruction.then_inc(chain_v, 1)
                dve.wait_ge(chain_v, count[0])

            def wide(small):
                return small.unsqueeze(2).to_broadcast([P, NT, E])

            halves = [slice(0, HALF), slice(HALF, NT)]
            for n, ts in enumerate(halves):
                if x_in is not None:
                    dve.wait_ge(x_loaded, 32)
                link(dve.tensor_reduce(s1[:, ts], X[:, ts, :], AX.X, ALU.add))
                link(dve.tensor_scalar(mean[:, ts], s1[:, ts], 1.0 / D, None, ALU.mult))
                dve.tensor_tensor(xn[:, ts, :], X[:, ts, :], mean[:, ts].unsqueeze(2).to_broadcast([P, HALF, D]),
                                  ALU.subtract).then_inc(centred, 1)
            for n, ts in enumerate(halves):
                dve.wait_ge(sq_done, n + 1)
                dve.tensor_reduce(s2[:, ts], sq[:, ts, :], AX.X, ALU.add).then_inc(var_done, 1)
            for n, ts in enumerate(halves):
                dve.wait_ge(std_done, n + 1)
                link(dve.reciprocal(rstd[:, ts], std[:, ts]))
                dve.tensor_tensor(xn[:, ts, :], xn[:, ts, :], rstd[:, ts].unsqueeze(2).to_broadcast([P, HALF, D]),
                                  ALU.mult).then_inc(xn_done, 1)
            dve.wait_ge(logits_ps, 1)
            if x_in is not None:
                dve.wait_ge(const, CONSTANTS_MADE)
            link(dve.tensor_tensor(logit[:, :, :], banks[4][:, 0:NT * E].rearrange("p (t e) -> p t e", e=E),
                                   br[:, :].unsqueeze(1).to_broadcast([P, NT, E]), ALU.add))
            for k in range(K):
                link(dve.tensor_reduce(top[:, k, :], logit[:, :, :], AX.X, ALU.max))
                link(dve.tensor_tensor(cand[:, :, :], logit[:, :, :], wide(top[:, k, :]), ALU.is_ge))
                link(dve.tensor_tensor(cand[:, :, :], cand[:, :, :],
                                       c["early"][:, :].unsqueeze(1).to_broadcast([P, NT, E]), ALU.mult))
                link(dve.tensor_reduce(best[:, :], cand[:, :, :], AX.X, ALU.max))
                link(dve.tensor_tensor(pick[:, k, :, :], cand[:, :, :], wide(best[:, :]), ALU.is_equal))
                if k == 0:
                    link(dve.scalar_tensor_tensor(out=logit[:, :, :], in0=pick[:, 0, :, :], scalar=-3.0e38,
                                                  in1=logit[:, :, :], op0=ALU.mult, op1=ALU.add))
            dve.tensor_tensor(both[:, :].rearrange("p (t e) -> p t e", e=E), pick[:, 0, :, :], pick[:, 1, :, :],
                              ALU.add).then_inc(both_done, 1)
            dve.tensor_tensor(gden[:, :], top[:, 1, :], top[:, 0, :], ALU.subtract).then_inc(gap_done, 1)
            dve.wait_ge(counts_ps, 1)
            link(dve.tensor_copy(total[:, :].rearrange("p (e t) -> p t e", e=E),
                                 banks[1][:, 0:NT * E].rearrange("p (t e) -> p t e", e=E)))
            link(dve.tensor_tensor_scan(incl[:, :], c["scanmask"][:, :], total[:, :], 0.0, ALU.mult, ALU.add))
            inclv = incl[:, :].rearrange("p (e t) -> p e t", e=E)
            link(dve.tensor_scalar(ntile_i[:, :], inclv[:, :, NT - 1], float(P - 1), None, ALU.add))
            link(dve.tensor_scalar(ntile_i[:, :], ntile_i[:, :], 7, None, ALU.arith_shift_right))
            link(dve.tensor_copy(ntile[:, :], ntile_i[:, :]))
            link(dve.tensor_tensor_scan(ends[:, :], c["scanmask"][:, 1:1 + E], ntile[:, :], 0.0, ALU.mult, ALU.add))
            link(dve.tensor_tensor(base[:, :], ends[:, :], ntile[:, :], ALU.subtract))
            link(dve.tensor_scalar(base[:, :], base[:, :], float(P), None, ALU.mult))
            link(dve.tensor_tensor(before[:, :, :], inclv, total[:, :].rearrange("p (e t) -> p e t", e=E), ALU.subtract))
            link(dve.tensor_tensor(before[:, :, :], before[:, :, :], base[:, :].unsqueeze(2).to_broadcast([P, E, NT]), ALU.add))
            link(dve.tensor_tensor(posall[:, :, :], banks[0][:, 0:NT * E].rearrange("p (t e) -> p t e", e=E),
                                   before[:, :, :].rearrange("p e t -> p t e"), ALU.add))
            for k in range(K):
                link(dve.tensor_tensor(possel[:, :, :], posall[:, :, :], pick[:, k, :, :], ALU.mult))
                link(dve.tensor_reduce(pos[:, k, :], possel[:, :, :], AX.X, ALU.add))
            link(dve.tensor_copy(pos_i[:, :], pos[:, :, :].rearrange("p k t -> p (k t)")))
            link(dve.tensor_scalar(hilo_i[:, 0, :], pos_i[:, :], 7, None, ALU.arith_shift_right))
            link(dve.tensor_scalar(hilo_i[:, 1, :], pos_i[:, :], P - 1, None, ALU.bitwise_and))
            link(dve.tensor_copy(hilo[:, :, :], hilo_i[:, :, :]))
            for k in range(K):
                qs = slice(k * NT, (k + 1) * NT)
                dve.tensor_tensor(hi1h[:, qs, 0, :], c["iota"][:, 0:NS].unsqueeze(1).to_broadcast([P, NT, NS]),
                                  hilo[:, 0, qs].unsqueeze(2).to_broadcast([P, NT, NS]), ALU.is_equal).then_inc(onehots, 1)
                dve.tensor_tensor(lo1h[:, qs, :], c["iota"][:, :].unsqueeze(1).to_broadcast([P, NT, P]),
                                  hilo[:, 1, qs].unsqueeze(2).to_broadcast([P, NT, P]), ALU.is_equal).then_inc(onehots, 1)
                dve.wait_ge(onehots, 4 * k + 2)
                dve.tensor_scalar(hi1h[:, qs, 1, :], hi1h[:, qs, 0, :], c["part"][:, 0:1], None, ALU.mult).then_inc(onehots, 1)
                dve.tensor_tensor(hi1h[:, qs, 2, :], hi1h[:, qs, 0, :],
                                  c["pairtile"][:, qs].unsqueeze(2).to_broadcast([P, NT, NS]), ALU.mult).then_inc(onehots, 1)
            link(dve.tensor_tensor(past[:, :, :], c["iota"][0:1, 0:NS].unsqueeze(2).to_broadcast([1, NS, E]),
                                   ends[0:1, :].unsqueeze(1).to_broadcast([1, NS, E]), ALU.is_ge))
            link(dve.tensor_reduce(eid_f[:, :], past[:, :, :], AX.X, ALU.add))
            link(dve.tensor_scalar(eid_f[:, :], eid_f[:, :], float(E - 1), None, ALU.min))
            link(dve.tensor_copy(eid[:, 0:NS], eid_f[:, :]))
            dve.wait_ge(ex_done, 1)
            link(dve.tensor_scalar(gden[:, :], ex[:, :], 1.0, 2.0, ALU.add, ALU.mult))
            link(dve.reciprocal(gate[:, 0, :], gden[:, :]))
            link(dve.tensor_tensor(gate[:, 1, :], gate[:, 0, :], ex[:, :], ALU.mult))
            dve.wait_ge(inv_ps, 1)
            link(dve.tensor_copy(inv[:, :, :], banks[2][:, 0:3 * NS].rearrange("p (w s) -> p w s", w=3)))
            link(dve.scalar_tensor_tensor(out=code[:, :], in0=inv[:, 2, :], scalar=float(P), in1=inv[:, 1, :],
                                          op0=ALU.mult, op1=ALU.add))
            link(dve.tensor_scalar(late[:, :], code[:, :], float(TOK), -float(TOK), ALU.is_ge, ALU.mult))
            link(dve.tensor_tensor(late[:, :], late[:, :], code[:, :], ALU.add))
            link(dve.tensor_copy(gat_u[:, 0:NS], late[:, :]))
            link(dve.tensor_scalar(dump[:, :], inv[:, 0, :], -1.0, 1.0, ALU.mult, ALU.add))
            link(dve.tensor_tensor(dump[:, :], dump[:, :], c["dumprow"][:, 0:NS], ALU.mult))
            link(dve.tensor_tensor(code[:, :], code[:, :], dump[:, :], ALU.add))
            dve.tensor_copy(sca_u[:, 0:NS], code[:, :]).then_inc(routed, 1)
            dve.wait_ge(c2_ps, 1)
            for n in range(2):
                last = dve.tensor_tensor(c2row[:, n * 512:(n + 1) * 512], banks[6 + n][0:1, :],
                                         b2row[:, n * 512:(n + 1) * 512], ALU.add)
                if n == 0:
                    link(last)
            last.then_inc(c2_done, 1)

            def step(i, u):
                par = u % 2
                static = isinstance(i, int)
                live = lambda t: not static or 0 <= t < NS
                first = lambda t: static and t < 2
                if live(i - 1):
                    q = 1 - par
                    dve.wait_ge(sd1_done, i)
                    dve.reciprocal(rs1[:, q:q + 1], sd1[:, q:q + 1]).then_inc(rs1_done, 1)
                    if not first(i - 1):
                        dve.wait_ge(hnT_ps, i - 2)
                    dve.wait_ge(rs1_done, i)
                    dve.tensor_scalar(hn[:, q, :], h[:, q, :], mv1[:, q, 0:1], rs1[:, q:q + 1],
                                      ALU.subtract, ALU.mult).then_inc(hn_done, 1)
                if live(i):
                    dve.wait_ge(h_done, i + 1)
                    dve.bn_stats(stat1[:, par, :], h[:, par, :]).then_inc(measured, 1)
                if live(i - 2):
                    dve.wait_ge(y_done, i - 1)
                    dve.bn_stats(stat2[:, par, :], y[:, par, :]).then_inc(measured, 1)
                if live(i - 3):
                    q = 1 - par
                    dve.wait_ge(sd2_done, i - 2)
                    dve.reciprocal(rs2[:, q:q + 1], sd2[:, q:q + 1]).then_inc(measured, 1)
                    e = dve.value_load(eid[0:1, bass.ds(i - 3, 1)], min_val=0, max_val=E - 1)
                dve.wait_ge(measured, 3 * i - 2 if not static else
                            min(i + 1, NS) + min(max(i - 1, 0), NS) + max(i - 2, 0))
                if live(i - 3):
                    dve.scalar_tensor_tensor(out=yg[:, q, :], in0=y[:, q, :], scalar=mv2[:, q, 0:1],
                                             in1=g2[:, bass.ts(e, D)], op0=ALU.subtract, op1=ALU.mult).then_inc(yg_done, 1)
                if live(i):
                    dve.bn_aggr(mv1[:, par, :], stat1[:, par, :]).then_inc(mv1_done, 1)
                if live(i - 2):
                    dve.bn_aggr(mv2[:, par, :], stat2[:, par, :]).then_inc(mv2_done, 1)
                if live(i - 3):
                    if not (static and i < 5):
                        dve.wait_ge(y_stored[q], 8 * (i - 3 - q))
                    dve.wait_ge(yg_done, i - 2)
                    dve.scalar_tensor_tensor(out=yo[:, q, :], in0=yg[:, q, :], scalar=rs2[:, q:q + 1],
                                             in1=be2[:, bass.ts(e, D)], op0=ALU.mult, op1=ALU.add).then_inc(yo_done, 1)

            dve.wait_ge(w_post, 32)
            for i in range(4):
                step(i, i % XB)
            with dve.Fori(4, LOOP_END, XB) as i:
                for u in range(XB):
                    step(i + u, u)
            for i in range(LOOP_END, NS + 3):
                step(i, i % XB)
            for n, ts in enumerate(halves):
                dve.wait_ge(yk_loaded[n], 32)
                link(dve.tensor_tensor(Yk[:, 0, ts, :], Yk[:, 0, ts, :],
                                       gate[:, 0, ts].unsqueeze(2).to_broadcast([P, HALF, D]), ALU.mult))
                link(dve.tensor_tensor(X[:, ts, :], X[:, ts, :], Yk[:, 0, ts, :], ALU.add))
                dve.wait_ge(prod2, n + 1)
                dve.tensor_tensor(X[:, ts, :], X[:, ts, :], Yk[:, 1, ts, :], ALU.add).then_inc(x_new, 1)
            dve.wait_ge(x_new, 2)


B = 2
T = TOK // B
QT = T // P
NH = 16
HS = 64
NP = NH // 2
NB = B * NP
VC = 2 * HS + 1
CHUNKS = [(Q, j, max(j * P, Q * 512), (Q + 1) * 512 - max(j * P, Q * 512)) for Q in range(2) for j in range(4 * Q + 4)]
NC = len(CHUNKS)
MAXES = [(i, k0, min((i + 1) * P - k0, 512)) for i in range(QT) for k0 in range(0, (i + 1) * P, 512)]
assert len(MAXES) == NC
MAX_AT = [0, 0, 0, 1, 2, 1, 2, 1, 2, 1, 2, 0]
assert sum(MAX_AT) == NC
LAG = 3
P_SCALE = 16.0
NEG = -1.0e30
VMAX = 2.0 ** 14


def wait(eng, semaphore, value):
    if not isinstance(value, int) or value > 0:
        eng.wait_ge(semaphore, value)


def attention_phase(nc, c, w, X):
    F32R = mybir.dt.float32r
    FP16 = mybir.dt.float16
    ctx = ExitStack()
    with ctx:
        def sb(name, shape, dt=FP32):
            return ctx.enter_context(nc.sbuf_tensor(f"at_{name}", shape, dt))

        def sem(name):
            return nc.alloc_semaphore(name=f"at_{name}")

        s1 = sb("s1", [P, NT])
        mean = sb("mean", [P, NT])
        s2 = sb("s2", [P, NT])
        std = sb("std", [P, NT])
        rstd = sb("rstd", [P, NT])
        xn = sb("xn", [P, NT, D])
        sq = sb("sq", [P, NT, D])
        xnT = sb("xnT", [P, TOK])
        latT = sb("latT", [P, TOK])
        wd = sb("wd", [P, P])
        wv = sb("wv", [P, NH * HS])
        wo = sb("wo", [P, NP, D])
        wq = sb("wq", [P, P])
        wk = sb("wk", [P, P])
        V = sb("V", [P, NB * 2 * QT * VC], FP16)
        wmax = sb("wmax", [P, 2])
        wmax_all = sb("wmax_all", [P, 2])
        vscale = sb("vscale", [P, 1])
        vunscale = sb("vunscale", [P, 1])
        QH = sb("QH", [P, T], F32R)
        QL = sb("QL", [P, T], F32R)
        KH = sb("KH", [P, T], F32R)
        KL = sb("KL", [P, T], F32R)
        QQ = [sb(f"QQ{s}", [P, T], F32R) for s in range(2)]
        KK = [sb(f"KK{s}", [P, T], F32R) for s in range(2)]
        QM = [sb(f"QM{s}", [P, T], F32R) for s in range(2)]
        KM = [sb(f"KM{s}", [P, T], F32R) for s in range(2)]
        fill = sb("fill", [HS, T])
        mx = sb("mx", [P, 2, QT])
        m = sb("m", [P, QT])
        mh = sb("mh", [P, QT], BF16)
        mr = sb("mr", [P, QT])
        mdiag = sb("mdiag", [P, QT, 2 * QT], BF16)
        Pf = sb("Pf", [P, 3, 512])
        Ph = sb("Ph", [P, 4, 512], FP16)
        Pl = sb("Pl", [P, 4, 512], FP16)
        rden = sb("rden", [P, 2, 4])
        rs = sb("rs", [P, 2, 4])
        yp = sb("yp", [P, QT, P])
        ypT = sb("ypT", [P, 2, 512])
        banks = [ctx.enter_context(nc.psum_tensor(f"at_bank{i}", [P, 512], FP32)) for i in range(7)]
        ps_shift = ctx.enter_context(nc.psum_tensor("at_shift", [P, 1024], BF16))
        ps_st = banks[0:2]
        ps_mx = banks[2:4]
        ps_pv = banks[4:6]
        ps_pr = banks[6]
        ps_yT = ps_shift[:, :].bitcast(FP32)

        w_in = sem("w_in")
        chain_v = sem("chain_v")
        chain_p = sem("chain_p")
        centred = sem("centred")
        sq_done = sem("sq_done")
        var_done = sem("var_done")
        std_done = sem("std_done")
        xn_done = sem("xn_done")
        xnT_ps = sem("xnT_ps")
        xnT_done = sem("xnT_done")
        lat_ps = sem("lat_ps")
        lat_done = sem("lat_done")
        v_ps = sem("v_ps")
        vh_done = sem("vh_done")
        vl_done = sem("vl_done")
        wmax_done = sem("wmax_done")
        wmax_red = sem("wmax_red")
        scale_done = sem("scale_done")
        ones_done = sem("ones_done")
        filled = sem("filled")
        stacks_set = sem("stacks_set")
        wpair = sem("wpair")
        proj_ps = sem("proj_ps")
        high_done = sem("high_done")
        low_done = sem("low_done")
        stack = [sem("stack_a"), sem("stack_b")]
        mx_ps = sem("mx_ps")
        mx_done = sem("mx_done")
        diag_done = sem("diag_done")
        shift_ps = sem("shift_ps")
        shift_done = sem("shift_done")
        st_ps = sem("st_ps")
        exp_done = sem("exp_done")
        ph_done = sem("ph_done")
        pl_done = sem("pl_done")
        pv_ps = sem("pv_ps")
        y_done = sem("y_done")
        yT_ps = sem("yT_ps")
        yT_done = sem("yT_done")
        o_ps = sem("o_ps")
        o_done = sem("o_done")
        y_own = sem("y_own")
        m_own = sem("m_own")

        block = ctx.enter_context(nc.Block())
        zero_rows = sq[0:HS, 0:T // D, :].rearrange("p a d -> p (a d)")
        HALF = NT // 2
        halves = [slice(0, HALF), slice(HALF, NT)]

        def v_view(v, col):
            t, g = v // 2, v % 2
            view = V[:, :].rearrange("p (b h t v) -> p b h t v", b=B, h=NH, t=QT)
            return view[:, t // QT, 8 * g:8 * g + 8, t % QT, col:col + HS]


        @block.sync
        def _(sp):
            sp.dma_start(wd[:, :], w["w_kv_down"]).then_inc(w_in, 16)
            sp.dma_start(wv[:, :], w["w_kv_up"][:, NH * HS:2 * NH * HS]).then_inc(w_in, 16)
            sp.dma_start(wo[:, :, :], w["w_out"].rearrange("(h p) d -> p h d", p=P)).then_inc(w_in, 16)

            def load_weights(n):
                wait(sp, proj_ps, 4 * n)
                hp = n % NP
                sp.dma_start(wq[:, :], w["w_q"][:, bass.ts(hp, P)]).then_inc(wpair, 16)
                sp.dma_start(wk[:, :], w["w_kv_up"][:, bass.ts(hp, P)]).then_inc(wpair, 16)

            def build_stack(n, s):
                if s == 0:
                    sp.wait_ge(low_done, 4 * n + 4)
                wait(sp, st_ps, NC * (2 * n + s - 1))
                wait(sp, mx_ps, NC * (2 * n + s - 1))
                own = slice(0, HS) if s == 0 else slice(HS, P)
                other = slice(HS, P) if s == 0 else slice(0, HS)
                for dst, src in ((QQ[s][own, :], QH), (QQ[s][other, :], QL), (KK[s][own, :], KH),
                                 (KK[s][other, :], KH), (QM[s][own, :], QH), (KM[s][own, :], KL)):
                    sp.dma_start(dst.bitcast(FP32), src[own, :].bitcast(FP32)).then_inc(stack[s], 16)

            load_weights(0)
            sp.wait_ge(filled, 4)
            for s, rows in ((0, slice(HS, P)), (1, slice(0, HS))):
                sp.dma_start(QM[s][rows, :].bitcast(FP32), zero_rows).then_inc(stacks_set, 16)
                sp.dma_start(KM[s][rows, :].bitcast(FP32), fill[:, :]).then_inc(stacks_set, 16)
            sp.wait_ge(stacks_set, 64)
            build_stack(0, 0)
            build_stack(0, 1)
            load_weights(1)
            build_stack(1, 0)
            with sp.Fori(1, NB - 1) as n:
                build_stack(n, 1)
                load_weights(n + 1)
                build_stack(n + 1, 0)
            build_stack(NB - 1, 1)

        def slot_pool(pool, n, s):
            for t, (Q, j, q0, cols) in enumerate(CHUNKS):
                k = NC * (2 * n + s) + t
                pool.wait_ge(ph_done, k + 1)
                wait(pool, pv_ps, k - 3)
                pool.tensor_tensor(Pl[:, t % 4, 0:cols], Pf[:, t % 3, 0:cols], Ph[:, t % 4, 0:cols],
                                   ALU.subtract).then_inc(pl_done, 1)

        @block.gpsimd
        def _(pool):
            pool.memset(V[:, :].rearrange("p (x v) -> p x v", v=VC)[:, :, VC - 1:VC], 1.0).then_inc(ones_done, 1)
            pool.memset(fill[:, :], 0.0).then_inc(filled, 1)
            pool.wait_ge(filled, 1)
            pool.memset(fill[0:2 * QT, :], -1.0).then_inc(filled, 1)
            pool.memset(mx[:, 1, 0:QT // 2], 2 * NEG).then_inc(filled, 1)
            pool.wait_ge(wmax_done, 1)
            pool.partition_all_reduce(wmax_all[:, :], wmax[:, :], P, bass.bass_isa.ReduceOp.max).then_inc(wmax_red, 1)
            pool.wait_ge(var_done, 2)
            pool.memset(zero_rows, 0.0).then_inc(filled, 1)
            for s in range(2):
                slot_pool(pool, 0, s)
            with pool.Fori(1, NB - 1) as n:
                for s in range(2):
                    slot_pool(pool, n, s)
            for s in range(2):
                slot_pool(pool, NB - 1, s)

        def slot_scalar(act, n, s, last=False):
            for t in range(NC + 1):
                if t < NC:
                    Q, j, q0, cols = CHUNKS[t]
                    k = NC * (2 * n + s) + t
                    act.wait_ge(st_ps, k + 1)
                    wait(act, pl_done, k - 2)
                    o = q0 % 512
                    act.activation(Pf[:, t % 3, 0:cols], ps_st[t % 2][:, o:o + cols], ACT.Exp,
                                   bias=c["lnscale"][:, 0:1]).then_inc(exp_done, 1)
                if t >= 1:
                    Q, j, q0, cols = CHUNKS[t - 1]
                    k = NC * (2 * n + s) + t - 1
                    act.wait_ge(exp_done, k + 1)
                    wait(act, pv_ps, k - 3)
                    act.activation(Ph[:, (t - 1) % 4, 0:cols], Pf[:, (t - 1) % 3, 0:cols], ACT.Copy).then_inc(ph_done, 1)
                if s == 0 and 7 <= t < 11 and not last:
                    high_part(act, n + 1, t - 7)
                if s == 1 and t == 10:
                    copy_yT(act, n, 0)
                if s == 0 and t == 4 and not (isinstance(n, int) and n == 0):
                    copy_yT(act, n - 1, 1)
            if not (last and s == 1):
                shift_rows(act, n if s == 0 else n + 1, 1 - s)

        def high_part(act, n, part):
            act.wait_ge(proj_ps, 4 * n + part + 1)
            if part == 0:
                for built in stack:
                    wait(act, built, 96 * n)
            dst = (QH, KH)[part // 2]
            act.activation(dst[:, part % 2 * 512:(part % 2 + 1) * 512], ps_pr[:, :], ACT.Copy,
                           scale=(HS ** -0.5, 1.0)[part // 2]).then_inc(high_done, 1)

        def copy_yT(act, n, half):
            act.wait_ge(yT_ps, 2 * n + half + 1)
            wait(act, o_ps, 2 * n + half - 1)
            act.activation(ypT[:, half, :], ps_yT, ACT.Copy).then_inc(yT_done, 1)

        def shift_rows(act, n, s):
            act.wait_ge(shift_ps, 2 * n + s + 1)
            r = HS if s == 0 else 0
            act.activation(QM[s][r:r + 2 * QT, :], ps_shift[0:2 * QT, :], ACT.Copy).then_inc(shift_done, 1)

        @block.scalar
        def _(act):
            for half, ts in enumerate(halves):
                act.wait_ge(centred, half + 1)
                act.activation(sq[:, ts, :], xn[:, ts, :], ACT.Square).then_inc(sq_done, 1)
            for half, ts in enumerate(halves):
                act.wait_ge(var_done, half + 1)
                act.activation(std[:, ts], s2[:, ts], ACT.Sqrt, bias=c["eps"][:, 0:1], scale=1.0 / D).then_inc(std_done, 1)
            for g in range(4):
                act.wait_ge(xnT_ps, g + 1)
                act.activation(xnT[:, g * 512:(g + 1) * 512], banks[g][:, :], ACT.Copy).then_inc(xnT_done, 1)
            for g in range(4):
                act.wait_ge(lat_ps, g + 1)
                act.activation(latT[:, g * 512:(g + 1) * 512], banks[g][:, :], ACT.Copy).then_inc(lat_done, 1)
            act.wait_ge(scale_done, 1)
            for v in range(2 * NT):
                act.wait_ge(v_ps, v + 1)
                act.activation(v_view(v, HS), banks[v % 4][:, :].rearrange("p (h d) -> p h d", d=HS), ACT.Copy,
                               scale=vscale[:, 0:1]).then_inc(vh_done, 1)
            for part in range(4):
                high_part(act, 0, part)
            act.wait_ge(stacks_set, 64)
            shift_rows(act, 0, 0)
            for s in range(2):
                slot_scalar(act, 0, s)
            with act.Fori(1, NB - 1) as n:
                for s in range(2):
                    slot_scalar(act, n, s)
            for s in range(2):
                slot_scalar(act, NB - 1, s, last=True)
            copy_yT(act, NB - 1, 1)

        def project(pe, n, part):
            if part == 0:
                pe.wait_ge(wpair, 32 * n + 32)
            wait(pe, low_done, 4 * n + part)
            if part == 0:
                wait(pe, o_done, 2 * n - 2)
            src = (xnT, latT)[part // 2]
            col = (n // NP) * T + part % 2 * 512
            pe.matmul(ps_pr[:, :], (wq, wk)[part // 2][:, :], src[:, bass.ds(col, 512)], start=True, stop=True).then_inc(proj_ps, 1)

        def max_chunk(pe, n, s, t):
            i, k0, cols = MAXES[t]
            k = NC * (2 * n + s) + t
            if t == 0:
                pe.wait_ge(stack[s], 96 * n + 96)
            wait(pe, mx_done, k - 1)
            wide = max(cols, 256)
            diag = k0 + cols == (i + 1) * P
            last = pe.matmul(ps_mx[t % 2][:, 0:wide], QQ[s][:, i * P:(i + 1) * P], KK[s][:, k0:k0 + wide],
                             start=True, stop=not diag, skip_group_check=diag)
            if diag:
                last = pe.matmul(ps_mx[t % 2][:, cols - P:cols], c["identb"][:, :], c["negmask"][:, :],
                                 start=False, stop=True, skip_group_check=True)
            last.then_inc(mx_ps, 1)

        def turn_max(pe, n, s):
            pe.wait_ge(diag_done, 2 * n + s + 1)
            h = 2 * n + s
            wait(pe, shift_done, h)
            wait(pe, yT_done, 2 * n - 1 if s == 0 else 2 * n)
            for i in range(QT):
                last = pe.transpose(ps_shift[0:2 * QT, i * P:(i + 1) * P], mdiag[:, i, :], c["identb"][:, :])
            last.then_inc(shift_ps, 1)

        def scores(pe, n, s, t):
            Q, j, q0, cols = CHUNKS[t]
            k = NC * (2 * n + s) + t
            if t == 0:
                pe.wait_ge(shift_done, 2 * n + s + 1)
            wait(pe, exp_done, k - 1)
            wide = max(cols, 256)
            lo = q0 + cols - wide
            out = ps_st[t % 2][:, lo % 512:lo % 512 + wide]
            diag = j >= 4 * Q
            pe.matmul(out, KK[s][:, j * P:(j + 1) * P], QQ[s][:, lo:lo + wide], start=True, stop=False, skip_group_check=diag)
            last = pe.matmul(out, KM[s][:, j * P:(j + 1) * P], QM[s][:, lo:lo + wide], start=False, stop=not diag,
                             skip_group_check=diag)
            if diag:
                last = pe.matmul(ps_st[t % 2][:, q0 % 512:q0 % 512 + P], c["negmask"][:, :], c["identb"][:, :],
                                 start=False, stop=True, skip_group_check=True)
            last.then_inc(st_ps, 1)

        def values(pe, n, s, t):
            Q, j, q0, cols = CHUNKS[t]
            k = NC * (2 * n + s) + t
            pe.wait_ge(pl_done, k + 1)
            if j == 0:
                wait(pe, y_done, 2 * (2 * n + s) + Q - 1)
            at = (n * 2 + s) * (QT * VC) + j * VC
            for i in range(q0 // P, (q0 + cols) // P):
                b = i * P - q0
                out = ps_pv[Q][:, (i % 4) * (HS + 1):(i % 4) * (HS + 1) + HS + 1]
                first, final = (j == 0 and i == 4 * Q), j == 4 * Q + 3
                pe.matmul(out, Ph[:, t % 4, b:b + P], V[:, bass.ds(at + HS, HS + 1)],
                          start=first, stop=False, skip_group_check=True)
                pe.matmul(out[:, 0:HS], Ph[:, t % 4, b:b + P], V[:, bass.ds(at, HS)],
                          start=False, stop=False, skip_group_check=True)
                last = pe.matmul(out, Pl[:, t % 4, b:b + P], V[:, bass.ds(at + HS, HS + 1)],
                                 start=False, stop=final, skip_group_check=True)
            last.then_inc(pv_ps, 1)

        def turn_y(pe, n, half):
            pe.wait_ge(y_done, 4 * n + 3 + half)
            if half == 1 and not n_has_next(n):
                pe.wait_ge(yT_done, 2 * n + 1)
            else:
                pe.wait_ge(shift_done, 2 * n + 2 + half)
            for i in range(4):
                last = pe.transpose(ps_yT[:, i * P:(i + 1) * P], yp[:, 4 * half + i, :], c["ident"][:, :])
            last.then_inc(yT_ps, 1)

        def out_product(pe, n, half):
            pe.wait_ge(yT_done, 2 * n + half + 1)
            pe.wait_ge(low_done, 4 * n + 8 if n_has_next(n) else 4 * n + 4)
            wait(pe, o_done, 2 * n + half)
            hp = n % NP
            wof = wo[:, :, :].rearrange("p h d -> p (h d)")
            for i in range(4):
                last = pe.matmul(ps_pr[:, i * P:(i + 1) * P], ypT[:, half, i * P:(i + 1) * P],
                                 wof[:, bass.ts(hp, D)], start=True, stop=True)
            last.then_inc(o_ps, 1)

        def n_has_next(n):
            return not (isinstance(n, int) and n == NB - 1)

        def slot_tensor(pe, n, s, last=False):
            first = isinstance(n, int) and n == 0
            nn, ns = (n, 1) if s == 0 else (n + 1, 0)
            mt = 0
            for t in range(NC):
                scores(pe, n, s, t)
                if not (last and s == 1):
                    for _ in range(MAX_AT[t]):
                        max_chunk(pe, nn, ns, mt)
                        mt += 1
                if t >= LAG:
                    values(pe, n, s, t - LAG)
                elif s == 1:
                    values(pe, n, 0, t + NC - LAG)
                elif not first:
                    values(pe, n - 1, 1, t + NC - LAG)
                if s == 0 and not last and 6 <= t < 10:
                    project(pe, n + 1, t - 6)
                if s == 1 and t == 9:
                    turn_y(pe, n, 0)
                if s == 1 and t == 11:
                    out_product(pe, n, 0)
                if s == 0 and not first and t == 3:
                    turn_y(pe, n - 1, 1)
                if s == 0 and not first and t == 5:
                    out_product(pe, n - 1, 1)
            if not (last and s == 1):
                turn_max(pe, nn, ns)

        @block.tensor
        def _(pe):
            for t in range(NT):
                if t % HALF == 0:
                    pe.wait_ge(xn_done, t // HALF + 1)
                last = pe.transpose(banks[t // 4][:, t % 4 * P:(t % 4 + 1) * P], xn[:, t, :], c["ident"][:, :])
                if t % 4 == 3:
                    last.then_inc(xnT_ps, 1)
            pe.wait_ge(w_in, 48)
            for g in range(4):
                pe.wait_ge(xnT_done, g + 1)
                pe.matmul(banks[g][:, :], wd[:, :], xnT[:, g * 512:(g + 1) * 512], start=True, stop=True).then_inc(lat_ps, 1)
            for v in range(2 * NT):
                if v % 8 == 0:
                    pe.wait_ge(lat_done, min(4, v // 8 + 1) if v else 4)
                wait(pe, vl_done, v - 3)
                pe.matmul(banks[v % 4][:, :], latT[:, v // 2 * P:(v // 2 + 1) * P], wv[:, v % 2 * 512:(v % 2 + 1) * 512],
                          start=True, stop=True).then_inc(v_ps, 1)
            for part in range(4):
                project(pe, 0, part)
            pe.wait_ge(vl_done, 2 * NT)
            for t in range(NC):
                max_chunk(pe, 0, 0, t)
            turn_max(pe, 0, 0)
            pe.wait_ge(ones_done, 1)
            for s in range(2):
                slot_tensor(pe, 0, s)
            with pe.Fori(1, NB - 1) as n:
                for s in range(2):
                    slot_tensor(pe, n, s)
            for s in range(2):
                slot_tensor(pe, NB - 1, s, last=True)
            for t in range(NC - LAG, NC):
                values(pe, NB - 1, 1, t)
            turn_y(pe, NB - 1, 1)
            out_product(pe, NB - 1, 1)

        def low_part(dve, n, part):
            dve.wait_ge(high_done, 4 * n + part + 1)
            high, low = ((QH, QL), (KH, KL))[part // 2]
            cs = slice(part % 2 * 512, (part % 2 + 1) * 512)
            dve.scalar_tensor_tensor(out=low[:, cs], in0=ps_pr[:, :], scalar=(HS ** -0.5, 1.0)[part // 2],
                                     in1=high[:, cs].bitcast(FP32), op0=ALU.mult, op1=ALU.subtract).then_inc(low_done, 1)

        def reduce_max(dve, n, s, t):
            i, k0, cols = MAXES[t]
            k = NC * (2 * n + s) + t
            dve.wait_ge(mx_ps, k + 1)
            dve.tensor_reduce(mx[:, k0 // 512, i:i + 1], ps_mx[t % 2][:, 0:cols], AX.X, ALU.max).then_inc(mx_done, 1)

        def output(dve, n, s, Q):
            h = 2 * n + s
            dve.wait_ge(pv_ps, NC * h + (4 if Q == 0 else NC))
            pv = ps_pv[Q][:, 0:4 * (HS + 1)].rearrange("p (i v) -> p i v", v=HS + 1)
            dve.reciprocal(rden[:, Q, :], pv[:, :, HS]).then_inc(y_own, 1)
            dve.wait_ge(y_own, 4 * h + 2 * Q + 1)
            dve.tensor_scalar(rs[:, Q, :], rden[:, Q, :], vunscale[:, 0:1], None, ALU.mult).then_inc(y_own, 1)
            dve.wait_ge(y_own, 4 * h + 2 * Q + 2)
            if s == 0:
                wait(dve, yT_ps, 2 * n - 1 + Q)
            dve.tensor_tensor(yp[:, 4 * Q:4 * Q + 4, s * HS:(s + 1) * HS], pv[:, :, 0:HS],
                              rs[:, Q, :].unsqueeze(2).to_broadcast([P, 4, HS]), ALU.mult).then_inc(y_done, 1)

        def add_output(dve, n, half):
            dve.wait_ge(o_ps, 2 * n + half + 1)
            Xf = X[:, :, :].rearrange("p t d -> p (t d)")
            at = (n // NP) * T + half * 512
            dve.tensor_tensor(Xf[:, bass.ds(at, 512)], ps_pr[:, :], Xf[:, bass.ds(at, 512)], ALU.add).then_inc(o_done, 1)


        def diagonals(dve, n, s):
            h = 2 * n + s
            eye = c["eye"][:, :].rearrange("p (i j) -> p i j", j=QT)
            dve.wait_ge(mx_done, NC * h + NC)
            dve.tensor_tensor(m[:, :], mx[:, 0, :], mx[:, 1, :], ALU.max).then_inc(m_own, 1)
            dve.wait_ge(m_own, 4 * h + 1)
            dve.tensor_copy(mh[:, :], m[:, :]).then_inc(m_own, 1)
            dve.wait_ge(m_own, 4 * h + 2)
            dve.tensor_tensor(mr[:, :], m[:, :], mh[:, :], ALU.subtract).then_inc(m_own, 1)
            wait(dve, shift_ps, h)
            dve.tensor_tensor(mdiag[:, :, 0:QT], eye, mh[:, :].unsqueeze(2).to_broadcast([P, QT, QT]), ALU.mult).then_inc(m_own, 1)
            dve.wait_ge(m_own, 4 * h + 4)
            dve.tensor_tensor(mdiag[:, :, QT:2 * QT], eye, mr[:, :].unsqueeze(2).to_broadcast([P, QT, QT]), ALU.mult).then_inc(diag_done, 1)

        def slot_vector(dve, n, s, last=False):
            first = isinstance(n, int) and n == 0
            nn, ns = (n, 1) if s == 0 else (n + 1, 0)
            mt = 0
            for t in range(NC):
                if not (last and s == 1):
                    for _ in range(MAX_AT[t]):
                        reduce_max(dve, nn, ns, mt)
                        mt += 1
                if t == 2 and not (first and s == 0):
                    output(dve, n - 1 if s == 0 else n, 1 - s, 1)
                if t == 7:
                    output(dve, n, s, 0)
                if s == 0 and not last and 6 <= t < 10:
                    low_part(dve, n + 1, t - 6)
                if s == 0 and not first and t == 5:
                    add_output(dve, n - 1, 1)
            if not (last and s == 1):
                diagonals(dve, nn, ns)
            if s == 1:
                add_output(dve, n, 0)

        @block.vector
        def _(dve):
            count = [0]

            def link(instruction):
                count[0] += 1
                instruction.then_inc(chain_v, 1)
                dve.wait_ge(chain_v, count[0])

            dve.wait_ge(w_in, 48)
            link(dve.tensor_reduce(wmax[:, 0:1], wd[:, :], AX.X, ALU.max, apply_absolute_value=True))
            dve.tensor_reduce(wmax[:, 1:2], wv[:, :], AX.X, ALU.max, apply_absolute_value=True).then_inc(wmax_done, 1)
            for n, ts in enumerate(halves):
                link(dve.tensor_reduce(s1[:, ts], X[:, ts, :], AX.X, ALU.add))
                link(dve.tensor_scalar(mean[:, ts], s1[:, ts], 1.0 / D, None, ALU.mult))
                dve.tensor_tensor(xn[:, ts, :], X[:, ts, :], mean[:, ts].unsqueeze(2).to_broadcast([P, HALF, D]),
                                  ALU.subtract).then_inc(centred, 1)
            for n, ts in enumerate(halves):
                dve.wait_ge(sq_done, n + 1)
                dve.tensor_reduce(s2[:, ts], sq[:, ts, :], AX.X, ALU.add).then_inc(var_done, 1)
            for n, ts in enumerate(halves):
                dve.wait_ge(std_done, n + 1)
                link(dve.reciprocal(rstd[:, ts], std[:, ts]))
                dve.tensor_tensor(xn[:, ts, :], xn[:, ts, :], rstd[:, ts].unsqueeze(2).to_broadcast([P, HALF, D]),
                                  ALU.mult).then_inc(xn_done, 1)
            dve.wait_ge(wmax_red, 1)
            link(dve.tensor_tensor(vscale[:, :], wmax_all[:, 0:1], wmax_all[:, 1:2], ALU.mult))
            link(dve.tensor_scalar(vscale[:, :], vscale[:, :], D * D * math.sqrt(D) / VMAX, 1e-30, ALU.mult, ALU.max))
            link(dve.reciprocal(vscale[:, :], vscale[:, :]))
            dve.reciprocal(vunscale[:, :], vscale[:, :]).then_inc(scale_done, 1)
            for v in range(2 * NT):
                dve.wait_ge(vh_done, v + 1)
                dve.scalar_tensor_tensor(out=v_view(v, 0), in0=banks[v % 4][:, :].rearrange("p (h d) -> p h d", d=HS),
                                         scalar=vscale[:, 0:1], in1=v_view(v, HS), op0=ALU.mult, op1=ALU.subtract).then_inc(vl_done, 1)
            for part in range(4):
                low_part(dve, 0, part)
            dve.wait_ge(filled, 3)
            for t in range(NC):
                reduce_max(dve, 0, 0, t)
            diagonals(dve, 0, 0)
            for s in range(2):
                slot_vector(dve, 0, s)
            with dve.Fori(1, NB - 1) as n:
                for s in range(2):
                    slot_vector(dve, n, s)
            for s in range(2):
                slot_vector(dve, NB - 1, s, last=True)
            output(dve, NB - 1, 1, 1)
            add_output(dve, NB - 1, 1)
            dve.wait_ge(o_done, 2 * NB)


def program(nc, x, w_kv_down, w_kv_up, w_q, w_out, Wr, br, W1, b1, g1, be1, W2, b2, g2, be2, out, phases="faf"):
    w = dict(Wr=Wr, br=br, W1=W1, b1=b1, g1=g1, be1=be1, W2=W2, b2=b2, g2=g2, be2=be2)
    ctx = ExitStack()
    with ctx:
        def sb(name, shape, dt=FP32):
            return ctx.enter_context(nc.sbuf_tensor(name, shape, dt))
        c = dict(ident=sb("ident", [P, P]), upper=sb("upper", [P, P], BF16), ones=sb("ones", [P, P], BF16),
                 sel3=sb("sel3", [P, P], BF16), scanmask=sb("scanmask", [P, E * NT]), eps=sb("eps", [P, 1]),
                 iota=sb("iota", [P, P]), part=sb("part", [P, 1]), early=sb("early", [P, E]),
                 pairtile=sb("pairtile", [P, K * NT]), dumprow=sb("dumprow", [P, NS + 1]),
                 identb=sb("identb", [P, P], BF16), negmask=sb("negmask", [P, P], BF16),
                 eye=sb("eye", [P, QT * QT]), lnscale=sb("lnscale", [P, 1]))
        X = sb("X", [P, NT, D])
        scratch = dict(xn=nc.dram_tensor("xn_rows", (TOK, D), FP32).ap(),
                       y=nc.dram_tensor("y_rows", (K * TOK + 2 * P, D), FP32).ap())
        with nc.cleanup_on_exit():
            ffn_phase(nc, "f0", c, w, X, scratch, x_in=x, x_out=out if phases == "f" else None)
        if "a" in phases:
            with nc.cleanup_on_exit():
                attention_phase(nc, c, dict(w_kv_down=w_kv_down, w_kv_up=w_kv_up, w_q=w_q, w_out=w_out), X)
        if phases == "fa":
            done = ctx.enter_context(nc.semaphore("done"))
            with nc.Block() as block:
                @block.sync
                def _(sp):
                    sp.dma_start(out.rearrange("b (t p) d -> p (b t) d", p=P), X[:, :, :]).then_inc(done, 16)
                    sp.wait_ge(done, 16)
        if phases == "faf":
            ffn_phase(nc, "f1", c, w, X, scratch, x_out=out)


_INS = ["L0_attn_x", "L0_attn_w_kv_down", "L0_attn_w_kv_up", "L0_attn_w_q", "L0_attn_w_out",
        "L0_ffn_Wr", "L0_ffn_br", "L0_ffn_W1", "L0_ffn_b1", "L0_ffn_g1", "L0_ffn_be1",
        "L0_ffn_W2", "L0_ffn_b2", "L0_ffn_g2", "L0_ffn_be2"]
_OUTS = [((2, 1024, 128), "float32")]


def kernel(**inputs):
    import numpy as _np
    import concourse.bacc as _bacc
    from concourse import mybir as _mybir
    from concourse.bass_utils import run_bass_kernel_spmd as _run

    nc = _bacc.Bacc("TRN2", target_bir_lowering=False, num_devices=1)
    arrays, args = {}, []
    for name in _INS:
        a = _np.ascontiguousarray(inputs[name])
        arrays[f"in_{name}_dram"] = a
        args.append(nc.dram_tensor(f"in_{name}_dram", a.shape, _mybir.dt.from_np(a.dtype), kind="ExternalInput").ap())
    for i, (shape, dtype) in enumerate(_OUTS):
        dt = _mybir.dt.from_np(_np.dtype(dtype))
        args.append(nc.dram_tensor(f"out_{i}_dram", shape, dt, kind="ExternalOutput").ap())
    program(nc, *args)
    r = _run(nc, [arrays], core_ids=[0])
    return r.results[0]["out_0_dram"]
```

```python
import math
from contextlib import ExitStack

import concourse.bass as bass
from concourse import mybir

FP32 = mybir.dt.float32
BF16 = mybir.dt.bfloat16
I32 = mybir.dt.int32
U32 = mybir.dt.uint32
ALU = mybir.AluOpType
ACT = mybir.ActivationFunctionType
AX = mybir.AxisListType

P = 128
D = 128
TOK = 2048
NT = TOK // P
E = 8
K = 2
F = 512
FC = F // P
EPS = 1e-5
NS = K * TOK // P + E - 1
XB = 4
LEAD = 6
LOOP_START = 2 * XB
LOOP_END = NS - LEAD - (NS - LEAD) % XB
C2_FIRST = 2
DUMP = K * TOK


def make_constants(nc, pool_eng, c, made):
    pool_eng.memset(c["ident"][:, :], 0.0).then_inc(made, 1)
    pool_eng.memset(c["upper"][:, :], 1.0).then_inc(made, 1)
    pool_eng.memset(c["ones"][:, :], 1.0).then_inc(made, 1)
    pool_eng.memset(c["sel3"][:, :], 0.0).then_inc(made, 1)
    pool_eng.memset(c["scanmask"][:, :], 1.0).then_inc(made, 1)
    pool_eng.memset(c["eps"][:, :], EPS).then_inc(made, 1)
    pool_eng.iota(c["iota"][:, :], [[1, P]], base=0, channel_multiplier=0,
                  allow_small_or_imprecise_dtypes=True).then_inc(made, 1)
    pool_eng.iota(c["part"][:, :], [[0, 1]], base=0, channel_multiplier=1,
                  allow_small_or_imprecise_dtypes=True).then_inc(made, 1)
    pool_eng.iota(c["early"][:, :], [[-1, E]], base=E, channel_multiplier=0,
                  allow_small_or_imprecise_dtypes=True).then_inc(made, 1)
    pool_eng.iota(c["pairtile"][:, :], [[1, K * NT]], base=0, channel_multiplier=0,
                  allow_small_or_imprecise_dtypes=True).then_inc(made, 1)
    pool_eng.iota(c["dumprow"][:, :], [[0, (NS + 1) // 2], [P, 2]], base=DUMP, channel_multiplier=1,
                  allow_small_or_imprecise_dtypes=True).then_inc(made, 1)
    pool_eng.memset(c["identb"][:, :], 0.0).then_inc(made, 1)
    pool_eng.memset(c["negmask"][:, :], 0.0).then_inc(made, 1)
    pool_eng.memset(c["eye"][:, :], 0.0).then_inc(made, 1)
    pool_eng.memset(c["lnscale"][:, :], math.log(P_SCALE)).then_inc(made, 1)
    pool_eng.wait_ge(made, 15)
    pool_eng.affine_select(out=c["identb"][:, :], in_=c["identb"][:, :], compare_op=ALU.not_equal,
                           fill=1.0, base=0, pattern=[[-1, P]], channel_multiplier=1).then_inc(made, 1)
    pool_eng.affine_select(out=c["negmask"][:, :], in_=c["negmask"][:, :], compare_op=ALU.is_ge,
                           fill=NEG, base=0, pattern=[[-1, P]], channel_multiplier=1).then_inc(made, 1)
    pool_eng.affine_select(out=c["eye"][:, :].rearrange("p (i j) -> p i j", j=QT), in_=c["eye"][:, :].rearrange("p (i j) -> p i j", j=QT),
                           compare_op=ALU.not_equal, fill=1.0, base=0, pattern=[[1, QT], [-1, QT]],
                           channel_multiplier=0).then_inc(made, 1)
    pool_eng.affine_select(out=c["ident"][:, :], in_=c["ident"][:, :], compare_op=ALU.not_equal,
                           fill=1.0, base=0, pattern=[[-1, P]], channel_multiplier=1).then_inc(made, 1)
    pool_eng.affine_select(out=c["upper"][:, :], in_=c["upper"][:, :], compare_op=ALU.is_gt,
                           fill=0.0, base=0, pattern=[[1, P]], channel_multiplier=-1).then_inc(made, 1)
    pool_eng.memset(c["sel3"][0:3, :], 1.0).then_inc(made, 1)
    pool_eng.memset(c["scanmask"][:, :].rearrange("p (e t) -> p e t", e=E)[:, :, 0:1], 0.0).then_inc(made, 1)


CONSTANTS_MADE = 22


def ffn_phase(nc, tag, c, w, X, scratch, x_in=None, x_out=None):
    ctx = ExitStack()
    with ctx:
        def sb(name, shape, dt=FP32):
            return ctx.enter_context(nc.sbuf_tensor(f"{tag}_{name}", shape, dt))

        def sem(name):
            return nc.alloc_semaphore(name=f"{tag}_{name}")

        W1 = sb("W1", [P, E * F])
        W2 = sb("W2", [P, E * FC, D])
        wr = sb("wr", [P, E])
        br = sb("br", [P, E])
        gb_rows = sb("gb_rows", [2 * E * FC, P])
        gb = sb("gb", [P, 2 * E * FC])
        bias = sb("bias", [P, 32 + 8])
        b2rows = sb("b2rows", [E, D])
        c2T = sb("c2T", [P, E])
        c2rows = sb("c2rows", [E, D])
        bpart = sb("bpart", [P, 3, 40], BF16)
        brest = sb("brest", [P, 2, 40])
        rows = sb("rows", [P, E * F + E * D], BF16)
        g2 = sb("g2", [P, E * D])
        be2 = sb("be2", [P, E * D])
        s1 = sb("s1", [P, NT])
        mean = sb("mean", [P, NT])
        xn = sb("xn", [P, NT, D])
        sq = sb("sq", [P, NT, D])
        s2 = sb("s2", [P, NT])
        std = sb("std", [P, NT])
        rstd = sb("rstd", [P, NT])
        xnT = sb("xnT", [P, NT * P])
        logit = sb("logit", [P, NT, E])
        cand = sb("cand", [P, NT, E])
        pick = sb("pick", [P, K, NT, E])
        top = sb("top", [P, K, NT])
        best = sb("best", [P, NT])
        both = sb("both", [P, NT * E], BF16)
        gate = sb("gate", [P, K, NT])
        gden = sb("gden", [P, NT])
        ex = sb("ex", [P, NT])
        total = sb("total", [P, E * NT])
        incl = sb("incl", [P, E * NT])
        before = sb("before", [P, E, NT])
        ntile_i = sb("ntile_i", [P, E], I32)
        ntile = sb("ntile", [P, E])
        ends = sb("ends", [P, E])
        base = sb("base", [P, E])
        posall = sb("posall", [P, NT, E])
        possel = sb("possel", [P, NT, E])
        pos = sb("pos", [P, K, NT])
        pos_i = sb("pos_i", [P, K * NT], I32)
        hilo_i = sb("hilo_i", [P, 2, K * NT], I32)
        hilo = sb("hilo", [P, 2, K * NT])
        lo1h = sb("lo1h", [P, K * NT, P], BF16)
        hi1h = sb("hi1h", [P, K * NT, 3, NS], BF16)
        inv = sb("inv", [P, 3, NS])
        code = sb("code", [P, NS])
        late = sb("late", [P, NS])
        dump = sb("dump", [P, NS])
        gat_u = sb("gat_u", [P, NS + XB], U32)
        sca_u = sb("sca_u", [P, NS + XB], U32)
        past = sb("past", [1, NS, E])
        eid_f = sb("eid_f", [1, NS])
        eid = sb("eid", [1, NS + XB], I32)
        gidx = sb("gidx", [P, XB], U32)
        sidx = sb("sidx", [P, XB], U32)
        xg = sb("xg", [P, XB, D])
        xgT = sb("xgT", [P, 2, P])
        h = sb("h", [P, 2, F])
        hn = sb("hn", [P, 2, F])
        hnT = sb("hnT", [P, 2, F])
        stat1 = sb("stat1", [P, 2, 6])
        mv1 = sb("mv1", [P, 2, 2])
        sd1 = sb("sd1", [P, 2])
        rs1 = sb("rs1", [P, 2])
        y = sb("y", [P, 2, D])
        yg = sb("yg", [P, 2, D])
        yo = sb("yo", [P, 2, D])
        stat2 = sb("stat2", [P, 2, 6])
        mv2 = sb("mv2", [P, 2, 2])
        sd2 = sb("sd2", [P, 2])
        rs2 = sb("rs2", [P, 2])
        Yk = sb("Yk", [P, K, NT, D])

        banks = [ctx.enter_context(nc.psum_tensor(f"{tag}_bank{i}", [P, 512], FP32)) for i in range(8)]
        ps_h = banks[0:2]
        ps_t = banks[2:4]
        ps_y = banks[4:6]
        ps_x = banks[6:8]

        x_loaded = sem("x_loaded")
        w_small = sem("w_small")
        w_post = sem("w_post")
        w1_loaded = sem("w1_loaded")
        w2_loaded = sem("w2_loaded")
        const = sem("const")
        chain_v = sem("chain_v")
        sq_done = sem("sq_done")
        var_done = sem("var_done")
        std_done = sem("std_done")
        centred = sem("centred")
        xn_done = sem("xn_done")
        xn_stored = sem("xn_stored")
        xnT_ps = sem("xnT_ps")
        xnT_done = sem("xnT_done")
        logits_ps = sem("logits_ps")
        both_done = sem("both_done")
        counts_ps = sem("counts_ps")
        gap_done = sem("gap_done")
        ex_done = sem("ex_done")
        onehots = sem("onehots")
        hi_tile = sem("hi_tile")
        inv_ps = sem("inv_ps")
        gates_done = sem("gates_done")
        routed = sem("routed")
        gb_ps = sem("gb_ps")
        gb_done = sem("gb_done")
        c2_ps = sem("c2_ps")
        c2_done = sem("c2_done")
        c2_spread = sem("c2_spread")
        w2_scaled = sem("w2_scaled")
        rows_zero = sem("rows_zero")
        chain_p = sem("chain_p")
        parts_done = sem("parts_done")
        rows_done = sem("rows_done")
        idx_done = sem("idx_done")
        xg_loaded = [sem(f"xg_loaded{n}") for n in range(XB)]
        xgT_ps = sem("xgT_ps")
        xgT_done = sem("xgT_done")
        h_ps = sem("h_ps")
        h_done = sem("h_done")
        mv1_done = sem("mv1_done")
        sd1_done = sem("sd1_done")
        hn_done = sem("hn_done")
        hnT_ps = sem("hnT_ps")
        hnT_done = sem("hnT_done")
        y_ps = sem("y_ps")
        y_done = sem("y_done")
        mv2_done = sem("mv2_done")
        sd2_done = sem("sd2_done")
        rs1_done = sem("rs1_done")
        measured = sem("measured")
        yg_done = sem("yg_done")
        yo_done = sem("yo_done")
        y_stored = [sem(f"y_stored{n}") for n in range(2)]
        yk_loaded = [sem(f"yk_loaded{n}") for n in range(2)]
        x_new = sem("x_new")
        prod2 = sem("prod2")
        out_stored = sem("out_stored")

        xn_rows = scratch["xn"]
        y_rows = scratch["y"]

        block = ctx.enter_context(nc.Block())
        HALF = NT // 2

        @block.sync
        def _(sp):
            if x_in is not None:
                src = x_in.rearrange("b (t p) d -> p (b t) d", p=P)
                for half in range(2):
                    ts = slice(half * HALF, half * HALF + HALF)
                    sp.dma_start(X[:, ts, :], src[:, ts, :]).then_inc(x_loaded, 16)
            sp.dma_start(wr[:, :], w["Wr"]).then_inc(w_small, 16)
            sp.dma_start(br[:, :], w["br"].partition_broadcast(P)).then_inc(w_small, 16)
            sp.dma_start(gb_rows[0:E * FC, :], w["g1"].rearrange("e (c p) -> (e c) p", p=P)).then_inc(w_small, 16)
            sp.dma_start(gb_rows[E * FC:2 * E * FC, :], w["be1"].rearrange("e (c p) -> (e c) p", p=P)).then_inc(w_small, 16)
            sp.dma_start(bias[:, 0:32], w["b1"].rearrange("e (q j) -> (e q) j", j=32)).then_inc(w_small, 16)
            sp.dma_start(b2rows[:, :], w["b2"]).then_inc(w_small, 16)
            sp.dma_start(W2[:, :, :], w["W2"].rearrange("e (c p) d -> p (e c) d", p=P)).then_inc(w2_loaded, 16)
            sp.dma_start(W1[:, :].rearrange("p (e f) -> p e f", e=E), w["W1"].rearrange("e d f -> d e f")).then_inc(w1_loaded, 16)
            dst = xn_rows.rearrange("(t p) d -> p t d", p=P)
            for half in range(2):
                ts = slice(half * HALF, half * HALF + HALF)
                sp.wait_ge(xn_done, half + 1)
                sp.dma_start(dst[:, ts, :], xn[:, ts, :]).then_inc(xn_stored, 16)
            sp.dma_start(g2[:, :], w["g2"].rearrange("e d -> (e d)").partition_broadcast(P)).then_inc(w_post, 16)
            sp.dma_start(be2[:, :], w["be2"].rearrange("e d -> (e d)").partition_broadcast(P)).then_inc(w_post, 16)
            sp.wait_ge(c2_done, 2)
            for e in range(E):
                sp.dma_start(bias[e * P // E:(e + 1) * P // E, 32:40],
                             c2rows[e:e + 1, :].rearrange("o (p j) -> o p j", j=8)).then_inc(c2_spread, 16)
            sp.wait_ge(parts_done, 1)
            sp.wait_ge(rows_zero, 1)
            for part in range(3):
                sp.dma_start(rows[part:part + 1, 0:E * F].rearrange("o (p j) -> o p j", j=32),
                             bpart[:, part, 0:32]).then_inc(rows_done, 16)
                sp.dma_start(rows[part:part + 1, E * F:].rearrange("o (p j) -> o p j", j=8),
                             bpart[:, part, 32:40]).then_inc(rows_done, 16)
            for par in range(2):
                sp.wait_ge(y_stored[par], 16 * len(range(par, NS, 2)))
            for half in range(2):
                ts = slice(half * HALF, half * HALF + HALF)
                for k in range(K):
                    src = y_rows[k * TOK:(k + 1) * TOK, :].rearrange("(t p) d -> p t d", p=P)
                    sp.dma_start(Yk[:, k, ts, :], src[:, ts, :]).then_inc(yk_loaded[half], 16)
            if x_out is not None:
                dst = x_out.rearrange("b (t p) d -> p (b t) d", p=P)
                for half in range(2):
                    ts = slice(half * HALF, half * HALF + HALF)
                    sp.wait_ge(x_new, half + 1)
                    sp.dma_start(dst[:, ts, :], X[:, ts, :]).then_inc(out_stored, 16)
                sp.wait_ge(out_stored, 32)

        @block.gpsimd
        def _(pool):
            count = [0]

            def link(instruction):
                count[0] += 1
                instruction.then_inc(chain_p, 1)
                pool.wait_ge(chain_p, count[0])

            if x_in is not None:
                make_constants(nc, pool, c, const)
            pool.memset(rows[:, :], 0.0).then_inc(rows_zero, 1)
            for k in range(K):
                qs = slice(k * NT, (k + 1) * NT)
                pool.wait_ge(onehots, 3 * k + 1)
                pool.tensor_tensor(hi1h[:, qs, 2, :], hi1h[:, qs, 0, :],
                                   c["pairtile"][:, qs].unsqueeze(2).to_broadcast([P, NT, NS]), ALU.mult).then_inc(hi_tile, 1)
            pool.wait_ge(w_small, 96)
            pool.wait_ge(c2_spread, 16 * E)
            link(pool.tensor_copy(bpart[:, 0, :], bias[:, :]))
            link(pool.tensor_tensor(brest[:, 0, :], bias[:, :], bpart[:, 0, :], ALU.subtract))
            link(pool.tensor_copy(bpart[:, 1, :], brest[:, 0, :]))
            link(pool.tensor_tensor(brest[:, 1, :], brest[:, 0, :], bpart[:, 1, :], ALU.subtract))
            pool.tensor_copy(bpart[:, 2, :], brest[:, 1, :]).then_inc(parts_done, 1)

            def token_rows(i, buf):
                if not (isinstance(i, int) and i < XB):
                    pool.wait_ge(xgT_ps, i - (XB - 1))
                pool.tensor_copy(gidx[:, buf:buf + 1], gat_u[:, bass.ds(i, 1)]).then_inc(idx_done, 1)

            def pair_rows(i, buf):
                pool.tensor_copy(sidx[:, buf:buf + 1], sca_u[:, bass.ds(i, 1)]).then_inc(idx_done, 1)

            def gather(buf):
                pool.indirect_dma_start(xg[:, buf, :], None, xn_rows,
                                        bass.IndirectOffsetOnAxis(ap=gidx[:, buf:buf + 1], axis=0),
                                        bounds_check=TOK - 1).then_inc(xg_loaded[buf], 16)

            def step(i, u):
                par = u % 2
                static = isinstance(i, int)
                ahead = not static or i + LEAD < NS
                pool.wait_ge(yo_done, i + 1)
                if ahead:
                    token_rows(i + LEAD, (u + LEAD) % XB)
                pool.wait_ge(idx_done, 2 * i + LEAD + 2 if ahead else NS + i + 1)
                if not (static and i == NS - 1):
                    pair_rows(i + 1, (u + 1) % XB)
                if ahead:
                    gather((u + LEAD) % XB)
                pool.indirect_dma_start(y_rows, bass.IndirectOffsetOnAxis(ap=sidx[:, u:u + 1], axis=0),
                                        yo[:, par, :], None,
                                        bounds_check=K * TOK + 2 * P - 1).then_inc(y_stored[par], 16)

            pool.wait_ge(routed, 1)
            pool.wait_ge(xn_stored, 32)
            for i in range(LEAD):
                token_rows(i, i % XB)
                pool.wait_ge(idx_done, i + 1)
                gather(i % XB)
            pair_rows(0, 0)
            for i in range(LOOP_START):
                step(i, i % XB)
            with pool.Fori(LOOP_START, LOOP_END, XB) as i:
                for u in range(XB):
                    step(i + u, u)
            for i in range(LOOP_END, NS):
                step(i, i % XB)
            pool.wait_ge(gates_done, 1)
            for half in range(2):
                ts = slice(half * HALF, half * HALF + HALF)
                pool.wait_ge(yk_loaded[half], 32)
                pool.tensor_tensor(Yk[:, 1, ts, :], Yk[:, 1, ts, :],
                                   gate[:, 1, ts].unsqueeze(2).to_broadcast([P, HALF, D]),
                                   ALU.mult).then_inc(prod2, 1)

        @block.scalar
        def _(act):
            if x_in is not None:
                act.wait_ge(const, CONSTANTS_MADE)
            for half in range(2):
                ts = slice(half * HALF, half * HALF + HALF)
                act.wait_ge(centred, half + 1)
                act.activation(sq[:, ts, :], xn[:, ts, :], ACT.Square).then_inc(sq_done, 1)
                act.wait_ge(var_done, half + 1)
                act.activation(std[:, ts], s2[:, ts], ACT.Sqrt, bias=c["eps"][:, 0:1], scale=1.0 / D).then_inc(std_done, 1)
            for g in range(NT // 4):
                act.wait_ge(xnT_ps, g + 1)
                act.activation(xnT[:, g * 512:(g + 1) * 512], banks[g][:, :], ACT.Copy).then_inc(xnT_done, 1)
            act.wait_ge(gb_ps, 1)
            act.activation(gb[:, :], banks[5][:, 0:2 * E * FC], ACT.Copy).then_inc(gb_done, 1)
            act.wait_ge(gap_done, 1)
            act.activation(ex[:, :], gden[:, :], ACT.Exp).then_inc(ex_done, 1)
            act.wait_ge(c2_ps, 1)
            act.activation(c2T[:, :], banks[6][:, 0:E], ACT.Copy).then_inc(c2_done, 1)
            act.wait_ge(c2_ps, 2)
            act.activation(c2rows[:, :], banks[7][0:E, 0:D], ACT.Copy).then_inc(c2_done, 1)
            for j in range(E * FC):
                last = act.activation(W2[:, j, :], W2[:, j, :], ACT.Copy, scale=gb[:, j:j + 1])
            last.then_inc(w2_scaled, 1)

            def relu_h(i, par, first):
                act.wait_ge(h_ps, i + 1)
                if not first:
                    act.wait_ge(hn_done, i - 1)
                act.activation(h[:, par, :], ps_h[par][:, :], ACT.Relu).then_inc(h_done, 1)

            def copy_xT(i, par, first):
                act.wait_ge(xgT_ps, i + 1)
                if not first:
                    act.wait_ge(h_ps, i - 1)
                act.activation(xgT[:, par, :], ps_x[par][:, 0:P], ACT.Copy).then_inc(xgT_done, 1)

            def relu_y(i, par, first):
                act.wait_ge(y_ps, i + 1)
                if not first:
                    act.wait_ge(yg_done, i - 1)
                act.activation(y[:, par, :], ps_y[par][:, 0:D], ACT.Relu).then_inc(y_done, 1)

            def sd_h(i, par, first):
                act.wait_ge(mv1_done, i + 1)
                act.activation(sd1[:, par:par + 1], mv1[:, par, 1:2], ACT.Sqrt, bias=c["eps"][:, 0:1]).then_inc(sd1_done, 1)

            def copy_hT(i, par, first):
                act.wait_ge(hnT_ps, i + 1)
                if not first:
                    act.wait_ge(y_ps, i - 1)
                act.activation(hnT[:, par, :], ps_t[par][:, :], ACT.Copy).then_inc(hnT_done, 1)

            def sd_y(i, par, first):
                act.wait_ge(mv2_done, i + 1)
                act.activation(sd2[:, par:par + 1], mv2[:, par, 1:2], ACT.Sqrt, bias=c["eps"][:, 0:1]).then_inc(sd2_done, 1)

            def step(i, u):
                par = u % 2
                static = isinstance(i, int)
                live = lambda t: not static or 0 <= t < NS
                first = lambda t: static and t < 2
                if live(i):
                    relu_h(i, par, first(i))
                if live(i + 1):
                    copy_xT(i + 1, 1 - par, first(i + 1))
                if live(i - 2):
                    relu_y(i - 2, par, first(i - 2))
                if live(i - 1):
                    copy_hT(i - 1, 1 - par, first(i - 1))
                if live(i):
                    sd_h(i, par, first(i))
                if live(i - 2):
                    sd_y(i - 2, par, first(i - 2))

            copy_xT(0, 0, True)
            for i in range(LOOP_START):
                step(i, i % XB)
            with act.Fori(LOOP_START, LOOP_END, XB) as i:
                for u in range(XB):
                    step(i + u, u)
            for i in range(LOOP_END, NS + 2):
                step(i, i % XB)

        @block.tensor
        def _(pe):
            if x_in is not None:
                pe.wait_ge(const, CONSTANTS_MADE)
            ident = c["ident"]
            for half in range(2):
                pe.wait_ge(xn_done, half + 1)
                for t in range(half * HALF, half * HALF + HALF):
                    last = pe.transpose(banks[t // 4][:, t % 4 * P:(t % 4 + 1) * P], xn[:, t, :], ident[:, :])
                    if t % 4 == 3:
                        last.then_inc(xnT_ps, 1)
                if half == 0:
                    pe.wait_ge(w_small, 96)
                for t in range(half * HALF, half * HALF + HALF):
                    if t % 4 == 0:
                        pe.wait_ge(xnT_done, t // 4 + 1)
                    last = pe.matmul(banks[4][:, t * E:(t + 1) * E], xnT[:, t * P:(t + 1) * P], wr[:, :], start=True, stop=True)
            last.then_inc(logits_ps, 1)
            pe.transpose(banks[5][:, 0:2 * E * FC], gb_rows[:, :], ident[0:2 * E * FC, 0:2 * E * FC]).then_inc(gb_ps, 1)
            def be1_W2(experts):
                for e in experts:
                    for ch in range(FC):
                        j = e * FC + ch
                        last = pe.matmul(banks[6][:, e:e + 1], W2[:, j, :], gb[:, E * FC + j:E * FC + j + 1],
                                         start=(ch == 0), stop=(ch == FC - 1))
                return last

            pe.wait_ge(gb_done, 1)
            pe.wait_ge(w2_loaded, 16)
            be1_W2(range(C2_FIRST))
            pe.wait_ge(both_done, 1)
            pe.wait_ge(xnT_done, 4)
            pe.matmul(banks[0][:, 0:NT * E], c["upper"][:, :], both[:, :], start=True, stop=True)
            pe.matmul(banks[1][:, 0:NT * E], c["ones"][:, :], both[:, :], start=True, stop=True).then_inc(counts_ps, 1)
            be1_W2(range(C2_FIRST, E)).then_inc(c2_ps, 1)
            pe.wait_ge(c2_done, 1)
            pe.matmul(banks[7][0:E, 0:D], c2T[:, :], ident[:, :], start=True, stop=False)
            pe.matmul(banks[7][0:E, 0:D], ident[0:E, 0:E], b2rows[:, :], start=False, stop=True).then_inc(c2_ps, 1)
            for q in range(K * NT):
                if q % NT == 0:
                    pe.wait_ge(onehots, 3 * (q // NT + 1))
                    pe.wait_ge(hi_tile, q // NT + 1)
                last = pe.matmul(banks[2][:, 0:3 * NS], lo1h[:, q, :], hi1h[:, q, :, :].rearrange("p w s -> p (w s)"),
                                 start=(q == 0), stop=(q == K * NT - 1))
            last.then_inc(inv_ps, 1)

            def transpose_x(i, par, buf, first):
                pe.wait_ge(xg_loaded[buf], 16 // XB * (i - buf) + 16)
                if not first:
                    pe.wait_ge(xgT_done, i - 1)
                pe.transpose(ps_x[par][:, 0:P], xg[:, buf, :], ident[:, :]).then_inc(xgT_ps, 1)

            def expert(i):
                return pe.value_load(eid[0:1, bass.ds(i, 1)], min_val=0, max_val=E - 1)

            def up(i, e, par, first):
                pe.wait_ge(xgT_done, i + 1)
                if not first:
                    pe.wait_ge(h_done, i - 1)
                pe.matmul(ps_h[par][:, :], c["sel3"][:, :], rows[:, bass.ts(e, F)], start=True, stop=False)
                pe.matmul(ps_h[par][:, :], xgT[:, par, :], W1[:, bass.ts(e, F)], start=False, stop=True).then_inc(h_ps, 1)

            def transpose_h(i, par, first):
                pe.wait_ge(hn_done, i + 1)
                if not first:
                    pe.wait_ge(hnT_done, i - 1)
                for ch in range(FC):
                    last = pe.transpose(ps_t[par][:, ch * P:(ch + 1) * P], hn[:, par, ch * P:(ch + 1) * P], ident[:, :])
                last.then_inc(hnT_ps, 1)

            def down(i, e, par, first):
                pe.wait_ge(hnT_done, i + 1)
                if not first:
                    pe.wait_ge(y_done, i - 1)
                pe.matmul(ps_y[par][:, 0:D], c["sel3"][:, :], rows[:, bass.ds(e * D + E * F, D)], start=True, stop=False)
                w2 = W2[:, :, :].rearrange("p j d -> p (j d)")
                for ch in range(FC):
                    last = pe.matmul(ps_y[par][:, 0:D], hnT[:, par, ch * P:(ch + 1) * P],
                                     w2[:, bass.ds(e * (FC * D) + ch * D, D)], start=False, stop=(ch == FC - 1))
                last.then_inc(y_ps, 1)

            def step(i, u, experts):
                par = u % 2
                static = isinstance(i, int)
                live = lambda t: not static or 0 <= t < NS
                first = lambda t: static and t < 2
                if live(i):
                    experts.append(expert(i))
                    up(i, experts[-1], par, first(i))
                if live(i + 1):
                    transpose_x(i + 1, 1 - par, (u + 1) % XB, first(i + 1))
                if live(i - 2):
                    down(i - 2, experts.pop(0), par, first(i - 2))
                if live(i - 1):
                    transpose_h(i - 1, 1 - par, first(i - 1))

            pe.wait_ge(w1_loaded, 16)
            pe.wait_ge(w2_scaled, 1)
            pe.wait_ge(rows_done, 96)
            pe.wait_ge(c2_done, 2)
            pe.wait_ge(routed, 1)
            transpose_x(0, 0, 0, True)
            kept = [pe.alloc_register(f"{tag}_kept{n}") for n in range(2)]

            def keep(experts):
                for register, e in zip(kept, experts):
                    pe.reg_mov(register, e)

            def recall():
                return [pe.snap(register, min_val=0, max_val=E - 1) for register in kept]

            experts = []
            for i in range(LOOP_START):
                step(i, i % XB, experts)
            keep(experts)
            with pe.Fori(LOOP_START, LOOP_END, XB) as i:
                experts = recall()
                for u in range(XB):
                    step(i + u, u, experts)
                keep(experts)
            experts = recall()
            for i in range(LOOP_END, NS + 2):
                step(i, i % XB, experts)

        @block.vector
        def _(dve):
            count = [0]

            def link(instruction):
                count[0] += 1
                instruction.then_inc(chain_v, 1)
                dve.wait_ge(chain_v, count[0])

            def wide(small):
                return small.unsqueeze(2).to_broadcast([P, NT, E])

            halves = [slice(0, HALF), slice(HALF, NT)]
            def mean_of(n):
                link(dve.tensor_reduce(s1[:, halves[n]], X[:, halves[n], :], AX.X, ALU.add))
                link(dve.tensor_scalar(mean[:, halves[n]], s1[:, halves[n]], 1.0 / D, None, ALU.mult))

            def centre(n):
                dve.tensor_tensor(xn[:, halves[n], :], X[:, halves[n], :],
                                  mean[:, halves[n]].unsqueeze(2).to_broadcast([P, HALF, D]),
                                  ALU.subtract).then_inc(centred, 1)

            def sum_squares(n):
                dve.wait_ge(sq_done, n + 1)
                dve.tensor_reduce(s2[:, halves[n]], sq[:, halves[n], :], AX.X, ALU.add).then_inc(var_done, 1)

            def normalise(n):
                dve.wait_ge(std_done, n + 1)
                link(dve.reciprocal(rstd[:, halves[n]], std[:, halves[n]]))
                dve.tensor_tensor(xn[:, halves[n], :], xn[:, halves[n], :],
                                  rstd[:, halves[n]].unsqueeze(2).to_broadcast([P, HALF, D]), ALU.mult).then_inc(xn_done, 1)

            if x_in is not None:
                dve.wait_ge(x_loaded, 32)
            mean_of(0)
            centre(0)
            mean_of(1)
            sum_squares(0)
            centre(1)
            normalise(0)
            sum_squares(1)
            normalise(1)
            dve.wait_ge(logits_ps, 1)
            if x_in is not None:
                dve.wait_ge(const, CONSTANTS_MADE)
            link(dve.tensor_tensor(logit[:, :, :], banks[4][:, 0:NT * E].rearrange("p (t e) -> p t e", e=E),
                                   br[:, :].unsqueeze(1).to_broadcast([P, NT, E]), ALU.add))
            for k in range(K):
                link(dve.tensor_reduce(top[:, k, :], logit[:, :, :], AX.X, ALU.max))
                link(dve.tensor_tensor(cand[:, :, :], logit[:, :, :], wide(top[:, k, :]), ALU.is_ge))
                link(dve.tensor_tensor(cand[:, :, :], cand[:, :, :],
                                       c["early"][:, :].unsqueeze(1).to_broadcast([P, NT, E]), ALU.mult))
                link(dve.tensor_reduce(best[:, :], cand[:, :, :], AX.X, ALU.max))
                link(dve.tensor_tensor(pick[:, k, :, :], cand[:, :, :], wide(best[:, :]), ALU.is_equal))
                if k == 0:
                    link(dve.scalar_tensor_tensor(out=logit[:, :, :], in0=pick[:, 0, :, :], scalar=-3.0e38,
                                                  in1=logit[:, :, :], op0=ALU.mult, op1=ALU.add))
            dve.tensor_tensor(both[:, :].rearrange("p (t e) -> p t e", e=E), pick[:, 0, :, :], pick[:, 1, :, :],
                              ALU.add).then_inc(both_done, 1)
            dve.tensor_tensor(gden[:, :], top[:, 1, :], top[:, 0, :], ALU.subtract).then_inc(gap_done, 1)
            dve.wait_ge(counts_ps, 1)
            link(dve.tensor_copy(total[:, :].rearrange("p (e t) -> p t e", e=E),
                                 banks[1][:, 0:NT * E].rearrange("p (t e) -> p t e", e=E)))
            link(dve.tensor_tensor_scan(incl[:, :], c["scanmask"][:, :], total[:, :], 0.0, ALU.mult, ALU.add))
            inclv = incl[:, :].rearrange("p (e t) -> p e t", e=E)
            link(dve.tensor_scalar(ntile_i[:, :], inclv[:, :, NT - 1], float(P - 1), None, ALU.add))
            link(dve.tensor_scalar(ntile_i[:, :], ntile_i[:, :], 7, None, ALU.arith_shift_right))
            link(dve.tensor_copy(ntile[:, :], ntile_i[:, :]))
            link(dve.tensor_tensor_scan(ends[:, :], c["scanmask"][:, 1:1 + E], ntile[:, :], 0.0, ALU.mult, ALU.add))
            link(dve.tensor_tensor(base[:, :], ends[:, :], ntile[:, :], ALU.subtract))
            link(dve.tensor_scalar(base[:, :], base[:, :], float(P), None, ALU.mult))
            link(dve.tensor_tensor(before[:, :, :], inclv, total[:, :].rearrange("p (e t) -> p e t", e=E), ALU.subtract))
            link(dve.tensor_tensor(before[:, :, :], before[:, :, :], base[:, :].unsqueeze(2).to_broadcast([P, E, NT]), ALU.add))
            link(dve.tensor_tensor(posall[:, :, :], banks[0][:, 0:NT * E].rearrange("p (t e) -> p t e", e=E),
                                   before[:, :, :].rearrange("p e t -> p t e"), ALU.add))
            for k in range(K):
                link(dve.tensor_tensor(possel[:, :, :], posall[:, :, :], pick[:, k, :, :], ALU.mult))
                link(dve.tensor_reduce(pos[:, k, :], possel[:, :, :], AX.X, ALU.add))
            link(dve.tensor_copy(pos_i[:, :], pos[:, :, :].rearrange("p k t -> p (k t)")))
            link(dve.tensor_scalar(hilo_i[:, 0, :], pos_i[:, :], 7, None, ALU.arith_shift_right))
            link(dve.tensor_scalar(hilo_i[:, 1, :], pos_i[:, :], P - 1, None, ALU.bitwise_and))
            link(dve.tensor_copy(hilo[:, :, :], hilo_i[:, :, :]))
            for k in range(K):
                qs = slice(k * NT, (k + 1) * NT)
                dve.tensor_tensor(hi1h[:, qs, 0, :], c["iota"][:, 0:NS].unsqueeze(1).to_broadcast([P, NT, NS]),
                                  hilo[:, 0, qs].unsqueeze(2).to_broadcast([P, NT, NS]), ALU.is_equal).then_inc(onehots, 1)
                dve.tensor_tensor(lo1h[:, qs, :], c["iota"][:, :].unsqueeze(1).to_broadcast([P, NT, P]),
                                  hilo[:, 1, qs].unsqueeze(2).to_broadcast([P, NT, P]), ALU.is_equal).then_inc(onehots, 1)
                dve.wait_ge(onehots, 3 * k + 1)
                dve.tensor_scalar(hi1h[:, qs, 1, :], hi1h[:, qs, 0, :], c["part"][:, 0:1], None, ALU.mult).then_inc(onehots, 1)
            link(dve.tensor_tensor(past[:, :, :], c["iota"][0:1, 0:NS].unsqueeze(2).to_broadcast([1, NS, E]),
                                   ends[0:1, :].unsqueeze(1).to_broadcast([1, NS, E]), ALU.is_ge))
            link(dve.tensor_reduce(eid_f[:, :], past[:, :, :], AX.X, ALU.add))
            link(dve.tensor_scalar(eid_f[:, :], eid_f[:, :], float(E - 1), None, ALU.min))
            link(dve.tensor_copy(eid[:, 0:NS], eid_f[:, :]))
            dve.wait_ge(inv_ps, 1)
            link(dve.tensor_copy(inv[:, :, :], banks[2][:, 0:3 * NS].rearrange("p (w s) -> p w s", w=3)))
            link(dve.scalar_tensor_tensor(out=code[:, :], in0=inv[:, 2, :], scalar=float(P), in1=inv[:, 1, :],
                                          op0=ALU.mult, op1=ALU.add))
            link(dve.tensor_scalar(late[:, :], code[:, :], float(TOK), -float(TOK), ALU.is_ge, ALU.mult))
            link(dve.tensor_tensor(late[:, :], late[:, :], code[:, :], ALU.add))
            link(dve.tensor_copy(gat_u[:, 0:NS], late[:, :]))
            link(dve.tensor_scalar(dump[:, :], inv[:, 0, :], -1.0, 1.0, ALU.mult, ALU.add))
            link(dve.tensor_tensor(dump[:, :], dump[:, :], c["dumprow"][:, 0:NS], ALU.mult))
            link(dve.tensor_tensor(code[:, :], code[:, :], dump[:, :], ALU.add))
            dve.tensor_copy(sca_u[:, 0:NS], code[:, :]).then_inc(routed, 1)
            dve.wait_ge(ex_done, 1)
            link(dve.tensor_scalar(gden[:, :], ex[:, :], 1.0, 2.0, ALU.add, ALU.mult))
            link(dve.reciprocal(gate[:, 0, :], gden[:, :]))
            dve.tensor_tensor(gate[:, 1, :], gate[:, 0, :], ex[:, :], ALU.mult).then_inc(gates_done, 1)

            def step(i, u):
                par = u % 2
                static = isinstance(i, int)
                live = lambda t: not static or 0 <= t < NS
                first = lambda t: static and t < 2
                if live(i - 3):
                    e = dve.value_load(eid[0:1, bass.ds(i - 3, 1)], min_val=0, max_val=E - 1)
                if live(i - 1):
                    q = 1 - par
                    dve.wait_ge(sd1_done, i)
                    dve.reciprocal(rs1[:, q:q + 1], sd1[:, q:q + 1]).then_inc(rs1_done, 1)
                    if not first(i - 1):
                        dve.wait_ge(hnT_ps, i - 2)
                    dve.wait_ge(rs1_done, i)
                    dve.tensor_scalar(hn[:, q, :], h[:, q, :], mv1[:, q, 0:1], rs1[:, q:q + 1],
                                      ALU.subtract, ALU.mult).then_inc(hn_done, 1)
                if live(i):
                    dve.wait_ge(h_done, i + 1)
                    dve.bn_stats(stat1[:, par, :], h[:, par, :]).then_inc(measured, 1)
                if live(i - 2):
                    dve.wait_ge(y_done, i - 1)
                    dve.bn_stats(stat2[:, par, :], y[:, par, :]).then_inc(measured, 1)
                if live(i - 3):
                    q = 1 - par
                    dve.wait_ge(sd2_done, i - 2)
                    dve.reciprocal(rs2[:, q:q + 1], sd2[:, q:q + 1]).then_inc(measured, 1)
                dve.wait_ge(measured, 3 * i - 2 if not static else
                            min(i + 1, NS) + min(max(i - 1, 0), NS) + max(i - 2, 0))
                if live(i - 3):
                    dve.scalar_tensor_tensor(out=yg[:, q, :], in0=y[:, q, :], scalar=mv2[:, q, 0:1],
                                             in1=g2[:, bass.ts(e, D)], op0=ALU.subtract, op1=ALU.mult).then_inc(yg_done, 1)
                if live(i):
                    dve.bn_aggr(mv1[:, par, :], stat1[:, par, :]).then_inc(mv1_done, 1)
                if live(i - 2):
                    dve.bn_aggr(mv2[:, par, :], stat2[:, par, :]).then_inc(mv2_done, 1)
                if live(i - 3):
                    if not (static and i < 5):
                        dve.wait_ge(y_stored[q], 8 * (i - 3 - q))
                    dve.wait_ge(yg_done, i - 2)
                    dve.scalar_tensor_tensor(out=yo[:, q, :], in0=yg[:, q, :], scalar=rs2[:, q:q + 1],
                                             in1=be2[:, bass.ts(e, D)], op0=ALU.mult, op1=ALU.add).then_inc(yo_done, 1)

            dve.wait_ge(w_post, 32)
            for i in range(LOOP_START):
                step(i, i % XB)
            with dve.Fori(LOOP_START, LOOP_END, XB) as i:
                for u in range(XB):
                    step(i + u, u)
            for i in range(LOOP_END, NS + 3):
                step(i, i % XB)
            for n, ts in enumerate(halves):
                dve.wait_ge(yk_loaded[n], 32)
                link(dve.tensor_tensor(Yk[:, 0, ts, :], Yk[:, 0, ts, :],
                                       gate[:, 0, ts].unsqueeze(2).to_broadcast([P, HALF, D]), ALU.mult))
                link(dve.tensor_tensor(X[:, ts, :], X[:, ts, :], Yk[:, 0, ts, :], ALU.add))
                dve.wait_ge(prod2, n + 1)
                dve.tensor_tensor(X[:, ts, :], X[:, ts, :], Yk[:, 1, ts, :], ALU.add).then_inc(x_new, 1)
            dve.wait_ge(x_new, 2)


B = 2
T = TOK // B
QT = T // P
NH = 16
HS = 64
NP = NH // 2
NB = B * NP
VC = 2 * HS + 1
CHUNKS = [(Q, j, max(j * P, Q * 512), (Q + 1) * 512 - max(j * P, Q * 512)) for Q in range(2) for j in range(4 * Q + 4)]
NC = len(CHUNKS)
MAXES = [(i, k0, min((i + 1) * P - k0, 512)) for i in range(QT) for k0 in range(0, (i + 1) * P, 512)]
assert len(MAXES) == NC
MAX_AT = [2, 2, 2, 2, 1, 1, 1, 1, 0, 0, 0, 0]
assert sum(MAX_AT) == NC
LAG = 4
RF = 4
RP = 6
assert NC % RF == 0 and NC % RP == 0
P_SCALE = 16.0
NEG = -1.0e30
VMAX = 2.0 ** 14


def wait(eng, semaphore, value):
    if not isinstance(value, int) or value > 0:
        eng.wait_ge(semaphore, value)


def attention_phase(nc, c, w, X):
    F32R = mybir.dt.float32r
    FP16 = mybir.dt.float16
    ctx = ExitStack()
    with ctx:
        def sb(name, shape, dt=FP32):
            return ctx.enter_context(nc.sbuf_tensor(f"at_{name}", shape, dt))

        def sem(name):
            return nc.alloc_semaphore(name=f"at_{name}")

        s1 = sb("s1", [P, NT])
        mean = sb("mean", [P, NT])
        s2 = sb("s2", [P, NT])
        std = sb("std", [P, NT])
        rstd = sb("rstd", [P, NT])
        xn = sb("xn", [P, NT, D])
        sq = sb("sq", [P, NT, D])
        xnT = sb("xnT", [P, TOK])
        latT = sb("latT", [P, TOK])
        wd = sb("wd", [P, P])
        wo = sb("wo", [P, NP, D])
        wq = sb("wq", [P, P])
        wk = sb("wk", [P, P])
        V = sb("V", [P, NB * 2 * QT * VC], FP16)
        wmax = sb("wmax", [P, 2])
        wmax_all = sb("wmax_all", [P, 2])
        vscale = sb("vscale", [P, 1])
        vunscale = sb("vunscale", [P, 1])
        QH = sb("QH", [P, T], F32R)
        QL = sb("QL", [P, T], F32R)
        KH = sb("KH", [P, T], F32R)
        KL = sb("KL", [P, T], F32R)
        QQ = [[sb(f"QQ{g}{s}", [P, T], F32R) for s in range(2)] for g in range(2)]
        KK = [[sb(f"KK{g}{s}", [P, T], F32R) for s in range(2)] for g in range(2)]
        QM = [sb(f"QM{s}", [P, T], F32R) for s in range(2)]
        KM = [sb(f"KM{s}", [P, T], F32R) for s in range(2)]
        mx = sb("mx", [P, 2, QT])
        m = sb("m", [P, QT])
        mh = sb("mh", [P, QT], BF16)
        mr = sb("mr", [P, QT])
        mdiag = sb("mdiag", [P, QT, 2 * QT], BF16)
        Pf = sb("Pf", [P, RF, 512])
        Ph = sb("Ph", [P, RP, 512], FP16)
        Pl = sb("Pl", [P, RP, 512], FP16)
        rden = sb("rden", [P, 2, 4])
        rs = sb("rs", [P, 2, 4])
        yp = sb("yp", [P, QT, P])
        ypT = sb("ypT", [P, 2, 512])
        wv = yp[:, :, :].rearrange("p t d -> p (t d)")
        fill = ypT[0:HS, :, :].rearrange("p a d -> p (a d)")
        banks = [ctx.enter_context(nc.psum_tensor(f"at_bank{i}", [P, 512], FP32)) for i in range(7)]
        ps_shift = ctx.enter_context(nc.psum_tensor("at_shift", [P, 1024], BF16))
        ps_st = banks[0:2]
        ps_mx = banks[2:4]
        ps_pv = banks[4:6]
        ps_pr = banks[6]
        ps_yT = ps_shift[:, :].bitcast(FP32)
        ps_proj = (ps_pr[:, :], ps_yT)

        w_in = sem("w_in")
        chain_v = sem("chain_v")
        chain_p = sem("chain_p")
        centred = sem("centred")
        sq_done = sem("sq_done")
        var_done = sem("var_done")
        std_done = sem("std_done")
        xn_done = sem("xn_done")
        xnT_ps = sem("xnT_ps")
        xnT_done = sem("xnT_done")
        lat_ps = sem("lat_ps")
        lat_done = sem("lat_done")
        v_ps = sem("v_ps")
        vh_done = sem("vh_done")
        vl_done = sem("vl_done")
        wmax_done = sem("wmax_done")
        wmax_red = sem("wmax_red")
        scale_done = sem("scale_done")
        ones_done = sem("ones_done")
        filled = sem("filled")
        stacks_set = sem("stacks_set")
        wpair = sem("wpair")
        proj_ps = sem("proj_ps")
        high_done = sem("high_done")
        low_done = sem("low_done")
        qk_stack = [sem("qk_stack_a"), sem("qk_stack_b")]
        qm_stack = [sem("qm_stack_a"), sem("qm_stack_b")]
        mx_ps = sem("mx_ps")
        mx_done = sem("mx_done")
        diag_done = sem("diag_done")
        shift_ps = sem("shift_ps")
        shift_done = sem("shift_done")
        st_ps = sem("st_ps")
        exp_done = sem("exp_done")
        ph_done = sem("ph_done")
        pl_done = sem("pl_done")
        pv_ps = sem("pv_ps")
        y_done = sem("y_done")
        yT_ps = sem("yT_ps")
        yT_done = sem("yT_done")
        o_ps = sem("o_ps")
        o_done = sem("o_done")
        y_own = sem("y_own")
        m_own = sem("m_own")

        PROJECT_AT = [3, 4, 5, 6]
        COPY_Y_AT = 2
        OUT_AT = [8, 10]
        TURN_MAX_AT = NC - 3

        block = ctx.enter_context(nc.Block())
        zero_rows = sq[0:HS, 0:T // D, :].rearrange("p a d -> p (a d)")
        HALF = NT // 2
        halves = [slice(0, HALF), slice(HALF, NT)]

        def v_view(v, col):
            t, g = v // 2, v % 2
            view = V[:, :].rearrange("p (b h t v) -> p b h t v", b=B, h=NH, t=QT)
            return view[:, t // QT, 8 * g:8 * g + 8, t % QT, col:col + HS]


        @block.sync
        def _(sp):
            sp.dma_start(wd[:, :], w["w_kv_down"]).then_inc(w_in, 16)
            sp.dma_start(wv, w["w_kv_up"][:, NH * HS:2 * NH * HS]).then_inc(w_in, 16)
            sp.dma_start(wo[:, :, :], w["w_out"].rearrange("(h p) d -> p h d", p=P)).then_inc(w_in, 16)

            def load_weights(n):
                hp = n % NP
                sp.dma_start(wq[:, :], w["w_q"][:, bass.ts(hp, P)]).then_inc(wpair, 16)
                sp.dma_start(wk[:, :], w["w_kv_up"][:, bass.ts(hp, P)]).then_inc(wpair, 16)

            def halves_of(s):
                return (slice(0, HS), slice(HS, P)) if s == 0 else (slice(HS, P), slice(0, HS))

            def build_qk(n, g):
                for operand, sources in ((QQ, (QH, QL)), (KK, (KH, KH))):
                    sp.wait_ge(low_done, 4 * n + (2 if operand is QQ else 4))
                    for s in range(2):
                        own, other = halves_of(s)
                        for rows, src in zip((own, other), sources):
                            sp.dma_start(operand[g][s][rows, :].bitcast(FP32),
                                         src[own, :].bitcast(FP32)).then_inc(qk_stack[s], 16)

            def build_qm(n, s):
                wait(sp, st_ps, NC * (2 * n + s - 1))
                own, _ = halves_of(s)
                for dst, src in ((QM[s][own, :], QH), (KM[s][own, :], KL)):
                    sp.dma_start(dst.bitcast(FP32), src[own, :].bitcast(FP32)).then_inc(qm_stack[s], 16)

            def pair(n, g, more):
                build_qk(n + 1, 1 - g)
                if more:
                    load_weights(n + 2)
                for s in range(2):
                    build_qm(n + 1, s)

            load_weights(0)
            sp.wait_ge(filled, 4)
            for s, rows in ((0, slice(HS, P)), (1, slice(0, HS))):
                sp.dma_start(QM[s][rows, :].bitcast(FP32), zero_rows).then_inc(stacks_set, 16)
                sp.dma_start(KM[s][rows, :].bitcast(FP32), fill).then_inc(stacks_set, 16)
            sp.wait_ge(stacks_set, 64)
            build_qk(0, 0)
            for s in range(2):
                build_qm(0, s)
            load_weights(1)
            pair(0, 0, True)
            with sp.Fori(0, NB // 2 - 2) as twice:
                pair(2 * twice + 1, 1, True)
                pair(2 * twice + 2, 0, True)
            pair(NB - 3, 1, True)
            pair(NB - 2, 0, False)

        def slot_pool(pool, n, s):
            for t, (Q, j, q0, cols) in enumerate(CHUNKS):
                k = NC * (2 * n + s) + t
                pool.wait_ge(ph_done, k + 1)
                wait(pool, pv_ps, k - RP + 1)
                pool.tensor_tensor(Pl[:, t % RP, 0:cols], Pf[:, t % RF, 0:cols], Ph[:, t % RP, 0:cols],
                                   ALU.subtract).then_inc(pl_done, 1)

        @block.gpsimd
        def _(pool):
            pool.memset(V[:, :].rearrange("p (x v) -> p x v", v=VC)[:, :, VC - 1:VC], 1.0).then_inc(ones_done, 1)
            pool.memset(fill, 0.0).then_inc(filled, 1)
            pool.wait_ge(filled, 1)
            pool.memset(fill[0:2 * QT], -1.0).then_inc(filled, 1)
            pool.memset(mx[:, 1, 0:QT // 2], 2 * NEG).then_inc(filled, 1)
            pool.wait_ge(wmax_done, 1)
            pool.partition_all_reduce(wmax_all[:, :], wmax[:, :], P, bass.bass_isa.ReduceOp.max).then_inc(wmax_red, 1)
            pool.wait_ge(var_done, 2)
            pool.memset(zero_rows, 0.0).then_inc(filled, 1)
            for s in range(2):
                slot_pool(pool, 0, s)
            with pool.Fori(1, NB) as n:
                for s in range(2):
                    slot_pool(pool, n, s)

        def slot_scalar(act, n, s, last=False):
            first = isinstance(n, int) and n == 0
            for t in range(NC + 1):
                if t < NC:
                    Q, j, q0, cols = CHUNKS[t]
                    k = NC * (2 * n + s) + t
                    act.wait_ge(st_ps, k + 1)
                    wait(act, pl_done, k - RF + 1)
                    o = q0 % 512
                    act.activation(Pf[:, t % RF, 0:cols], ps_st[t % 2][:, o:o + cols], ACT.Exp,
                                   bias=c["lnscale"][:, 0:1]).then_inc(exp_done, 1)
                if t >= 1:
                    Q, j, q0, cols = CHUNKS[t - 1]
                    k = NC * (2 * n + s) + t - 1
                    act.wait_ge(exp_done, k + 1)
                    wait(act, pv_ps, k - RP + 1)
                    act.activation(Ph[:, (t - 1) % RP, 0:cols], Pf[:, (t - 1) % RF, 0:cols], ACT.Copy).then_inc(ph_done, 1)
                if s == 0 and not last and t in PROJECT_AT:
                    high_part(act, n + 1, PROJECT_AT.index(t))
                if not first and t == COPY_Y_AT:
                    copy_yT(act, n - 1, s)

        def high_part(act, n, part):
            act.wait_ge(proj_ps, 4 * n + part + 1)
            if part == 0:
                for s in range(2):
                    wait(act, qk_stack[s], 64 * n)
                    wait(act, qm_stack[s], 32 * n)
            dst = (QH, KH)[part // 2]
            act.activation(dst[:, part % 2 * 512:(part % 2 + 1) * 512], ps_proj[part % 2], ACT.Copy,
                           scale=(HS ** -0.5, 1.0)[part // 2]).then_inc(high_done, 1)

        def copy_yT(act, n, half):
            act.wait_ge(yT_ps, 2 * n + half + 1)
            act.activation(ypT[:, half, :], ps_yT, ACT.Copy).then_inc(yT_done, 1)

        @block.scalar
        def _(act):
            for half, ts in enumerate(halves):
                act.wait_ge(centred, half + 1)
                act.activation(sq[:, ts, :], xn[:, ts, :], ACT.Square).then_inc(sq_done, 1)
                act.wait_ge(var_done, half + 1)
                act.activation(std[:, ts], s2[:, ts], ACT.Sqrt, bias=c["eps"][:, 0:1], scale=1.0 / D).then_inc(std_done, 1)
            for g in range(4):
                act.wait_ge(xnT_ps, g + 1)
                act.activation(xnT[:, g * 512:(g + 1) * 512], banks[g][:, :], ACT.Copy).then_inc(xnT_done, 1)
            for g in range(4):
                act.wait_ge(lat_ps, g + 1)
                act.activation(latT[:, g * 512:(g + 1) * 512], banks[g][:, :], ACT.Copy).then_inc(lat_done, 1)
            act.wait_ge(scale_done, 1)
            for v in range(2 * NT):
                act.wait_ge(v_ps, v + 1)
                act.activation(v_view(v, HS), banks[v % 4][:, :].rearrange("p (h d) -> p h d", d=HS), ACT.Copy,
                               scale=vscale[:, 0:1]).then_inc(vh_done, 1)
            for part in range(4):
                high_part(act, 0, part)
            for s in range(2):
                slot_scalar(act, 0, s)
            with act.Fori(1, NB - 1) as n:
                for s in range(2):
                    slot_scalar(act, n, s)
            for s in range(2):
                slot_scalar(act, NB - 1, s, last=True)
            for half in range(2):
                copy_yT(act, NB - 1, half)

        def project(pe, n, part):
            if part == 0:
                pe.wait_ge(wpair, 32 * n + 32)
            if part >= 2:
                pe.wait_ge(low_done, 4 * n + part - 1)
            elif part == 1:
                wait(pe, yT_done, 2 * n - 3)
            src = (xnT, latT)[part // 2]
            col = (n // NP) * T + part % 2 * 512
            pe.matmul(ps_proj[part % 2], (wq, wk)[part // 2][:, :], src[:, bass.ds(col, 512)], start=True, stop=True).then_inc(proj_ps, 1)

        def max_chunk(pe, n, g, s, t):
            i, k0, cols = MAXES[t]
            k = NC * (2 * n + s) + t
            if t == 0:
                pe.wait_ge(qk_stack[s], 64 * n + 64)
            wait(pe, mx_done, k - 1)
            wide = max(cols, 256)
            diag = k0 + cols == (i + 1) * P
            last = pe.matmul(ps_mx[t % 2][:, 0:wide], QQ[g][s][:, i * P:(i + 1) * P], KK[g][s][:, k0:k0 + wide],
                             start=True, stop=not diag, skip_group_check=diag)
            if diag:
                last = pe.matmul(ps_mx[t % 2][:, cols - P:cols], c["identb"][:, :], c["negmask"][:, :],
                                 start=False, stop=True, skip_group_check=True)
            last.then_inc(mx_ps, 1)

        def turn_max(pe, n, s):
            pe.wait_ge(diag_done, 2 * n + s + 1)
            h = 2 * n + s
            if s == 0:
                wait(pe, shift_done, h)
                wait(pe, yT_done, 2 * n - 2)
            else:
                wait(pe, yT_done, 2 * n - 1)
                pe.wait_ge(low_done, min(4 * n + 8, 4 * NB) if isinstance(n, int) else 4 * n + 8)
            for i in range(QT):
                last = pe.transpose(ps_shift[0:2 * QT, i * P:(i + 1) * P], mdiag[:, i, :], c["identb"][:, :])
            last.then_inc(shift_ps, 1)

        def scores(pe, n, g, s, t):
            Q, j, q0, cols = CHUNKS[t]
            k = NC * (2 * n + s) + t
            if t == 0:
                pe.wait_ge(qm_stack[s], 32 * n + 32)
                pe.wait_ge(shift_done, 2 * n + s + 1)
            wait(pe, exp_done, k - 1)
            wide = max(cols, 256)
            lo = q0 + cols - wide
            out = ps_st[t % 2][:, lo % 512:lo % 512 + wide]
            diag = j >= 4 * Q
            pe.matmul(out, KK[g][s][:, j * P:(j + 1) * P], QQ[g][s][:, lo:lo + wide], start=True, stop=False, skip_group_check=diag)
            last = pe.matmul(out, KM[s][:, j * P:(j + 1) * P], QM[s][:, lo:lo + wide], start=False, stop=not diag,
                             skip_group_check=diag)
            if diag:
                last = pe.matmul(ps_st[t % 2][:, q0 % 512:q0 % 512 + P], c["negmask"][:, :], c["identb"][:, :],
                                 start=False, stop=True, skip_group_check=True)
            last.then_inc(st_ps, 1)

        def values(pe, n, s, t):
            Q, j, q0, cols = CHUNKS[t]
            k = NC * (2 * n + s) + t
            pe.wait_ge(pl_done, k + 1)
            if j == 0:
                wait(pe, y_done, 2 * (2 * n + s) + Q - 1)
            at = (n * 2 + s) * (QT * VC) + j * VC
            for i in range(q0 // P, (q0 + cols) // P):
                b = i * P - q0
                out = ps_pv[Q][:, (i % 4) * (HS + 1):(i % 4) * (HS + 1) + HS + 1]
                first, final = (j == 0 and i == 4 * Q), j == 4 * Q + 3
                pe.matmul(out, Ph[:, t % RP, b:b + P], V[:, bass.ds(at + HS, HS + 1)],
                          start=first, stop=False, skip_group_check=True)
                pe.matmul(out[:, 0:HS], Ph[:, t % RP, b:b + P], V[:, bass.ds(at, HS)],
                          start=False, stop=False, skip_group_check=True)
                last = pe.matmul(out, Pl[:, t % RP, b:b + P], V[:, bass.ds(at + HS, HS + 1)],
                                 start=False, stop=final, skip_group_check=True)
            last.then_inc(pv_ps, 1)

        def turn_y(pe, n, half):
            pe.wait_ge(y_done, 4 * n + 3 + half)
            if half == 1:
                pe.wait_ge(shift_done, min(2 * n + 4, 2 * NB) if isinstance(n, int) else 2 * n + 4)
                pe.wait_ge(yT_done, 2 * n + 1)
            elif not (isinstance(n, int) and n == NB - 1):
                pe.wait_ge(shift_done, 2 * n + 3)
            for i in range(4):
                last = pe.transpose(ps_yT[:, i * P:(i + 1) * P], yp[:, 4 * half + i, :], c["ident"][:, :])
            last.then_inc(yT_ps, 1)

        def out_product(pe, n, half):
            static = isinstance(n, int)
            pe.wait_ge(yT_done, 2 * n + half + 1)
            pe.wait_ge(low_done, min(4 * n + 12, 4 * NB) if static else 4 * n + 12)
            if static or half == 1:
                wait(pe, o_done, 2 * n + half)
            hp = n % NP
            wof = wo[:, :, :].rearrange("p h d -> p (h d)")
            for i in range(4):
                last = pe.matmul(ps_pr[:, i * P:(i + 1) * P], ypT[:, half, i * P:(i + 1) * P],
                                 wof[:, bass.ts(hp, D)], start=True, stop=True)
            last.then_inc(o_ps, 1)

        def slot_tensor(pe, n, g, s, last=False):
            first = isinstance(n, int) and n == 0
            nn, ng, ns = (n, g, 1) if s == 0 else (n + 1, 1 - g, 0)
            mt = 0
            for t in range(NC):
                scores(pe, n, g, s, t)
                if not (last and s == 1):
                    for _ in range(MAX_AT[t]):
                        max_chunk(pe, nn, ng, ns, mt)
                        mt += 1
                if t >= LAG:
                    values(pe, n, s, t - LAG)
                elif s == 1:
                    values(pe, n, 0, t + NC - LAG)
                elif not first:
                    values(pe, n - 1, 1, t + NC - LAG)
                if s == 0 and not last and t + 1 in PROJECT_AT:
                    project(pe, n + 1, PROJECT_AT.index(t + 1))
                if not first and t + 1 == COPY_Y_AT:
                    turn_y(pe, n - 1, s)
                if s == 1 and not first and t in OUT_AT:
                    out_product(pe, n - 1, OUT_AT.index(t))
                if t == TURN_MAX_AT and not (last and s == 1):
                    turn_max(pe, nn, ns)

        @block.tensor
        def _(pe):
            for t in range(NT):
                if t % HALF == 0:
                    pe.wait_ge(xn_done, t // HALF + 1)
                last = pe.transpose(banks[t // 4][:, t % 4 * P:(t % 4 + 1) * P], xn[:, t, :], c["ident"][:, :])
                if t % 4 == 3:
                    last.then_inc(xnT_ps, 1)
            pe.wait_ge(w_in, 48)
            for g in range(4):
                pe.wait_ge(xnT_done, g + 1)
                pe.matmul(banks[g][:, :], wd[:, :], xnT[:, g * 512:(g + 1) * 512], start=True, stop=True).then_inc(lat_ps, 1)
            for v in range(2 * NT):
                if v % 8 == 0:
                    pe.wait_ge(lat_done, min(4, v // 8 + 1) if v else 4)
                wait(pe, vl_done, v - 3)
                pe.matmul(banks[v % 4][:, :], latT[:, v // 2 * P:(v // 2 + 1) * P], wv[:, v % 2 * 512:(v % 2 + 1) * 512],
                          start=True, stop=True).then_inc(v_ps, 1)
            for part in range(4):
                project(pe, 0, part)
            pe.wait_ge(vl_done, 2 * NT)
            for t in range(NC):
                max_chunk(pe, 0, 0, 0, t)
            turn_max(pe, 0, 0)
            pe.wait_ge(ones_done, 1)
            for s in range(2):
                slot_tensor(pe, 0, 0, s)
            with pe.Fori(0, NB // 2 - 1) as twice:
                for u in range(2):
                    for s in range(2):
                        slot_tensor(pe, 2 * twice + (1 + u), 1 - u, s)
            for s in range(2):
                slot_tensor(pe, NB - 1, 1, s, last=True)
            for t in range(NC - LAG, NC):
                values(pe, NB - 1, 1, t)
            for half in range(2):
                turn_y(pe, NB - 1, half)
                out_product(pe, NB - 1, half)

        def low_part(dve, n, part):
            dve.wait_ge(high_done, 4 * n + part + 1)
            high, low = ((QH, QL), (KH, KL))[part // 2]
            cs = slice(part % 2 * 512, (part % 2 + 1) * 512)
            dve.scalar_tensor_tensor(out=low[:, cs], in0=ps_proj[part % 2], scalar=(HS ** -0.5, 1.0)[part // 2],
                                     in1=high[:, cs].bitcast(FP32), op0=ALU.mult, op1=ALU.subtract).then_inc(low_done, 1)

        def reduce_max(dve, n, s, t):
            i, k0, cols = MAXES[t]
            k = NC * (2 * n + s) + t
            dve.wait_ge(mx_ps, k + 1)
            dve.tensor_reduce(mx[:, k0 // 512, i:i + 1], ps_mx[t % 2][:, 0:cols], AX.X, ALU.max).then_inc(mx_done, 1)

        def output(dve, n, s, Q):
            h = 2 * n + s
            dve.wait_ge(pv_ps, NC * h + (4 if Q == 0 else NC))
            pv = ps_pv[Q][:, 0:4 * (HS + 1)].rearrange("p (i v) -> p i v", v=HS + 1)
            dve.reciprocal(rden[:, Q, :], pv[:, :, HS]).then_inc(y_own, 1)
            dve.wait_ge(y_own, 4 * h + 2 * Q + 1)
            dve.tensor_scalar(rs[:, Q, :], rden[:, Q, :], vunscale[:, 0:1], None, ALU.mult).then_inc(y_own, 1)
            dve.wait_ge(y_own, 4 * h + 2 * Q + 2)
            if s == 0:
                wait(dve, yT_ps, 2 * n - 1 + Q)
            dve.tensor_tensor(yp[:, 4 * Q:4 * Q + 4, s * HS:(s + 1) * HS], pv[:, :, 0:HS],
                              rs[:, Q, :].unsqueeze(2).to_broadcast([P, 4, HS]), ALU.mult).then_inc(y_done, 1)

        def add_output(dve, n, half):
            dve.wait_ge(o_ps, 2 * n + half + 1)
            Xf = X[:, :, :].rearrange("p t d -> p (t d)")
            at = (n // NP) * T + half * 512
            dve.tensor_tensor(Xf[:, bass.ds(at, 512)], ps_pr[:, :], Xf[:, bass.ds(at, 512)], ALU.add).then_inc(o_done, 1)


        def diagonals(dve, n, s):
            h = 2 * n + s
            eye = c["eye"][:, :].rearrange("p (i j) -> p i j", j=QT)
            dve.wait_ge(mx_done, NC * h + NC)
            dve.tensor_tensor(m[:, :], mx[:, 0, :], mx[:, 1, :], ALU.max).then_inc(m_own, 1)
            dve.wait_ge(m_own, 4 * h + 1)
            dve.tensor_copy(mh[:, :], m[:, :]).then_inc(m_own, 1)
            dve.wait_ge(m_own, 4 * h + 2)
            dve.tensor_tensor(mr[:, :], m[:, :], mh[:, :], ALU.subtract).then_inc(m_own, 1)
            wait(dve, shift_ps, h)
            dve.tensor_tensor(mdiag[:, :, 0:QT], eye, mh[:, :].unsqueeze(2).to_broadcast([P, QT, QT]), ALU.mult).then_inc(m_own, 1)
            dve.wait_ge(m_own, 4 * h + 4)
            dve.tensor_tensor(mdiag[:, :, QT:2 * QT], eye, mr[:, :].unsqueeze(2).to_broadcast([P, QT, QT]), ALU.mult).then_inc(diag_done, 1)

        def shift_rows(dve, n, s):
            dve.wait_ge(shift_ps, 2 * n + s + 1)
            r = HS if s == 0 else 0
            dve.tensor_copy(QM[s][r:r + 2 * QT, :], ps_shift[0:2 * QT, :]).then_inc(shift_done, 1)

        def slot_vector(dve, n, s, last=False):
            first = isinstance(n, int) and n == 0
            nn, ns = (n, 1) if s == 0 else (n + 1, 0)
            mt = 0
            for t in range(NC):
                if not (last and s == 1):
                    for _ in range(MAX_AT[t]):
                        reduce_max(dve, nn, ns, mt)
                        mt += 1
                if s == 0 and not last and t in PROJECT_AT:
                    low_part(dve, n + 1, PROJECT_AT.index(t))
                if t == LAG and not (first and s == 0):
                    output(dve, n - 1 if s == 0 else n, 1 - s, 1)
                if t == TURN_MAX_AT - 1 and not (last and s == 1):
                    diagonals(dve, nn, ns)
                if t == LAG + 4:
                    output(dve, n, s, 0)
                if s == 1 and not first and t - 1 in OUT_AT:
                    add_output(dve, n - 1, OUT_AT.index(t - 1))
                if t == TURN_MAX_AT + 1 and not (last and s == 1):
                    shift_rows(dve, nn, ns)

        @block.vector
        def _(dve):
            count = [0]

            def link(instruction):
                count[0] += 1
                instruction.then_inc(chain_v, 1)
                dve.wait_ge(chain_v, count[0])

            dve.wait_ge(w_in, 48)
            link(dve.tensor_reduce(wmax[:, 0:1], wd[:, :], AX.X, ALU.max, apply_absolute_value=True))
            dve.tensor_reduce(wmax[:, 1:2], wv, AX.X, ALU.max, apply_absolute_value=True).then_inc(wmax_done, 1)
            def mean_of(n):
                link(dve.tensor_reduce(s1[:, halves[n]], X[:, halves[n], :], AX.X, ALU.add))
                link(dve.tensor_scalar(mean[:, halves[n]], s1[:, halves[n]], 1.0 / D, None, ALU.mult))

            def centre(n):
                dve.tensor_tensor(xn[:, halves[n], :], X[:, halves[n], :],
                                  mean[:, halves[n]].unsqueeze(2).to_broadcast([P, HALF, D]),
                                  ALU.subtract).then_inc(centred, 1)

            def sum_squares(n):
                dve.wait_ge(sq_done, n + 1)
                dve.tensor_reduce(s2[:, halves[n]], sq[:, halves[n], :], AX.X, ALU.add).then_inc(var_done, 1)

            def normalise(n):
                dve.wait_ge(std_done, n + 1)
                link(dve.reciprocal(rstd[:, halves[n]], std[:, halves[n]]))
                dve.tensor_tensor(xn[:, halves[n], :], xn[:, halves[n], :],
                                  rstd[:, halves[n]].unsqueeze(2).to_broadcast([P, HALF, D]), ALU.mult).then_inc(xn_done, 1)

            mean_of(0)
            centre(0)
            mean_of(1)
            sum_squares(0)
            centre(1)
            normalise(0)
            sum_squares(1)
            normalise(1)
            dve.wait_ge(wmax_red, 1)
            link(dve.tensor_tensor(vscale[:, :], wmax_all[:, 0:1], wmax_all[:, 1:2], ALU.mult))
            link(dve.tensor_scalar(vscale[:, :], vscale[:, :], D * D * math.sqrt(D) / VMAX, 1e-30, ALU.mult, ALU.max))
            link(dve.reciprocal(vscale[:, :], vscale[:, :]))
            dve.reciprocal(vunscale[:, :], vscale[:, :]).then_inc(scale_done, 1)
            for v in range(2 * NT):
                dve.wait_ge(vh_done, v + 1)
                dve.scalar_tensor_tensor(out=v_view(v, 0), in0=banks[v % 4][:, :].rearrange("p (h d) -> p h d", d=HS),
                                         scalar=vscale[:, 0:1], in1=v_view(v, HS), op0=ALU.mult, op1=ALU.subtract).then_inc(vl_done, 1)
            for part in range(4):
                low_part(dve, 0, part)
            dve.wait_ge(filled, 3)
            for t in range(NC):
                reduce_max(dve, 0, 0, t)
            diagonals(dve, 0, 0)
            dve.wait_ge(stacks_set, 64)
            shift_rows(dve, 0, 0)
            for s in range(2):
                slot_vector(dve, 0, s)
            with dve.Fori(1, NB - 1) as n:
                for s in range(2):
                    slot_vector(dve, n, s)
            for s in range(2):
                slot_vector(dve, NB - 1, s, last=True)
            output(dve, NB - 1, 1, 1)
            for half in range(2):
                add_output(dve, NB - 1, half)
            dve.wait_ge(o_done, 2 * NB)


def program(nc, x, w_kv_down, w_kv_up, w_q, w_out, Wr, br, W1, b1, g1, be1, W2, b2, g2, be2, out, phases="faf"):
    w = dict(Wr=Wr, br=br, W1=W1, b1=b1, g1=g1, be1=be1, W2=W2, b2=b2, g2=g2, be2=be2)
    ctx = ExitStack()
    with ctx:
        def sb(name, shape, dt=FP32):
            return ctx.enter_context(nc.sbuf_tensor(name, shape, dt))
        c = dict(ident=sb("ident", [P, P]), upper=sb("upper", [P, P], BF16), ones=sb("ones", [P, P], BF16),
                 sel3=sb("sel3", [P, P], BF16), scanmask=sb("scanmask", [P, E * NT]), eps=sb("eps", [P, 1]),
                 iota=sb("iota", [P, P]), part=sb("part", [P, 1]), early=sb("early", [P, E]),
                 pairtile=sb("pairtile", [P, K * NT]), dumprow=sb("dumprow", [P, NS + 1]),
                 identb=sb("identb", [P, P], BF16), negmask=sb("negmask", [P, P], BF16),
                 eye=sb("eye", [P, QT * QT]), lnscale=sb("lnscale", [P, 1]))
        X = sb("X", [P, NT, D])
        scratch = dict(xn=nc.dram_tensor("xn_rows", (TOK, D), FP32).ap(),
                       y=nc.dram_tensor("y_rows", (K * TOK + 2 * P, D), FP32).ap())
        with nc.cleanup_on_exit():
            ffn_phase(nc, "f0", c, w, X, scratch, x_in=x, x_out=out if phases == "f" else None)
        if "a" in phases:
            with nc.cleanup_on_exit():
                attention_phase(nc, c, dict(w_kv_down=w_kv_down, w_kv_up=w_kv_up, w_q=w_q, w_out=w_out), X)
        if phases == "fa":
            done = ctx.enter_context(nc.semaphore("done"))
            with nc.Block() as block:
                @block.sync
                def _(sp):
                    sp.dma_start(out.rearrange("b (t p) d -> p (b t) d", p=P), X[:, :, :]).then_inc(done, 16)
                    sp.wait_ge(done, 16)
        if phases == "faf":
            ffn_phase(nc, "f1", c, w, X, scratch, x_out=out)


_INS = ["L0_attn_x", "L0_attn_w_kv_down", "L0_attn_w_kv_up", "L0_attn_w_q", "L0_attn_w_out",
        "L0_ffn_Wr", "L0_ffn_br", "L0_ffn_W1", "L0_ffn_b1", "L0_ffn_g1", "L0_ffn_be1",
        "L0_ffn_W2", "L0_ffn_b2", "L0_ffn_g2", "L0_ffn_be2"]
_OUTS = [((2, 1024, 128), "float32")]


def kernel(**inputs):
    import numpy as _np
    import concourse.bacc as _bacc
    from concourse import mybir as _mybir
    from concourse.bass_utils import run_bass_kernel_spmd as _run

    nc = _bacc.Bacc("TRN2", target_bir_lowering=False, num_devices=1)
    arrays, args = {}, []
    for name in _INS:
        a = _np.ascontiguousarray(inputs[name])
        arrays[f"in_{name}_dram"] = a
        args.append(nc.dram_tensor(f"in_{name}_dram", a.shape, _mybir.dt.from_np(a.dtype), kind="ExternalInput").ap())
    for i, (shape, dtype) in enumerate(_OUTS):
        dt = _mybir.dt.from_np(_np.dtype(dtype))
        args.append(nc.dram_tensor(f"out_{i}_dram", shape, dt, kind="ExternalOutput").ap())
    program(nc, *args)
    r = _run(nc, [arrays], core_ids=[0])
    return r.results[0]["out_0_dram"]
```

```python
import math
from contextlib import ExitStack

import concourse.bass as bass
from concourse import mybir

FP32 = mybir.dt.float32
BF16 = mybir.dt.bfloat16
I32 = mybir.dt.int32
U32 = mybir.dt.uint32
ALU = mybir.AluOpType
ACT = mybir.ActivationFunctionType
AX = mybir.AxisListType

P = 128
D = 128
TOK = 2048
NT = TOK // P
E = 8
K = 2
F = 512
FC = F // P
EPS = 1e-5
NS = K * TOK // P + E - 1
XB = 4
LEAD = 8
LOOP_START = 2 * XB
LOOP_END = NS - LEAD - (NS - LEAD) % XB
XN_ACT = 3
W2_ACT = 24
C2_FIRST = 2
DUMP = K * TOK


def make_constants(nc, pool_eng, c, made):
    pool_eng.memset(c["ident"][:, :], 0.0).then_inc(made, 1)
    pool_eng.memset(c["upper"][:, :], 1.0).then_inc(made, 1)
    pool_eng.memset(c["ones"][:, :], 1.0).then_inc(made, 1)
    pool_eng.memset(c["sel3"][:, :], 0.0).then_inc(made, 1)
    pool_eng.memset(c["scanmask"][:, :], 1.0).then_inc(made, 1)
    pool_eng.memset(c["eps"][:, :], EPS).then_inc(made, 1)
    pool_eng.iota(c["iota"][:, :], [[1, P]], base=0, channel_multiplier=0,
                  allow_small_or_imprecise_dtypes=True).then_inc(made, 1)
    pool_eng.iota(c["part"][:, :], [[0, 1]], base=0, channel_multiplier=1,
                  allow_small_or_imprecise_dtypes=True).then_inc(made, 1)
    pool_eng.iota(c["early"][:, :], [[-1, E]], base=E, channel_multiplier=0,
                  allow_small_or_imprecise_dtypes=True).then_inc(made, 1)
    pool_eng.iota(c["pairtile"][:, :], [[1, K * NT]], base=0, channel_multiplier=0,
                  allow_small_or_imprecise_dtypes=True).then_inc(made, 1)
    pool_eng.iota(c["dumprow"][:, :], [[0, (NS + 1) // 2], [P, 2]], base=DUMP, channel_multiplier=1,
                  allow_small_or_imprecise_dtypes=True).then_inc(made, 1)
    pool_eng.memset(c["identb"][:, :], 0.0).then_inc(made, 1)
    pool_eng.memset(c["negmask"][:, :], 0.0).then_inc(made, 1)
    pool_eng.memset(c["eye"][:, :], 0.0).then_inc(made, 1)
    pool_eng.memset(c["lnscale"][:, :], math.log(P_SCALE)).then_inc(made, 1)
    pool_eng.wait_ge(made, 15)
    pool_eng.affine_select(out=c["identb"][:, :], in_=c["identb"][:, :], compare_op=ALU.not_equal,
                           fill=1.0, base=0, pattern=[[-1, P]], channel_multiplier=1).then_inc(made, 1)
    pool_eng.affine_select(out=c["negmask"][:, :], in_=c["negmask"][:, :], compare_op=ALU.is_ge,
                           fill=NEG, base=0, pattern=[[-1, P]], channel_multiplier=1).then_inc(made, 1)
    pool_eng.affine_select(out=c["eye"][:, :].rearrange("p (i j) -> p i j", j=QT), in_=c["eye"][:, :].rearrange("p (i j) -> p i j", j=QT),
                           compare_op=ALU.not_equal, fill=1.0, base=0, pattern=[[1, QT], [-1, QT]],
                           channel_multiplier=0).then_inc(made, 1)
    pool_eng.affine_select(out=c["ident"][:, :], in_=c["ident"][:, :], compare_op=ALU.not_equal,
                           fill=1.0, base=0, pattern=[[-1, P]], channel_multiplier=1).then_inc(made, 1)
    pool_eng.affine_select(out=c["upper"][:, :], in_=c["upper"][:, :], compare_op=ALU.is_gt,
                           fill=0.0, base=0, pattern=[[1, P]], channel_multiplier=-1).then_inc(made, 1)
    pool_eng.memset(c["sel3"][0:3, :], 1.0).then_inc(made, 1)
    pool_eng.memset(c["scanmask"][:, :].rearrange("p (e t) -> p e t", e=E)[:, :, 0:1], 0.0).then_inc(made, 1)


CONSTANTS_MADE = 22


def ffn_phase(nc, tag, c, w, X, scratch, x_in=None, x_out=None):
    ctx = ExitStack()
    with ctx:
        def sb(name, shape, dt=FP32):
            return ctx.enter_context(nc.sbuf_tensor(f"{tag}_{name}", shape, dt))

        def sem(name):
            return nc.alloc_semaphore(name=f"{tag}_{name}")

        W1 = sb("W1", [P, E * F])
        W2 = sb("W2", [P, E * FC, D])
        wr = sb("wr", [P, E])
        br = sb("br", [P, E])
        gb_rows = sb("gb_rows", [2 * E * FC, P])
        gb = sb("gb", [P, 2 * E * FC])
        b1 = sb("b1", [P, E * F // P])
        b2rows = sb("b2rows", [E, D])
        c2T = sb("c2T", [P, E])
        c2rows = sb("c2rows", [E, D])
        b1part = sb("b1part", [P, 3, E * F // P], BF16)
        b1rest = sb("b1rest", [P, 2, E * F // P])
        c2part = sb("c2part", [E, 3, D], BF16)
        c2rest = sb("c2rest", [E, 2, D])
        rows = sb("rows", [P, E * F + E * D], BF16)
        g2 = sb("g2", [P, E * D])
        be2 = sb("be2", [P, E * D])
        stats = sb("stats", [P, NT, 6])
        mv = sb("mv", [P, NT, 2])
        negmean = sb("negmean", [P, NT])
        xn = sb("xn", [P, NT, D])
        std = sb("std", [P, NT])
        rstd = sb("rstd", [P, NT])
        xnT = sb("xnT", [P, NT * P])
        logit = sb("logit", [P, NT, E])
        cand = sb("cand", [P, NT, E])
        pick = sb("pick", [P, K, NT, E])
        top = sb("top", [P, K, NT])
        best = sb("best", [P, NT])
        both = sb("both", [P, NT * E], BF16)
        gate = sb("gate", [P, K, NT])
        gden = sb("gden", [P, NT])
        ex = sb("ex", [P, NT])
        total = sb("total", [P, E * NT])
        incl = sb("incl", [P, E * NT])
        before = sb("before", [P, E, NT])
        ntile_i = sb("ntile_i", [P, E], I32)
        ntile = sb("ntile", [P, E])
        ends = sb("ends", [P, E])
        base = sb("base", [P, E])
        posall = sb("posall", [P, NT, E])
        possel = sb("possel", [P, NT, E])
        pos = sb("pos", [P, K, NT])
        pos_i = sb("pos_i", [P, K * NT], I32)
        hilo_i = sb("hilo_i", [P, 2, K * NT], I32)
        hilo = sb("hilo", [P, 2, K * NT])
        lo1h = sb("lo1h", [P, K * NT, P], BF16)
        hi1h = sb("hi1h", [P, K * NT, 3, NS], BF16)
        inv = sb("inv", [P, 3, NS])
        code = sb("code", [P, NS])
        late = sb("late", [P, NS])
        dump = sb("dump", [P, NS])
        gat_u = sb("gat_u", [P, NS + XB], U32)
        sca_u = sb("sca_u", [P, NS + XB], U32)
        past = sb("past", [1, NS, E])
        eid_f = sb("eid_f", [1, NS])
        eid = sb("eid", [1, NS + XB], I32)
        gidx = sb("gidx", [P, XB], U32)
        sidx = sb("sidx", [P, XB], U32)
        xg = sb("xg", [P, XB, D])
        xgT = sb("xgT", [P, 2, P])
        h = sb("h", [P, 2, F])
        hn = sb("hn", [P, 2, F])
        hnT = sb("hnT", [P, 2, F])
        stat1 = sb("stat1", [P, 2, 6])
        mv1 = sb("mv1", [P, 2, 2])
        sd1 = sb("sd1", [P, 2])
        rs1 = sb("rs1", [P, 2])
        y = sb("y", [P, 2, D])
        yg = sb("yg", [P, 2, D])
        yo = sb("yo", [P, 2, D])
        stat2 = sb("stat2", [P, 2, 6])
        mv2 = sb("mv2", [P, 2, 2])
        sd2 = sb("sd2", [P, 2])
        rs2 = sb("rs2", [P, 2])
        Yk = sb("Yk", [P, K, NT, D])

        banks = [ctx.enter_context(nc.psum_tensor(f"{tag}_bank{i}", [P, 512], FP32)) for i in range(8)]
        ps_h = banks[0:2]
        ps_t = banks[2:4]
        ps_y = banks[4:6]
        ps_x = banks[6:8]

        x_loaded = sem("x_loaded")
        w_small = sem("w_small")
        w_post = sem("w_post")
        w1_loaded = sem("w1_loaded")
        w2_loaded = sem("w2_loaded")
        const = sem("const")
        chain_v = sem("chain_v")
        std_done = sem("std_done")
        measured_x = sem("measured_x")
        scales_done = sem("scales_done")
        xn_done = sem("xn_done")
        xn2_done = sem("xn2_done")
        xn_stored = sem("xn_stored")
        xnT_ps = sem("xnT_ps")
        xnT_done = sem("xnT_done")
        logits_ps = sem("logits_ps")
        both_done = sem("both_done")
        counts_ps = sem("counts_ps")
        gap_done = sem("gap_done")
        ex_done = sem("ex_done")
        onehots = sem("onehots")
        hi_tile = sem("hi_tile")
        inv_ps = sem("inv_ps")
        gates_done = sem("gates_done")
        sources_found = sem("sources_found")
        routed = sem("routed")
        gb_ps = sem("gb_ps")
        gb_done = sem("gb_done")
        c2_ps = sem("c2_ps")
        c2_done = sem("c2_done")
        w2_scaled = sem("w2_scaled")
        w2_rest_scaled = sem("w2_rest_scaled")
        rows_zero = sem("rows_zero")
        chain_p = sem("chain_p")
        parts_done = sem("parts_done")
        rows_done = sem("rows_done")
        idx_done = sem("idx_done")
        xg_loaded = [sem(f"xg_loaded{n}") for n in range(XB)]
        xgT_ps = sem("xgT_ps")
        xgT_done = sem("xgT_done")
        h_ps = sem("h_ps")
        h_done = sem("h_done")
        mv1_done = sem("mv1_done")
        sd1_done = sem("sd1_done")
        hn_done = sem("hn_done")
        hnT_ps = sem("hnT_ps")
        hnT_done = sem("hnT_done")
        y_ps = sem("y_ps")
        y_done = sem("y_done")
        mv2_done = sem("mv2_done")
        sd2_done = sem("sd2_done")
        rs1_done = sem("rs1_done")
        measured = sem("measured")
        yo_done = sem("yo_done")
        y_stored = [sem(f"y_stored{n}") for n in range(2)]
        yk_loaded = [[sem(f"yk_loaded{n}{k}") for k in range(K)] for n in range(2)]
        x_new = sem("x_new")
        share = [sem(f"share{k}") for k in range(K)]
        out_stored = sem("out_stored")

        xn_rows = scratch["xn"]
        y_rows = scratch["y"]

        block = ctx.enter_context(nc.Block())
        HALF = NT // 2

        @block.sync
        def _(sp):
            if x_in is not None:
                src = x_in.rearrange("b (t p) d -> p (b t) d", p=P)
                for half in range(2):
                    ts = slice(half * HALF, half * HALF + HALF)
                    sp.dma_start(X[:, ts, :], src[:, ts, :]).then_inc(x_loaded, 16)
            sp.dma_start(wr[:, :], w["Wr"]).then_inc(w_small, 16)
            sp.dma_start(br[:, :], w["br"].partition_broadcast(P)).then_inc(w_small, 16)
            sp.dma_start(gb_rows[0:E * FC, :], w["g1"].rearrange("e (c p) -> (e c) p", p=P)).then_inc(w_small, 16)
            sp.dma_start(gb_rows[E * FC:2 * E * FC, :], w["be1"].rearrange("e (c p) -> (e c) p", p=P)).then_inc(w_small, 16)
            sp.dma_start(b1[:, :], w["b1"].rearrange("e (q j) -> (e q) j", j=E * F // P)).then_inc(w_small, 16)
            sp.dma_start(b2rows[:, :], w["b2"]).then_inc(w_small, 16)
            sp.dma_start(W2[:, :, :], w["W2"].rearrange("e (c p) d -> p (e c) d", p=P)).then_inc(w2_loaded, 16)
            sp.dma_start(W1[:, :].rearrange("p (e f) -> p e f", e=E), w["W1"].rearrange("e d f -> d e f")).then_inc(w1_loaded, 16)
            dst = xn_rows.rearrange("(t p) d -> p t d", p=P)
            for half in range(2):
                ts = slice(half * HALF, half * HALF + HALF)
                sp.wait_ge(xn_done, half + 1)
                sp.wait_ge(xn2_done, half + 1)
                sp.dma_start(dst[:, ts, :], xn[:, ts, :]).then_inc(xn_stored, 16)
            sp.dma_start(g2[:, :], w["g2"].rearrange("e d -> (e d)").partition_broadcast(P)).then_inc(w_post, 16)
            sp.dma_start(be2[:, :], w["be2"].rearrange("e d -> (e d)").partition_broadcast(P)).then_inc(w_post, 16)
            sp.wait_ge(rows_zero, 1)
            sp.wait_ge(parts_done, 1)
            for part in range(3):
                sp.dma_start(rows[part:part + 1, 0:E * F].rearrange("o (p j) -> o p j", p=P),
                             b1part[:, part, :]).then_inc(rows_done, 16)
            sp.wait_ge(parts_done, 2)
            for part in range(3):
                sp.dma_start(rows[part:part + 1, E * F:].rearrange("o (e d) -> o e d", e=E),
                             c2part[:, part, :]).then_inc(rows_done, 16)
            for par in range(2):
                sp.wait_ge(y_stored[par], 16 * len(range(par, NS, 2)))
            for half in range(2):
                ts = slice(half * HALF, half * HALF + HALF)
                for k in range(K):
                    src = y_rows[k * TOK:(k + 1) * TOK, :].rearrange("(t p) d -> p t d", p=P)
                    sp.dma_start(Yk[:, k, ts, :], src[:, ts, :]).then_inc(yk_loaded[half][k], 16)
            if x_out is not None:
                dst = x_out.rearrange("b (t p) d -> p (b t) d", p=P)
                for half in range(2):
                    ts = slice(half * HALF, half * HALF + HALF)
                    sp.wait_ge(x_new, half + 1)
                    sp.dma_start(dst[:, ts, :], X[:, ts, :]).then_inc(out_stored, 16)
                sp.wait_ge(out_stored, 32)

        @block.gpsimd
        def _(pool):
            count = [0]

            def link(instruction):
                count[0] += 1
                instruction.then_inc(chain_p, 1)
                pool.wait_ge(chain_p, count[0])

            def split(whole, part, rest):
                link(pool.tensor_copy(part[:, 0, :], whole[:, :]))
                link(pool.tensor_tensor(rest[:, 0, :], whole[:, :], part[:, 0, :], ALU.subtract))
                link(pool.tensor_copy(part[:, 1, :], rest[:, 0, :]))
                link(pool.tensor_tensor(rest[:, 1, :], rest[:, 0, :], part[:, 1, :], ALU.subtract))
                pool.tensor_copy(part[:, 2, :], rest[:, 1, :]).then_inc(parts_done, 1)

            if x_in is not None:
                make_constants(nc, pool, c, const)
            pool.memset(rows[:, :], 0.0).then_inc(rows_zero, 1)
            pool.wait_ge(w_small, 96)
            split(b1, b1part, b1rest)
            for k in range(K):
                qs = slice(k * NT, (k + 1) * NT)
                pool.wait_ge(onehots, 3 * k + 1)
                pool.tensor_tensor(hi1h[:, qs, 2, :], hi1h[:, qs, 0, :],
                                   c["pairtile"][:, qs].unsqueeze(2).to_broadcast([P, NT, NS]), ALU.mult).then_inc(hi_tile, 1)
            pool.wait_ge(c2_done, 2)
            split(c2rows, c2part, c2rest)

            def token_rows(i, buf):
                if not (isinstance(i, int) and i < XB):
                    pool.wait_ge(xgT_ps, i - (XB - 1))
                pool.tensor_copy(gidx[:, buf:buf + 1], gat_u[:, bass.ds(i, 1)]).then_inc(idx_done, 1)

            def pair_rows(i, buf):
                pool.tensor_copy(sidx[:, buf:buf + 1], sca_u[:, bass.ds(i, 1)]).then_inc(idx_done, 1)

            def gather(buf):
                pool.indirect_dma_start(xg[:, buf, :], None, xn_rows,
                                        bass.IndirectOffsetOnAxis(ap=gidx[:, buf:buf + 1], axis=0),
                                        bounds_check=TOK - 1).then_inc(xg_loaded[buf], 16)

            def step(i, u):
                par = u % 2
                static = isinstance(i, int)
                ahead = not static or i + LEAD < NS
                pool.wait_ge(yo_done, i + 1)
                if ahead:
                    token_rows(i + LEAD, (u + LEAD) % XB)
                pool.wait_ge(idx_done, 2 * i + LEAD + 2 if ahead else NS + i + 1)
                if not (static and i == NS - 1):
                    pair_rows(i + 1, (u + 1) % XB)
                pool.indirect_dma_start(y_rows, bass.IndirectOffsetOnAxis(ap=sidx[:, u:u + 1], axis=0),
                                        yo[:, par, :], None,
                                        bounds_check=K * TOK + 2 * P - 1).then_inc(y_stored[par], 16)
                if ahead:
                    gather((u + LEAD) % XB)

            pool.wait_ge(sources_found, 1)
            pool.wait_ge(xn_stored, 32)
            for i in range(LEAD):
                token_rows(i, i % XB)
                pool.wait_ge(idx_done, i + 1)
                gather(i % XB)
            pool.wait_ge(routed, 1)
            pair_rows(0, 0)
            for i in range(LOOP_START):
                step(i, i % XB)
            with pool.Fori(LOOP_START, LOOP_END, XB) as i:
                for u in range(XB):
                    step(i + u, u)
            for i in range(LOOP_END, NS):
                step(i, i % XB)
            pool.wait_ge(gates_done, 1)
            ts = slice(HALF, NT)
            pool.wait_ge(yk_loaded[1][1], 16)
            pool.tensor_tensor(Yk[:, 1, ts, :], Yk[:, 1, ts, :],
                               gate[:, 1, ts].unsqueeze(2).to_broadcast([P, HALF, D]),
                               ALU.mult).then_inc(share[1], 1)

        @block.scalar
        def _(act):
            if x_in is not None:
                act.wait_ge(const, CONSTANTS_MADE)
            for n in range(2):
                ts = slice(n * HALF, n * HALF + HALF)
                act.wait_ge(measured_x, n + 1)
                act.activation(std[:, ts], mv[:, ts, 1], ACT.Sqrt, bias=c["eps"][:, 0:1]).then_inc(std_done, 1)
            for n in range(2):
                act.wait_ge(scales_done, n + 1)
                for t in range(n * HALF, n * HALF + XN_ACT):
                    last = act.activation(xn[:, t, :], X[:, t, :], ACT.Identity, bias=negmean[:, t:t + 1],
                                          scale=rstd[:, t:t + 1])
                last.then_inc(xn_done, 1)
            for g in range(NT // 4):
                act.wait_ge(xnT_ps, g + 1)
                act.activation(xnT[:, g * 512:(g + 1) * 512], banks[g][:, :], ACT.Copy).then_inc(xnT_done, 1)
            act.wait_ge(gb_ps, 1)
            act.activation(gb[:, :], banks[5][:, 0:2 * E * FC], ACT.Copy).then_inc(gb_done, 1)
            act.wait_ge(gap_done, 1)
            act.activation(ex[:, :], gden[:, :], ACT.Exp).then_inc(ex_done, 1)
            act.wait_ge(c2_ps, 1)
            act.activation(c2T[:, :], banks[6][:, 0:E], ACT.Copy).then_inc(c2_done, 1)
            act.wait_ge(c2_ps, 2)
            act.activation(c2rows[:, :], banks[7][0:E, 0:D], ACT.Copy).then_inc(c2_done, 1)
            for j in range(W2_ACT):
                last = act.activation(W2[:, j, :], W2[:, j, :], ACT.Copy, scale=gb[:, j:j + 1])
            last.then_inc(w2_scaled, 1)

            def relu_h(i, par, first):
                act.wait_ge(h_ps, i + 1)
                if not first:
                    act.wait_ge(hn_done, i - 1)
                act.activation(h[:, par, :], ps_h[par][:, :], ACT.Relu).then_inc(h_done, 1)

            def copy_xT(i, par, first):
                act.wait_ge(xgT_ps, i + 1)
                if not first:
                    act.wait_ge(h_ps, i - 1)
                act.activation(xgT[:, par, :], ps_x[par][:, 0:P], ACT.Copy).then_inc(xgT_done, 1)

            def relu_y(i, par, first):
                act.wait_ge(y_ps, i + 1)
                if not first:
                    act.wait_ge(yo_done, i - 1)
                act.activation(y[:, par, :], ps_y[par][:, 0:D], ACT.Relu).then_inc(y_done, 1)

            def sd_h(i, par, first):
                act.wait_ge(mv1_done, i + 1)
                act.activation(sd1[:, par:par + 1], mv1[:, par, 1:2], ACT.Sqrt, bias=c["eps"][:, 0:1]).then_inc(sd1_done, 1)

            def copy_hT(i, par, first):
                act.wait_ge(hnT_ps, i + 1)
                if not first:
                    act.wait_ge(y_ps, i - 1)
                act.activation(hnT[:, par, :], ps_t[par][:, :], ACT.Copy).then_inc(hnT_done, 1)

            def sd_y(i, par, first):
                act.wait_ge(mv2_done, i + 1)
                act.activation(sd2[:, par:par + 1], mv2[:, par, 1:2], ACT.Sqrt, bias=c["eps"][:, 0:1]).then_inc(sd2_done, 1)

            def step(i, u):
                par = u % 2
                static = isinstance(i, int)
                live = lambda t: not static or 0 <= t < NS
                first = lambda t: static and t < 2
                if live(i):
                    relu_h(i, par, first(i))
                if live(i + 1):
                    copy_xT(i + 1, 1 - par, first(i + 1))
                if live(i - 2):
                    relu_y(i - 2, par, first(i - 2))
                if live(i - 1):
                    copy_hT(i - 1, 1 - par, first(i - 1))
                if live(i):
                    sd_h(i, par, first(i))
                if live(i - 2):
                    sd_y(i - 2, par, first(i - 2))

            copy_xT(0, 0, True)
            for i in range(LOOP_START):
                step(i, i % XB)
            with act.Fori(LOOP_START, LOOP_END, XB) as i:
                for u in range(XB):
                    step(i + u, u)
            for i in range(LOOP_END, NS + 2):
                step(i, i % XB)
            act.wait_ge(gates_done, 1)
            act.wait_ge(yk_loaded[1][0], 16)
            for t in range(HALF, NT):
                last = act.activation(Yk[:, 0, t, :], Yk[:, 0, t, :], ACT.Copy, scale=gate[:, 0, t:t + 1])
            last.then_inc(share[0], 1)

        @block.tensor
        def _(pe):
            if x_in is not None:
                pe.wait_ge(const, CONSTANTS_MADE)
            ident = c["ident"]
            for half in range(2):
                pe.wait_ge(xn_done, half + 1)
                pe.wait_ge(xn2_done, half + 1)
                for t in range(half * HALF, half * HALF + HALF):
                    last = pe.transpose(banks[t // 4][:, t % 4 * P:(t % 4 + 1) * P], xn[:, t, :], ident[:, :])
                    if t % 4 == 3:
                        last.then_inc(xnT_ps, 1)
                if half == 0:
                    pe.wait_ge(w_small, 96)
                for t in range(half * HALF, half * HALF + HALF):
                    if t % 4 == 0:
                        pe.wait_ge(xnT_done, t // 4 + 1)
                    last = pe.matmul(banks[4][:, t * E:(t + 1) * E], xnT[:, t * P:(t + 1) * P], wr[:, :], start=True, stop=True)
            last.then_inc(logits_ps, 1)
            pe.transpose(banks[5][:, 0:2 * E * FC], gb_rows[:, :], ident[0:2 * E * FC, 0:2 * E * FC]).then_inc(gb_ps, 1)
            def be1_W2(experts):
                for e in experts:
                    for ch in range(FC):
                        j = e * FC + ch
                        last = pe.matmul(banks[6][:, e:e + 1], W2[:, j, :], gb[:, E * FC + j:E * FC + j + 1],
                                         start=(ch == 0), stop=(ch == FC - 1))
                return last

            pe.wait_ge(gb_done, 1)
            pe.wait_ge(w2_loaded, 16)
            be1_W2(range(C2_FIRST))
            pe.wait_ge(both_done, 1)
            pe.wait_ge(xnT_done, 4)
            pe.matmul(banks[0][:, 0:NT * E], c["upper"][:, :], both[:, :], start=True, stop=True)
            pe.matmul(banks[1][:, 0:NT * E], c["ones"][:, :], both[:, :], start=True, stop=True).then_inc(counts_ps, 1)
            be1_W2(range(C2_FIRST, E)).then_inc(c2_ps, 1)
            pe.wait_ge(c2_done, 1)
            pe.matmul(banks[7][0:E, 0:D], c2T[:, :], ident[:, :], start=True, stop=False)
            pe.matmul(banks[7][0:E, 0:D], ident[0:E, 0:E], b2rows[:, :], start=False, stop=True).then_inc(c2_ps, 1)
            for q in range(K * NT):
                if q % NT == 0:
                    pe.wait_ge(onehots, 3 * (q // NT + 1))
                    pe.wait_ge(hi_tile, q // NT + 1)
                last = pe.matmul(banks[2][:, 0:3 * NS], lo1h[:, q, :], hi1h[:, q, :, :].rearrange("p w s -> p (w s)"),
                                 start=(q == 0), stop=(q == K * NT - 1))
            last.then_inc(inv_ps, 1)

            def transpose_x(i, par, buf, first):
                pe.wait_ge(xg_loaded[buf], 16 // XB * (i - buf) + 16)
                if not first:
                    pe.wait_ge(xgT_done, i - 1)
                pe.transpose(ps_x[par][:, 0:P], xg[:, buf, :], ident[:, :]).then_inc(xgT_ps, 1)

            def expert(i):
                return pe.value_load(eid[0:1, bass.ds(i, 1)], min_val=0, max_val=E - 1)

            def up(i, e, par, first):
                pe.wait_ge(xgT_done, i + 1)
                if not first:
                    pe.wait_ge(h_done, i - 1)
                pe.matmul(ps_h[par][:, :], c["sel3"][:, :], rows[:, bass.ts(e, F)], start=True, stop=False)
                pe.matmul(ps_h[par][:, :], xgT[:, par, :], W1[:, bass.ts(e, F)], start=False, stop=True).then_inc(h_ps, 1)

            def transpose_h(i, par, first):
                pe.wait_ge(hn_done, i + 1)
                if not first:
                    pe.wait_ge(hnT_done, i - 1)
                for ch in range(FC):
                    last = pe.transpose(ps_t[par][:, ch * P:(ch + 1) * P], hn[:, par, ch * P:(ch + 1) * P], ident[:, :])
                last.then_inc(hnT_ps, 1)

            def down(i, e, par, first):
                pe.wait_ge(hnT_done, i + 1)
                if not first:
                    pe.wait_ge(y_done, i - 1)
                pe.matmul(ps_y[par][:, 0:D], c["sel3"][:, :], rows[:, bass.ds(e * D + E * F, D)], start=True, stop=False)
                w2 = W2[:, :, :].rearrange("p j d -> p (j d)")
                for ch in range(FC):
                    last = pe.matmul(ps_y[par][:, 0:D], hnT[:, par, ch * P:(ch + 1) * P],
                                     w2[:, bass.ds(e * (FC * D) + ch * D, D)], start=False, stop=(ch == FC - 1))
                last.then_inc(y_ps, 1)

            def step(i, u, experts):
                par = u % 2
                static = isinstance(i, int)
                live = lambda t: not static or 0 <= t < NS
                first = lambda t: static and t < 2
                if live(i):
                    up(i, experts[-1], par, first(i))
                if live(i + 1):
                    transpose_x(i + 1, 1 - par, (u + 1) % XB, first(i + 1))
                if live(i - 2):
                    down(i - 2, experts.pop(0), par, first(i - 2))
                if live(i + 1):
                    experts.append(expert(i + 1))
                if live(i - 1):
                    transpose_h(i - 1, 1 - par, first(i - 1))

            pe.wait_ge(w1_loaded, 16)
            pe.wait_ge(w2_scaled, 1)
            pe.wait_ge(w2_rest_scaled, 1)
            pe.wait_ge(rows_done, 96)
            pe.wait_ge(c2_done, 2)
            pe.wait_ge(routed, 1)
            transpose_x(0, 0, 0, True)
            kept = [pe.alloc_register(f"{tag}_kept{n}") for n in range(3)]

            def keep(experts):
                for register, e in zip(kept, experts):
                    pe.reg_mov(register, e)

            def recall():
                return [pe.snap(register, min_val=0, max_val=E - 1) for register in kept]

            experts = [expert(0)]
            for i in range(LOOP_START):
                step(i, i % XB, experts)
            keep(experts)
            with pe.Fori(LOOP_START, LOOP_END, XB) as i:
                experts = recall()
                for u in range(XB):
                    step(i + u, u, experts)
                keep(experts)
            experts = recall()
            for i in range(LOOP_END, NS + 2):
                step(i, i % XB, experts)

        @block.vector
        def _(dve):
            count = [0]

            def link(instruction):
                count[0] += 1
                instruction.then_inc(chain_v, 1)
                dve.wait_ge(chain_v, count[0])

            def wide(small):
                return small.unsqueeze(2).to_broadcast([P, NT, E])

            halves = [slice(0, HALF), slice(HALF, NT)]
            if x_in is not None:
                dve.wait_ge(x_loaded, 32)
            for n in range(2):
                tiles = range(n * HALF, n * HALF + HALF)
                for t in tiles:
                    last = dve.bn_stats(stats[:, t, :], X[:, t, :])
                link(last)
                for t in tiles:
                    last = dve.bn_aggr(mv[:, t, :], stats[:, t, :])
                last.then_inc(measured_x, 1)
            for n in range(2):
                ts = slice(n * HALF, n * HALF + HALF)
                dve.wait_ge(std_done, n + 1)
                link(dve.reciprocal(rstd[:, ts], std[:, ts]))
                dve.scalar_tensor_tensor(out=negmean[:, ts], in0=mv[:, ts, 0], scalar=-1.0, in1=rstd[:, ts],
                                         op0=ALU.mult, op1=ALU.mult).then_inc(scales_done, 1)
                for t in range(n * HALF + XN_ACT, n * HALF + HALF):
                    last = dve.tensor_scalar(xn[:, t, :], X[:, t, :], mv[:, t, 0:1], rstd[:, t:t + 1],
                                             ALU.subtract, ALU.mult)
                last.then_inc(xn2_done, 1)
            dve.wait_ge(logits_ps, 1)
            if x_in is not None:
                dve.wait_ge(const, CONSTANTS_MADE)
            link(dve.tensor_tensor(logit[:, :, :], banks[4][:, 0:NT * E].rearrange("p (t e) -> p t e", e=E),
                                   br[:, :].unsqueeze(1).to_broadcast([P, NT, E]), ALU.add))
            for k in range(K):
                link(dve.tensor_reduce(top[:, k, :], logit[:, :, :], AX.X, ALU.max))
                link(dve.tensor_tensor(cand[:, :, :], logit[:, :, :], wide(top[:, k, :]), ALU.is_ge))
                link(dve.tensor_tensor(cand[:, :, :], cand[:, :, :],
                                       c["early"][:, :].unsqueeze(1).to_broadcast([P, NT, E]), ALU.mult))
                link(dve.tensor_reduce(best[:, :], cand[:, :, :], AX.X, ALU.max))
                link(dve.tensor_tensor(pick[:, k, :, :], cand[:, :, :], wide(best[:, :]), ALU.is_equal))
                if k == 0:
                    link(dve.scalar_tensor_tensor(out=logit[:, :, :], in0=pick[:, 0, :, :], scalar=-3.0e38,
                                                  in1=logit[:, :, :], op0=ALU.mult, op1=ALU.add))
            dve.tensor_tensor(both[:, :].rearrange("p (t e) -> p t e", e=E), pick[:, 0, :, :], pick[:, 1, :, :],
                              ALU.add).then_inc(both_done, 1)
            dve.tensor_tensor(gden[:, :], top[:, 1, :], top[:, 0, :], ALU.subtract).then_inc(gap_done, 1)
            dve.wait_ge(counts_ps, 1)
            link(dve.tensor_copy(total[:, :].rearrange("p (e t) -> p t e", e=E),
                                 banks[1][:, 0:NT * E].rearrange("p (t e) -> p t e", e=E)))
            link(dve.tensor_tensor_scan(incl[:, :], c["scanmask"][:, :], total[:, :], 0.0, ALU.mult, ALU.add))
            inclv = incl[:, :].rearrange("p (e t) -> p e t", e=E)
            link(dve.tensor_scalar(ntile_i[:, :], inclv[:, :, NT - 1], float(P - 1), None, ALU.add))
            link(dve.tensor_scalar(ntile_i[:, :], ntile_i[:, :], 7, None, ALU.arith_shift_right))
            link(dve.tensor_copy(ntile[:, :], ntile_i[:, :]))
            link(dve.tensor_tensor_scan(ends[:, :], c["scanmask"][:, 1:1 + E], ntile[:, :], 0.0, ALU.mult, ALU.add))
            link(dve.tensor_tensor(base[:, :], ends[:, :], ntile[:, :], ALU.subtract))
            link(dve.tensor_scalar(base[:, :], base[:, :], float(P), None, ALU.mult))
            link(dve.tensor_tensor(before[:, :, :], inclv, total[:, :].rearrange("p (e t) -> p e t", e=E), ALU.subtract))
            link(dve.tensor_tensor(before[:, :, :], before[:, :, :], base[:, :].unsqueeze(2).to_broadcast([P, E, NT]), ALU.add))
            link(dve.tensor_tensor(posall[:, :, :], banks[0][:, 0:NT * E].rearrange("p (t e) -> p t e", e=E),
                                   before[:, :, :].rearrange("p e t -> p t e"), ALU.add))
            for k in range(K):
                link(dve.tensor_tensor(possel[:, :, :], posall[:, :, :], pick[:, k, :, :], ALU.mult))
                link(dve.tensor_reduce(pos[:, k, :], possel[:, :, :], AX.X, ALU.add))
            link(dve.tensor_copy(pos_i[:, :], pos[:, :, :].rearrange("p k t -> p (k t)")))
            link(dve.tensor_scalar(hilo_i[:, 0, :], pos_i[:, :], 7, None, ALU.arith_shift_right))
            link(dve.tensor_scalar(hilo_i[:, 1, :], pos_i[:, :], P - 1, None, ALU.bitwise_and))
            link(dve.tensor_copy(hilo[:, :, :], hilo_i[:, :, :]))
            for k in range(K):
                qs = slice(k * NT, (k + 1) * NT)
                dve.tensor_tensor(hi1h[:, qs, 0, :], c["iota"][:, 0:NS].unsqueeze(1).to_broadcast([P, NT, NS]),
                                  hilo[:, 0, qs].unsqueeze(2).to_broadcast([P, NT, NS]), ALU.is_equal).then_inc(onehots, 1)
                dve.tensor_tensor(lo1h[:, qs, :], c["iota"][:, :].unsqueeze(1).to_broadcast([P, NT, P]),
                                  hilo[:, 1, qs].unsqueeze(2).to_broadcast([P, NT, P]), ALU.is_equal).then_inc(onehots, 1)
                dve.wait_ge(onehots, 3 * k + 1)
                dve.tensor_scalar(hi1h[:, qs, 1, :], hi1h[:, qs, 0, :], c["part"][:, 0:1], None, ALU.mult).then_inc(onehots, 1)
            link(dve.tensor_tensor(past[:, :, :], c["iota"][0:1, 0:NS].unsqueeze(2).to_broadcast([1, NS, E]),
                                   ends[0:1, :].unsqueeze(1).to_broadcast([1, NS, E]), ALU.is_ge))
            link(dve.tensor_reduce(eid_f[:, :], past[:, :, :], AX.X, ALU.add))
            link(dve.tensor_scalar(eid_f[:, :], eid_f[:, :], float(E - 1), None, ALU.min))
            link(dve.tensor_copy(eid[:, 0:NS], eid_f[:, :]))
            dve.wait_ge(inv_ps, 1)
            link(dve.tensor_copy(inv[:, :, :], banks[2][:, 0:3 * NS].rearrange("p (w s) -> p w s", w=3)))
            link(dve.scalar_tensor_tensor(out=code[:, :], in0=inv[:, 2, :], scalar=float(P), in1=inv[:, 1, :],
                                          op0=ALU.mult, op1=ALU.add))
            link(dve.tensor_scalar(late[:, :], code[:, :], float(TOK), -float(TOK), ALU.is_ge, ALU.mult))
            link(dve.tensor_tensor(late[:, :], late[:, :], code[:, :], ALU.add))
            dve.tensor_copy(gat_u[:, 0:NS], late[:, :]).then_inc(sources_found, 1)
            link(dve.tensor_scalar(dump[:, :], inv[:, 0, :], -1.0, 1.0, ALU.mult, ALU.add))
            link(dve.tensor_tensor(dump[:, :], dump[:, :], c["dumprow"][:, 0:NS], ALU.mult))
            link(dve.tensor_tensor(code[:, :], code[:, :], dump[:, :], ALU.add))
            dve.tensor_copy(sca_u[:, 0:NS], code[:, :]).then_inc(routed, 1)
            dve.wait_ge(ex_done, 1)
            link(dve.tensor_scalar(gden[:, :], ex[:, :], 1.0, 2.0, ALU.add, ALU.mult))
            link(dve.reciprocal(gate[:, 0, :], gden[:, :]))
            dve.tensor_tensor(gate[:, 1, :], gate[:, 0, :], ex[:, :], ALU.mult).then_inc(gates_done, 1)
            dve.wait_ge(gb_done, 1)
            dve.wait_ge(c2_ps, 1)
            for j in range(W2_ACT, E * FC):
                last = dve.tensor_scalar(W2[:, j, :], W2[:, j, :], gb[:, j:j + 1], None, ALU.mult)
            last.then_inc(w2_rest_scaled, 1)

            def step(i, u):
                par = u % 2
                static = isinstance(i, int)
                live = lambda t: not static or 0 <= t < NS
                first = lambda t: static and t < 2
                if live(i - 3):
                    e = dve.value_load(eid[0:1, bass.ds(i - 3, 1)], min_val=0, max_val=E - 1)
                if live(i - 1):
                    r = 1 - par
                    dve.wait_ge(sd1_done, i)
                    dve.reciprocal(rs1[:, r:r + 1], sd1[:, r:r + 1]).then_inc(rs1_done, 1)
                if live(i - 3):
                    q = 1 - par
                    dve.wait_ge(sd2_done, i - 2)
                    dve.reciprocal(rs2[:, q:q + 1], sd2[:, q:q + 1]).then_inc(measured, 1)
                if live(i - 1):
                    if not first(i - 1):
                        dve.wait_ge(hnT_ps, i - 2)
                    dve.wait_ge(rs1_done, i)
                    dve.tensor_scalar(hn[:, r, :], h[:, r, :], mv1[:, r, 0:1], rs1[:, r:r + 1],
                                      ALU.subtract, ALU.mult).then_inc(hn_done, 1)
                if live(i - 3):
                    dve.scalar_tensor_tensor(out=yg[:, q, :], in0=y[:, q, :], scalar=mv2[:, q, 0:1],
                                             in1=g2[:, bass.ts(e, D)], op0=ALU.subtract, op1=ALU.mult).then_inc(measured, 1)
                if live(i - 3) and not (static and i < 5):
                    dve.wait_ge(y_stored[1 - par], 8 * (i - 3 - (1 - par)))
                if live(i):
                    dve.wait_ge(h_done, i + 1)
                    dve.bn_stats(stat1[:, par, :], h[:, par, :]).then_inc(measured, 1)
                if live(i - 2):
                    dve.wait_ge(y_done, i - 1)
                    dve.bn_stats(stat2[:, par, :], y[:, par, :]).then_inc(measured, 1)
                dve.wait_ge(measured, 4 * i - 4 if not static else
                            min(i + 1, NS) + min(max(i - 1, 0), NS) + 2 * max(i - 2, 0))
                if live(i - 3):
                    dve.scalar_tensor_tensor(out=yo[:, q, :], in0=yg[:, q, :], scalar=rs2[:, q:q + 1],
                                             in1=be2[:, bass.ts(e, D)], op0=ALU.mult, op1=ALU.add).then_inc(yo_done, 1)
                if live(i):
                    dve.bn_aggr(mv1[:, par, :], stat1[:, par, :]).then_inc(mv1_done, 1)
                if live(i - 2):
                    dve.bn_aggr(mv2[:, par, :], stat2[:, par, :]).then_inc(mv2_done, 1)

            dve.wait_ge(w_post, 32)
            for i in range(LOOP_START):
                step(i, i % XB)
            with dve.Fori(LOOP_START, LOOP_END, XB) as i:
                for u in range(XB):
                    step(i + u, u)
            for i in range(LOOP_END, NS + 3):
                step(i, i % XB)
            for k in range(K):
                dve.wait_ge(yk_loaded[0][k], 16)
                for t in range(HALF):
                    last = dve.scalar_tensor_tensor(out=X[:, t, :], in0=Yk[:, k, t, :], scalar=gate[:, k, t:t + 1],
                                                    in1=X[:, t, :], op0=ALU.mult, op1=ALU.add)
                if k == 0:
                    link(last)
                else:
                    last.then_inc(x_new, 1)
            ts = halves[1]
            dve.wait_ge(share[0], 1)
            link(dve.tensor_tensor(X[:, ts, :], X[:, ts, :], Yk[:, 0, ts, :], ALU.add))
            dve.wait_ge(share[1], 1)
            dve.tensor_tensor(X[:, ts, :], X[:, ts, :], Yk[:, 1, ts, :], ALU.add).then_inc(x_new, 1)
            dve.wait_ge(x_new, 2)


B = 2
T = TOK // B
QT = T // P
NH = 16
HS = 64
NP = NH // 2
NB = B * NP
VC = 2 * HS + 1
CHUNKS = [(Q, j, max(j * P, Q * 512), (Q + 1) * 512 - max(j * P, Q * 512)) for Q in range(2) for j in range(4 * Q + 4)]
NC = len(CHUNKS)
MAXES = [(i, k0, min((i + 1) * P - k0, 512)) for i in range(QT) for k0 in range(0, (i + 1) * P, 512)]
assert len(MAXES) == NC
MAX_AT = [2, 2, 1, 2, 1, 2, 1, 1, 0, 0, 0, 0]
assert sum(MAX_AT) == NC
LAG = 4
RF = 4
RP = 6
assert NC % RF == 0 and NC % RP == 0 and LAG == 4
P_SCALE = 16.0
NEG = -1.0e30
VMAX = 2.0 ** 14


def wait(eng, semaphore, value):
    if not isinstance(value, int) or value > 0:
        eng.wait_ge(semaphore, value)


def attention_phase(nc, c, w, X):
    F32R = mybir.dt.float32r
    FP16 = mybir.dt.float16
    ctx = ExitStack()
    with ctx:
        def sb(name, shape, dt=FP32):
            return ctx.enter_context(nc.sbuf_tensor(f"at_{name}", shape, dt))

        def sem(name):
            return nc.alloc_semaphore(name=f"at_{name}")

        xnT_h = sb("xnT_h", [P, TOK], F32R)
        xnT_l = sb("xnT_l", [P, TOK], F32R)
        latT_h = sb("latT_h", [P, TOK], F32R)
        with nc.sbuf_tensor("at_xn", [P, NT, D], FP32) as xn:
            pass
        latT_l = sb("latT_l", [P, TOK], F32R)
        wo = sb("wo", [P, NP, D])
        wqk = sb("wqk", [P, 2, P])
        wqk_h = sb("wqk_h", [P, 2, P], F32R)
        wqk_l = sb("wqk_l", [P, 2, P], F32R)
        V = sb("V", [P, NB * 2 * QT * VC], FP16)
        wmax = sb("wmax", [P, 2])
        wmax_all = sb("wmax_all", [P, 2])
        vscale = sb("vscale", [P, 1])
        vunscale = sb("vunscale", [P, 1])
        QH = sb("QH", [P, T], F32R)
        QL = sb("QL", [P, T], F32R)
        KH = sb("KH", [P, T], F32R)
        KL = sb("KL", [P, T], F32R)
        QQ = [[sb(f"QQ{g}{s}", [P, T], F32R) for s in range(2)] for g in range(2)]
        KK = [[sb(f"KK{g}{s}", [P, T], F32R) for s in range(2)] for g in range(2)]
        QM = [sb(f"QM{s}", [P, T], F32R) for s in range(2)]
        KM = [sb(f"KM{s}", [P, T], F32R) for s in range(2)]
        mx = sb("mx", [P, 2, QT])
        m = sb("m", [P, QT])
        mh = sb("mh", [P, QT], BF16)
        mr = sb("mr", [P, QT])
        mdiag = sb("mdiag", [P, QT, 2 * QT], BF16)
        Pf = sb("Pf", [P, RF, 512])
        with ExitStack() as early:
            def soon(name, shape, dt=FP32):
                return early.enter_context(nc.sbuf_tensor(f"at_{name}", shape, dt))

            stats = soon("stats", [P, NT, 6])
            mv = soon("mv", [P, NT, 2])
            negmean = soon("negmean", [P, NT])
            std = soon("std", [P, NT])
            rstd = soon("rstd", [P, NT])
            wd = soon("wd", [P, P])
            wd_h = soon("wd_h", [P, P], F32R)
            wd_l = soon("wd_l", [P, P], F32R)
            wv_h = soon("wv_h", [P, NH * HS], F32R)
            wv_l = soon("wv_l", [P, NH * HS], F32R)
        Ph = sb("Ph", [P, RP, 512], FP16)
        Pl = sb("Pl", [P, RP, 512], FP16)
        rden = sb("rden", [P, 2, 4])
        rs = sb("rs", [P, 2, 4])
        yp = sb("yp", [P, QT, P])
        ypT = sb("ypT", [P, 2, 512])
        wv = yp[:, :, :].rearrange("p t d -> p (t d)")
        fill = ypT[0:HS, :, :].rearrange("p a d -> p (a d)")
        banks = [ctx.enter_context(nc.psum_tensor(f"at_bank{i}", [P, 512], FP32)) for i in range(7)]
        ps_shift = ctx.enter_context(nc.psum_tensor("at_shift", [P, 1024], BF16))
        ps_st = banks[0:2]
        ps_mx = banks[2:4]
        ps_pv = banks[4:6]
        ps_v = banks[0:2] + banks[4:6]
        ps_pr = banks[6]
        ps_yT = ps_shift[:, :].bitcast(FP32)
        ps_proj = (ps_pr[:, :], ps_yT)

        w_in = sem("w_in")
        wh_done = sem("wh_done")
        wl_done = sem("wl_done")
        wpair_high = sem("wpair_high")
        wpair_low = sem("wpair_low")
        chain_v = sem("chain_v")
        measured_x = sem("measured_x")
        scales_done = sem("scales_done")
        std_done = sem("std_done")
        xn_done = sem("xn_done")
        xn2_done = sem("xn2_done")
        xnT_ps = sem("xnT_ps")
        xnT_high = sem("xnT_high")
        xnT_done = sem("xnT_done")
        lat_ps = sem("lat_ps")
        lat_high = sem("lat_high")
        lat_done = sem("lat_done")
        v_ps = sem("v_ps")
        vh_done = sem("vh_done")
        vl_done = sem("vl_done")
        wmax_done = sem("wmax_done")
        wmax_red = sem("wmax_red")
        scale_done = sem("scale_done")
        ones_done = sem("ones_done")
        filled = sem("filled")
        stacks_set = sem("stacks_set")
        wpair = sem("wpair")
        proj_ps = sem("proj_ps")
        high_done = sem("high_done")
        low_done = sem("low_done")
        qk_stack = [sem("qk_stack_a"), sem("qk_stack_b")]
        qm_stack = [sem("qm_stack_a"), sem("qm_stack_b")]
        mx_ps = sem("mx_ps")
        mx_done = sem("mx_done")
        diag_done = sem("diag_done")
        shift_ps = sem("shift_ps")
        shift_done = sem("shift_done")
        st_ps = sem("st_ps")
        exp_done = sem("exp_done")
        ph_done = sem("ph_done")
        pl_done = sem("pl_done")
        pv_ps = sem("pv_ps")
        y_done = sem("y_done")
        yT_ps = sem("yT_ps")
        yT_done = sem("yT_done")
        o_ps = sem("o_ps")
        o_done = sem("o_done")
        y_own = sem("y_own")
        m_own = sem("m_own")

        PROJECT_AT = [3, 4, 5, 6]
        COPY_Y_AT = 2
        OUT_AT = [8, 10]
        FIRST_MAX_AT = range(2 * NT - 2 * NC - 1, 2 * NT - 1, 2)
        TURN_MAX_AT = NC - 3

        block = ctx.enter_context(nc.Block())
        zero_rows = Pf[0:HS, 0:T // 512, :].rearrange("p a d -> p (a d)")
        HALF = NT // 2
        halves = [slice(0, HALF), slice(HALF, NT)]

        def v_view(v, col):
            t, g = v // 2, v % 2
            view = V[:, :].rearrange("p (b h t v) -> p b h t v", b=B, h=NH, t=QT)
            return view[:, t // QT, 8 * g:8 * g + 8, t % QT, col:col + HS]


        @block.sync
        def _(sp):
            sp.dma_start(wd[:, :], w["w_kv_down"]).then_inc(w_in, 16)
            sp.dma_start(wv, w["w_kv_up"][:, NH * HS:2 * NH * HS]).then_inc(w_in, 16)
            sp.dma_start(wo[:, :, :], w["w_out"].rearrange("(h p) d -> p h d", p=P)).then_inc(w_in, 16)

            def load_weights(n):
                hp = n % NP
                sp.dma_start(wqk[:, 0, :], w["w_q"][:, bass.ts(hp, P)]).then_inc(wpair, 16)
                sp.dma_start(wqk[:, 1, :], w["w_kv_up"][:, bass.ts(hp, P)]).then_inc(wpair, 16)

            def halves_of(s):
                return (slice(0, HS), slice(HS, P)) if s == 0 else (slice(HS, P), slice(0, HS))

            def build_qk(n, g):
                for operand, sources in ((QQ, (QH, QL)), (KK, (KH, KH))):
                    sp.wait_ge(low_done, 4 * n + (2 if operand is QQ else 4))
                    for s in range(2):
                        own, other = halves_of(s)
                        for rows, src in zip((own, other), sources):
                            sp.dma_start(operand[g][s][rows, :].bitcast(FP32),
                                         src[own, :].bitcast(FP32)).then_inc(qk_stack[s], 16)

            def build_qm(n, s):
                wait(sp, st_ps, NC * (2 * n + s - 1))
                own, _ = halves_of(s)
                for dst, src in ((QM[s][own, :], QH), (KM[s][own, :], KL)):
                    sp.dma_start(dst.bitcast(FP32), src[own, :].bitcast(FP32)).then_inc(qm_stack[s], 16)

            def pair(n, g, more):
                build_qk(n + 1, 1 - g)
                if more:
                    load_weights(n + 2)
                for s in range(2):
                    build_qm(n + 1, s)

            load_weights(0)
            sp.wait_ge(filled, 4)
            for s, rows in ((0, slice(HS, P)), (1, slice(0, HS))):
                sp.dma_start(QM[s][rows, :].bitcast(FP32), zero_rows).then_inc(stacks_set, 16)
                sp.dma_start(KM[s][rows, :].bitcast(FP32), fill).then_inc(stacks_set, 16)
            sp.wait_ge(stacks_set, 64)
            build_qk(0, 0)
            for s in range(2):
                build_qm(0, s)
            load_weights(1)
            pair(0, 0, True)
            with sp.Fori(0, NB // 2 - 2) as twice:
                pair(2 * twice + 1, 1, True)
                pair(2 * twice + 2, 0, True)
            pair(NB - 3, 1, True)
            pair(NB - 2, 0, False)

        def slot_pool(pool, n, s):
            for t, (Q, j, q0, cols) in enumerate(CHUNKS):
                k = NC * (2 * n + s) + t
                pool.wait_ge(ph_done, k + 1)
                wait(pool, pv_ps, k - RP + 1)
                pool.tensor_tensor(Pl[:, t % RP, 0:cols], Pf[:, t % RF, 0:cols], Ph[:, t % RP, 0:cols],
                                   ALU.subtract).then_inc(pl_done, 1)

        @block.gpsimd
        def _(pool):
            pool.memset(V[:, :].rearrange("p (x v) -> p x v", v=VC)[:, :, VC - 1:VC], 1.0).then_inc(ones_done, 1)
            pool.memset(fill, 0.0).then_inc(filled, 1)
            pool.wait_ge(filled, 1)
            pool.memset(fill[0:2 * QT], -1.0).then_inc(filled, 1)
            pool.memset(mx[:, 1, 0:QT // 2], 2 * NEG).then_inc(filled, 1)
            pool.wait_ge(wh_done, 2)
            pool.tensor_tensor(wd_l[:, :], wd[:, :], wd_h[:, :].bitcast(FP32), ALU.subtract).then_inc(wl_done, 1)
            pool.tensor_tensor(wv_l[:, :], wv, wv_h[:, :].bitcast(FP32), ALU.subtract).then_inc(wl_done, 1)
            pool.wait_ge(wmax_done, 1)
            pool.partition_all_reduce(wmax_all[:, :], wmax[:, :], P, bass.bass_isa.ReduceOp.max).then_inc(wmax_red, 1)
            pool.memset(zero_rows, 0.0).then_inc(filled, 1)
            for s in range(2):
                slot_pool(pool, 0, s)
            with pool.Fori(1, NB) as n:
                for s in range(2):
                    slot_pool(pool, n, s)

        def slot_scalar(act, n, s, last=False):
            first = isinstance(n, int) and n == 0
            for t in range(NC + 1):
                if s == 0 and not last and t == 1:
                    weights_high(act, n + 1)
                if t < NC:
                    Q, j, q0, cols = CHUNKS[t]
                    k = NC * (2 * n + s) + t
                    act.wait_ge(st_ps, k + 1)
                    wait(act, pl_done, k - RF + 1)
                    o = q0 % 512
                    act.activation(Pf[:, t % RF, 0:cols], ps_st[t % 2][:, o:o + cols], ACT.Exp,
                                   bias=c["lnscale"][:, 0:1]).then_inc(exp_done, 1)
                if t >= 1:
                    Q, j, q0, cols = CHUNKS[t - 1]
                    k = NC * (2 * n + s) + t - 1
                    act.wait_ge(exp_done, k + 1)
                    wait(act, pv_ps, k - RP + 1)
                    act.activation(Ph[:, (t - 1) % RP, 0:cols], Pf[:, (t - 1) % RF, 0:cols], ACT.Copy).then_inc(ph_done, 1)
                if s == 0 and not last and t in PROJECT_AT:
                    high_part(act, n + 1, PROJECT_AT.index(t))
                if not first and t == COPY_Y_AT:
                    copy_yT(act, n - 1, s)

        def weights_high(act, n):
            act.wait_ge(wpair, 32 * n + 32)
            act.activation(wqk_h[:, :, :], wqk[:, :, :], ACT.Copy).then_inc(wpair_high, 1)

        def high_part(act, n, part):
            act.wait_ge(proj_ps, 4 * n + part + 1)
            if part == 0:
                for s in range(2):
                    wait(act, qk_stack[s], 64 * n)
                    wait(act, qm_stack[s], 32 * n)
            dst = (QH, KH)[part // 2]
            act.activation(dst[:, part % 2 * 512:(part % 2 + 1) * 512], ps_proj[part % 2], ACT.Copy,
                           scale=(HS ** -0.5, 1.0)[part // 2]).then_inc(high_done, 1)

        def copy_yT(act, n, half):
            act.wait_ge(yT_ps, 2 * n + half + 1)
            act.activation(ypT[:, half, :], ps_yT, ACT.Copy).then_inc(yT_done, 1)

        @block.scalar
        def _(act):
            for n in range(2):
                ts = slice(n * HALF, n * HALF + HALF)
                act.wait_ge(measured_x, n + 1)
                act.activation(std[:, ts], mv[:, ts, 1], ACT.Sqrt, bias=c["eps"][:, 0:1]).then_inc(std_done, 1)
            act.wait_ge(w_in, 48)
            act.activation(wd_h[:, :], wd[:, :], ACT.Copy).then_inc(wh_done, 1)
            act.activation(wv_h[:, :], wv, ACT.Copy).then_inc(wh_done, 1)
            for n in range(2):
                act.wait_ge(scales_done, n + 1)
                for t in range(n * HALF, n * HALF + XN_ACT):
                    last = act.activation(xn[:, t, :], X[:, t, :], ACT.Identity, bias=negmean[:, t:t + 1],
                                          scale=rstd[:, t:t + 1])
                last.then_inc(xn_done, 1)
            for g in range(4):
                act.wait_ge(xnT_ps, g + 1)
                act.activation(xnT_h[:, g * 512:(g + 1) * 512], banks[g][:, :], ACT.Copy).then_inc(xnT_high, 1)
            weights_high(act, 0)
            for g in range(4):
                act.wait_ge(lat_ps, g + 1)
                act.activation(latT_h[:, g * 512:(g + 1) * 512], banks[g][:, :], ACT.Copy).then_inc(lat_high, 1)
            for part in range(4):
                high_part(act, 0, part)
            act.wait_ge(scale_done, 1)
            for v in range(2 * NT):
                act.wait_ge(v_ps, v + 1)
                act.activation(v_view(v, HS), ps_v[v % 4][:, :].rearrange("p (h d) -> p h d", d=HS), ACT.Copy,
                               scale=vscale[:, 0:1]).then_inc(vh_done, 1)
            for s in range(2):
                slot_scalar(act, 0, s)
            with act.Fori(1, NB - 1) as n:
                for s in range(2):
                    slot_scalar(act, n, s)
            for s in range(2):
                slot_scalar(act, NB - 1, s, last=True)
            for half in range(2):
                copy_yT(act, NB - 1, half)

        def split_product(pe, out, lhs_h, lhs_l, rhs_h, rhs_l):
            pe.matmul(out, lhs_h, rhs_h, start=True, stop=False)
            pe.matmul(out, lhs_h, rhs_l, start=False, stop=False)
            return pe.matmul(out, lhs_l, rhs_h, start=False, stop=True)

        def project(pe, n, part):
            if part == 0:
                pe.wait_ge(wpair_low, n + 1)
            if part >= 2:
                pe.wait_ge(low_done, 4 * n + part - 1)
            elif part == 1:
                wait(pe, yT_done, 2 * n - 3)
            high, low = ((xnT_h, xnT_l), (latT_h, latT_l))[part // 2]
            col = (n // NP) * T + part % 2 * 512
            split_product(pe, ps_proj[part % 2], wqk_h[:, part // 2, :], wqk_l[:, part // 2, :],
                          high[:, bass.ds(col, 512)], low[:, bass.ds(col, 512)]).then_inc(proj_ps, 1)

        def max_chunk(pe, n, g, s, t):
            i, k0, cols = MAXES[t]
            k = NC * (2 * n + s) + t
            if t == 0:
                pe.wait_ge(qk_stack[s], 64 * n + 64)
            wait(pe, mx_done, k - 1)
            wide = max(cols, 256)
            diag = k0 + cols == (i + 1) * P
            last = pe.matmul(ps_mx[t % 2][:, 0:wide], QQ[g][s][:, i * P:(i + 1) * P], KK[g][s][:, k0:k0 + wide],
                             start=True, stop=not diag, skip_group_check=diag)
            if diag:
                last = pe.matmul(ps_mx[t % 2][:, cols - P:cols], c["identb"][:, :], c["negmask"][:, :],
                                 start=False, stop=True, skip_group_check=True)
            last.then_inc(mx_ps, 1)

        def turn_max(pe, n, s):
            pe.wait_ge(diag_done, 2 * n + s + 1)
            h = 2 * n + s
            if s == 0:
                wait(pe, shift_done, h)
                wait(pe, yT_done, 2 * n - 2)
            else:
                wait(pe, yT_done, 2 * n - 1)
                pe.wait_ge(low_done, min(4 * n + 8, 4 * NB) if isinstance(n, int) else 4 * n + 8)
            for i in range(QT):
                last = pe.transpose(ps_shift[0:2 * QT, i * P:(i + 1) * P], mdiag[:, i, :], c["identb"][:, :])
            last.then_inc(shift_ps, 1)

        def scores(pe, n, g, s, t):
            Q, j, q0, cols = CHUNKS[t]
            k = NC * (2 * n + s) + t
            if t == 0:
                pe.wait_ge(qm_stack[s], 32 * n + 32)
                pe.wait_ge(shift_done, 2 * n + s + 1)
            wait(pe, exp_done, k - 1)
            wide = max(cols, 256)
            lo = q0 + cols - wide
            out = ps_st[t % 2][:, lo % 512:lo % 512 + wide]
            diag = j >= 4 * Q
            pe.matmul(out, KK[g][s][:, j * P:(j + 1) * P], QQ[g][s][:, lo:lo + wide], start=True, stop=False, skip_group_check=diag)
            last = pe.matmul(out, KM[s][:, j * P:(j + 1) * P], QM[s][:, lo:lo + wide], start=False, stop=not diag,
                             skip_group_check=diag)
            if diag:
                last = pe.matmul(ps_st[t % 2][:, q0 % 512:q0 % 512 + P], c["negmask"][:, :], c["identb"][:, :],
                                 start=False, stop=True, skip_group_check=True)
            last.then_inc(st_ps, 1)

        def values(pe, n, s, t):
            Q, j, q0, cols = CHUNKS[t]
            k = NC * (2 * n + s) + t
            pe.wait_ge(pl_done, k + 1)
            if j == 0:
                wait(pe, y_done, 2 * (2 * n + s) + Q - 1)
            at = (n * 2 + s) * (QT * VC) + j * VC
            for i in range(q0 // P, (q0 + cols) // P):
                b = i * P - q0
                out = ps_pv[Q][:, (i % 4) * (HS + 1):(i % 4) * (HS + 1) + HS + 1]
                first, final = (j == 0 and i == 4 * Q), j == 4 * Q + 3
                pe.matmul(out, Ph[:, t % RP, b:b + P], V[:, bass.ds(at + HS, HS + 1)],
                          start=first, stop=False, skip_group_check=True)
                pe.matmul(out[:, 0:HS], Ph[:, t % RP, b:b + P], V[:, bass.ds(at, HS)],
                          start=False, stop=False, skip_group_check=True)
                last = pe.matmul(out, Pl[:, t % RP, b:b + P], V[:, bass.ds(at + HS, HS + 1)],
                                 start=False, stop=final, skip_group_check=True)
            last.then_inc(pv_ps, 1)

        def turn_y(pe, n, half):
            pe.wait_ge(y_done, 4 * n + 3 + half)
            if half == 1:
                pe.wait_ge(shift_done, min(2 * n + 4, 2 * NB) if isinstance(n, int) else 2 * n + 4)
                pe.wait_ge(yT_done, 2 * n + 1)
            elif not (isinstance(n, int) and n == NB - 1):
                pe.wait_ge(shift_done, 2 * n + 3)
            for i in range(4):
                last = pe.transpose(ps_yT[:, i * P:(i + 1) * P], yp[:, 4 * half + i, :], c["ident"][:, :])
            last.then_inc(yT_ps, 1)

        def out_product(pe, n, half):
            static = isinstance(n, int)
            pe.wait_ge(yT_done, 2 * n + half + 1)
            pe.wait_ge(low_done, min(4 * n + 12, 4 * NB) if static else 4 * n + 12)
            if static or half == 1:
                wait(pe, o_done, 2 * n + half)
            hp = n % NP
            wof = wo[:, :, :].rearrange("p h d -> p (h d)")
            for i in range(4):
                last = pe.matmul(ps_pr[:, i * P:(i + 1) * P], ypT[:, half, i * P:(i + 1) * P],
                                 wof[:, bass.ts(hp, D)], start=True, stop=True)
            last.then_inc(o_ps, 1)

        def slot_tensor(pe, n, g, s, last=False):
            first = isinstance(n, int) and n == 0
            nn, ng, ns = (n, g, 1) if s == 0 else (n + 1, 1 - g, 0)
            mt = 0
            for t in range(NC):
                scores(pe, n, g, s, t)
                if not (last and s == 1):
                    for _ in range(MAX_AT[t]):
                        max_chunk(pe, nn, ng, ns, mt)
                        mt += 1
                if t >= LAG:
                    values(pe, n, s, t - LAG)
                elif s == 1:
                    values(pe, n, 0, t + NC - LAG)
                elif not first:
                    values(pe, n - 1, 1, t + NC - LAG)
                if s == 0 and not last and t + 1 in PROJECT_AT:
                    project(pe, n + 1, PROJECT_AT.index(t + 1))
                if not first and t + 1 == COPY_Y_AT:
                    turn_y(pe, n - 1, s)
                if s == 1 and not first and t in OUT_AT:
                    out_product(pe, n - 1, OUT_AT.index(t))
                if t == TURN_MAX_AT and not (last and s == 1):
                    turn_max(pe, nn, ns)

        @block.tensor
        def _(pe):
            for t in range(NT):
                if t % HALF == 0:
                    pe.wait_ge(xn_done, t // HALF + 1)
                    pe.wait_ge(xn2_done, t // HALF + 1)
                last = pe.transpose(banks[t // 4][:, t % 4 * P:(t % 4 + 1) * P], xn[:, t, :], c["ident"][:, :])
                if t % 4 == 3:
                    last.then_inc(xnT_ps, 1)
            pe.wait_ge(wl_done, 2)
            for g in range(4):
                pe.wait_ge(xnT_done, g + 1)
                cs = slice(g * 512, (g + 1) * 512)
                split_product(pe, banks[g][:, :], wd_h[:, :], wd_l[:, :], xnT_h[:, cs], xnT_l[:, cs]).then_inc(lat_ps, 1)
            pe.wait_ge(lat_done, 4)
            for part in range(4):
                project(pe, 0, part)
            for v in range(2 * NT):
                wait(pe, vl_done, v - 3)
                ts, cs = slice(v // 2 * P, (v // 2 + 1) * P), slice(v % 2 * 512, (v % 2 + 1) * 512)
                split_product(pe, ps_v[v % 4][:, :], latT_h[:, ts], latT_l[:, ts], wv_h[:, cs], wv_l[:, cs]).then_inc(v_ps, 1)
                if v in FIRST_MAX_AT:
                    max_chunk(pe, 0, 0, 0, FIRST_MAX_AT.index(v))
            turn_max(pe, 0, 0)
            pe.wait_ge(vl_done, 2 * NT)
            pe.wait_ge(ones_done, 1)
            for s in range(2):
                slot_tensor(pe, 0, 0, s)
            with pe.Fori(0, NB // 2 - 1) as twice:
                for u in range(2):
                    for s in range(2):
                        slot_tensor(pe, 2 * twice + (1 + u), 1 - u, s)
            for s in range(2):
                slot_tensor(pe, NB - 1, 1, s, last=True)
            values(pe, NB - 1, 1, NC - 4)
            turn_y(pe, NB - 1, 0)
            values(pe, NB - 1, 1, NC - 3)
            out_product(pe, NB - 1, 0)
            values(pe, NB - 1, 1, NC - 2)
            values(pe, NB - 1, 1, NC - 1)
            turn_y(pe, NB - 1, 1)
            out_product(pe, NB - 1, 1)

        def weights_low(dve, n):
            dve.wait_ge(wpair_high, n + 1)
            dve.tensor_tensor(wqk_l[:, :, :], wqk[:, :, :], wqk_h[:, :, :].bitcast(FP32), ALU.subtract).then_inc(wpair_low, 1)

        def low_of(dve, low, high, g, ready, done):
            cs = slice(g * 512, (g + 1) * 512)
            dve.wait_ge(ready, g + 1)
            dve.tensor_tensor(low[:, cs], banks[g][:, :], high[:, cs].bitcast(FP32), ALU.subtract).then_inc(done, 1)

        def low_part(dve, n, part):
            dve.wait_ge(high_done, 4 * n + part + 1)
            high, low = ((QH, QL), (KH, KL))[part // 2]
            cs = slice(part % 2 * 512, (part % 2 + 1) * 512)
            dve.scalar_tensor_tensor(out=low[:, cs], in0=ps_proj[part % 2], scalar=(HS ** -0.5, 1.0)[part // 2],
                                     in1=high[:, cs].bitcast(FP32), op0=ALU.mult, op1=ALU.subtract).then_inc(low_done, 1)

        def reduce_max(dve, n, s, t):
            i, k0, cols = MAXES[t]
            k = NC * (2 * n + s) + t
            dve.wait_ge(mx_ps, k + 1)
            dve.tensor_reduce(mx[:, k0 // 512, i:i + 1], ps_mx[t % 2][:, 0:cols], AX.X, ALU.max).then_inc(mx_done, 1)

        def output(dve, n, s, Q):
            h = 2 * n + s
            dve.wait_ge(pv_ps, NC * h + (4 if Q == 0 else NC))
            pv = ps_pv[Q][:, 0:4 * (HS + 1)].rearrange("p (i v) -> p i v", v=HS + 1)
            dve.reciprocal(rden[:, Q, :], pv[:, :, HS]).then_inc(y_own, 1)
            dve.wait_ge(y_own, 4 * h + 2 * Q + 1)
            dve.tensor_scalar(rs[:, Q, :], rden[:, Q, :], vunscale[:, 0:1], None, ALU.mult).then_inc(y_own, 1)
            dve.wait_ge(y_own, 4 * h + 2 * Q + 2)
            if s == 0:
                wait(dve, yT_ps, 2 * n - 1 + Q)
            dve.tensor_tensor(yp[:, 4 * Q:4 * Q + 4, s * HS:(s + 1) * HS], pv[:, :, 0:HS],
                              rs[:, Q, :].unsqueeze(2).to_broadcast([P, 4, HS]), ALU.mult).then_inc(y_done, 1)

        def add_output(dve, n, half):
            dve.wait_ge(o_ps, 2 * n + half + 1)
            Xf = X[:, :, :].rearrange("p t d -> p (t d)")
            at = (n // NP) * T + half * 512
            dve.tensor_tensor(Xf[:, bass.ds(at, 512)], ps_pr[:, :], Xf[:, bass.ds(at, 512)], ALU.add).then_inc(o_done, 1)


        def diagonals(dve, n, s):
            h = 2 * n + s
            eye = c["eye"][:, :].rearrange("p (i j) -> p i j", j=QT)
            dve.wait_ge(mx_done, NC * h + NC)
            dve.tensor_tensor(m[:, :], mx[:, 0, :], mx[:, 1, :], ALU.max).then_inc(m_own, 1)
            dve.wait_ge(m_own, 4 * h + 1)
            dve.tensor_copy(mh[:, :], m[:, :]).then_inc(m_own, 1)
            dve.wait_ge(m_own, 4 * h + 2)
            dve.tensor_tensor(mr[:, :], m[:, :], mh[:, :], ALU.subtract).then_inc(m_own, 1)
            wait(dve, shift_ps, h)
            dve.tensor_tensor(mdiag[:, :, 0:QT], eye, mh[:, :].unsqueeze(2).to_broadcast([P, QT, QT]), ALU.mult).then_inc(m_own, 1)
            dve.wait_ge(m_own, 4 * h + 4)
            dve.tensor_tensor(mdiag[:, :, QT:2 * QT], eye, mr[:, :].unsqueeze(2).to_broadcast([P, QT, QT]), ALU.mult).then_inc(diag_done, 1)

        def shift_rows(dve, n, s):
            dve.wait_ge(shift_ps, 2 * n + s + 1)
            r = HS if s == 0 else 0
            dve.tensor_copy(QM[s][r:r + 2 * QT, :], ps_shift[0:2 * QT, :]).then_inc(shift_done, 1)

        def slot_vector(dve, n, s, last=False):
            first = isinstance(n, int) and n == 0
            nn, ns = (n, 1) if s == 0 else (n + 1, 0)
            mt = 0
            for t in range(NC):
                if s == 0 and not last and t == 1:
                    weights_low(dve, n + 1)
                if not (last and s == 1):
                    for _ in range(MAX_AT[t]):
                        reduce_max(dve, nn, ns, mt)
                        mt += 1
                if s == 0 and not last and t in PROJECT_AT:
                    low_part(dve, n + 1, PROJECT_AT.index(t))
                if t == LAG and not (first and s == 0):
                    output(dve, n - 1 if s == 0 else n, 1 - s, 1)
                if t == TURN_MAX_AT - 1 and not (last and s == 1):
                    diagonals(dve, nn, ns)
                if t == LAG + 4:
                    output(dve, n, s, 0)
                if s == 1 and not first and t - 1 in OUT_AT:
                    add_output(dve, n - 1, OUT_AT.index(t - 1))
                if t == TURN_MAX_AT + 1 and not (last and s == 1):
                    shift_rows(dve, nn, ns)

        @block.vector
        def _(dve):
            count = [0]

            def link(instruction):
                count[0] += 1
                instruction.then_inc(chain_v, 1)
                dve.wait_ge(chain_v, count[0])

            for n in range(2):
                tiles = range(n * HALF, n * HALF + HALF)
                for t in tiles:
                    last = dve.bn_stats(stats[:, t, :], X[:, t, :])
                link(last)
                for t in tiles:
                    last = dve.bn_aggr(mv[:, t, :], stats[:, t, :])
                last.then_inc(measured_x, 1)
            for n in range(2):
                ts = slice(n * HALF, n * HALF + HALF)
                dve.wait_ge(std_done, n + 1)
                link(dve.reciprocal(rstd[:, ts], std[:, ts]))
                dve.scalar_tensor_tensor(out=negmean[:, ts], in0=mv[:, ts, 0], scalar=-1.0, in1=rstd[:, ts],
                                         op0=ALU.mult, op1=ALU.mult).then_inc(scales_done, 1)
                for t in range(n * HALF + XN_ACT, n * HALF + HALF):
                    last = dve.tensor_scalar(xn[:, t, :], X[:, t, :], mv[:, t, 0:1], rstd[:, t:t + 1],
                                             ALU.subtract, ALU.mult)
                last.then_inc(xn2_done, 1)
            dve.wait_ge(w_in, 48)
            link(dve.tensor_reduce(wmax[:, 0:1], wd[:, :], AX.X, ALU.max, apply_absolute_value=True))
            dve.tensor_reduce(wmax[:, 1:2], wv, AX.X, ALU.max, apply_absolute_value=True).then_inc(wmax_done, 1)
            for g in range(4):
                low_of(dve, xnT_l, xnT_h, g, xnT_high, xnT_done)
            weights_low(dve, 0)
            dve.wait_ge(wmax_red, 1)
            link(dve.tensor_tensor(vscale[:, :], wmax_all[:, 0:1], wmax_all[:, 1:2], ALU.mult))
            link(dve.tensor_scalar(vscale[:, :], vscale[:, :], D * D * math.sqrt(D) / VMAX, 1e-30, ALU.mult, ALU.max))
            link(dve.reciprocal(vscale[:, :], vscale[:, :]))
            dve.reciprocal(vunscale[:, :], vscale[:, :]).then_inc(scale_done, 1)
            for g in range(4):
                low_of(dve, latT_l, latT_h, g, lat_high, lat_done)
            for part in range(4):
                low_part(dve, 0, part)
            dve.wait_ge(filled, 3)
            for v in range(2 * NT):
                dve.wait_ge(vh_done, v + 1)
                dve.scalar_tensor_tensor(out=v_view(v, 0), in0=ps_v[v % 4][:, :].rearrange("p (h d) -> p h d", d=HS),
                                         scalar=vscale[:, 0:1], in1=v_view(v, HS), op0=ALU.mult, op1=ALU.subtract).then_inc(vl_done, 1)
                if v in FIRST_MAX_AT:
                    reduce_max(dve, 0, 0, FIRST_MAX_AT.index(v))
                if v == FIRST_MAX_AT[-1] + 1:
                    diagonals(dve, 0, 0)
            dve.wait_ge(stacks_set, 64)
            shift_rows(dve, 0, 0)
            for s in range(2):
                slot_vector(dve, 0, s)
            with dve.Fori(1, NB - 1) as n:
                for s in range(2):
                    slot_vector(dve, n, s)
            for s in range(2):
                slot_vector(dve, NB - 1, s, last=True)
            add_output(dve, NB - 1, 0)
            output(dve, NB - 1, 1, 1)
            add_output(dve, NB - 1, 1)
            dve.wait_ge(o_done, 2 * NB)


def program(nc, x, w_kv_down, w_kv_up, w_q, w_out, Wr, br, W1, b1, g1, be1, W2, b2, g2, be2, out, phases="faf"):
    w = dict(Wr=Wr, br=br, W1=W1, b1=b1, g1=g1, be1=be1, W2=W2, b2=b2, g2=g2, be2=be2)
    ctx = ExitStack()
    with ctx:
        def sb(name, shape, dt=FP32):
            return ctx.enter_context(nc.sbuf_tensor(name, shape, dt))
        c = dict(ident=sb("ident", [P, P]), upper=sb("upper", [P, P], BF16), ones=sb("ones", [P, P], BF16),
                 sel3=sb("sel3", [P, P], BF16), scanmask=sb("scanmask", [P, E * NT]), eps=sb("eps", [P, 1]),
                 iota=sb("iota", [P, P]), part=sb("part", [P, 1]), early=sb("early", [P, E]),
                 pairtile=sb("pairtile", [P, K * NT]), dumprow=sb("dumprow", [P, NS + 1]),
                 identb=sb("identb", [P, P], BF16), negmask=sb("negmask", [P, P], BF16),
                 eye=sb("eye", [P, QT * QT]), lnscale=sb("lnscale", [P, 1]))
        X = sb("X", [P, NT, D])
        scratch = dict(xn=nc.dram_tensor("xn_rows", (TOK, D), FP32).ap(),
                       y=nc.dram_tensor("y_rows", (K * TOK + 2 * P, D), FP32).ap())
        with nc.cleanup_on_exit():
            ffn_phase(nc, "f0", c, w, X, scratch, x_in=x, x_out=out if phases == "f" else None)
        if "a" in phases:
            with nc.cleanup_on_exit():
                attention_phase(nc, c, dict(w_kv_down=w_kv_down, w_kv_up=w_kv_up, w_q=w_q, w_out=w_out), X)
        if phases == "fa":
            done = ctx.enter_context(nc.semaphore("done"))
            with nc.Block() as block:
                @block.sync
                def _(sp):
                    sp.dma_start(out.rearrange("b (t p) d -> p (b t) d", p=P), X[:, :, :]).then_inc(done, 16)
                    sp.wait_ge(done, 16)
        if phases == "faf":
            ffn_phase(nc, "f1", c, w, X, scratch, x_out=out)


_INS = ["L0_attn_x", "L0_attn_w_kv_down", "L0_attn_w_kv_up", "L0_attn_w_q", "L0_attn_w_out",
        "L0_ffn_Wr", "L0_ffn_br", "L0_ffn_W1", "L0_ffn_b1", "L0_ffn_g1", "L0_ffn_be1",
        "L0_ffn_W2", "L0_ffn_b2", "L0_ffn_g2", "L0_ffn_be2"]
_OUTS = [((2, 1024, 128), "float32")]


def kernel(**inputs):
    import numpy as _np
    import concourse.bacc as _bacc
    from concourse import mybir as _mybir
    from concourse.bass_utils import run_bass_kernel_spmd as _run

    nc = _bacc.Bacc("TRN2", target_bir_lowering=False, num_devices=1)
    arrays, args = {}, []
    for name in _INS:
        a = _np.ascontiguousarray(inputs[name])
        arrays[f"in_{name}_dram"] = a
        args.append(nc.dram_tensor(f"in_{name}_dram", a.shape, _mybir.dt.from_np(a.dtype), kind="ExternalInput").ap())
    for i, (shape, dtype) in enumerate(_OUTS):
        dt = _mybir.dt.from_np(_np.dtype(dtype))
        args.append(nc.dram_tensor(f"out_{i}_dram", shape, dt, kind="ExternalOutput").ap())
    program(nc, *args)
    r = _run(nc, [arrays], core_ids=[0])
    return r.results[0]["out_0_dram"]
```
